# Optimizing a Trainium2 kernel written in Bass

```python
import numpy as np
import jax
import jax.numpy as jnp

def _softmax(x, axis=-1):
    return jax.nn.softmax(x, axis=axis)

def _gelu(x):
    return jax.nn.gelu(x, approximate=True)

def _silu(x):
    return jax.nn.silu(x)

def _sigmoid(x):
    return jax.nn.sigmoid(x)

def _layernorm(x, axis=-1, eps=1e-05):
    m = jnp.mean(x, axis=axis, keepdims=True)
    v = jnp.var(x, axis=axis, keepdims=True)
    return (x - m) / jnp.sqrt(v + eps)

def _scatter_add(tgt, idx, src, axis=0):
    return tgt.at[idx].add(src)

def _segment_sum(src, seg, n):
    return jax.ops.segment_sum(src, seg, n)
kernel_name = 'mk_adj_ffn_d2_adj_r2_071bc0'

def setup_inputs(seed: int=0):
    np.random.seed(seed)
    _w = jnp.asarray

    def _rec_inputs():
        import jax
        import jax.numpy as jnp
        _gk = jax.random.key(seed)
        x = -2.104e-05 + 0.9999 * jax.random.normal(jax.random.fold_in(_gk, 1), (128, 128, 128), jnp.float32)
        _a = jax.random.bernoulli(jax.random.fold_in(_gk, 2), 0.03125, (128, 128))
        _a = jnp.logical_or(_a, jnp.swapaxes(_a, -1, -2))
        _a = jnp.logical_or(_a, jnp.eye(128, dtype=bool))
        _af = _a.astype(jnp.float32)
        _af = _af / jnp.maximum(_af.sum(-1, keepdims=True), 1.0)
        adj = _af
        return (x, adj)
    x, adj = _rec_inputs()

    def _L0_gnn_setup():
        import jax, jax.numpy as jnp
        import numpy as np
        N = 3445
        B = 32
        IN_DIM = 128
        HID_DIM = 128

        def _make_adj(key):
            a = jax.random.uniform(key, (N, N), dtype=jnp.float32)
            a = (a < 0.001).astype(jnp.float32)
            a = jnp.maximum(a, a.T)
            deg = jnp.sum(a, axis=1, keepdims=True)
            return a / jnp.maximum(deg, 1.0)

        def _graph_conv(x, adj, w_loop, w_neigh, b):
            loop = jnp.einsum('bnd,dh->bnh', x, w_loop)
            neigh = jnp.einsum('nm,bmh->bnh', adj, jnp.einsum('bnd,dh->bnh', x, w_neigh))
            return loop + neigh + b
        key = jax.random.key(seed)
        k = jax.random.split(key, 8)
        s1 = 1.0 / np.sqrt(IN_DIM)
        s2 = 1.0 / np.sqrt(HID_DIM)
        return {'x': jax.random.normal(k[0], (B, N, IN_DIM), dtype=jnp.float32), 'adj': _make_adj(k[1]), 'w1_loop': jax.random.normal(k[2], (IN_DIM, HID_DIM), dtype=jnp.float32) * s1, 'w1_neigh': jax.random.normal(k[3], (IN_DIM, HID_DIM), dtype=jnp.float32) * s1, 'b1': jnp.zeros((HID_DIM,), dtype=jnp.float32), 'w2_loop': jax.random.normal(k[4], (HID_DIM, IN_DIM), dtype=jnp.float32) * s2, 'w2_neigh': jax.random.normal(k[5], (HID_DIM, IN_DIM), dtype=jnp.float32) * s2, 'b2': jnp.zeros((IN_DIM,), dtype=jnp.float32)}
    _L0_gnn_all = _L0_gnn_setup()
    _L0_gnn_in = {k: v for k, v in _L0_gnn_all.items() if k in ('w1_loop', 'w1_neigh', 'b1', 'w2_loop', 'w2_neigh', 'b2')}
    del _L0_gnn_all

    def _L0_ffn_setup():
        import jax, jax.numpy as jnp
        import numpy as np
        from jax import lax
        key = jax.random.key(seed)
        B, T, I, H = (64, 1024, 128, 128)
        ks = jax.random.split(key, 13)
        s = 1.0 / np.sqrt(H)

        def w(k, shape):
            return jax.random.uniform(k, shape, jnp.float32, -s, s)
        return {'x': jax.random.normal(ks[0], (B, T, I), jnp.float32), 'U_i': w(ks[1], (I, H)), 'V_i': w(ks[2], (H, H)), 'b_i': w(ks[3], (H,)), 'U_f': w(ks[4], (I, H)), 'V_f': w(ks[5], (H, H)), 'b_f': w(ks[6], (H,)), 'U_c': w(ks[7], (I, H)), 'V_c': w(ks[8], (H, H)), 'b_c': w(ks[9], (H,)), 'U_o': w(ks[10], (I, H)), 'V_o': w(ks[11], (H, H)), 'b_o': w(ks[12], (H,))}
    _L0_ffn_all = _L0_ffn_setup()
    _L0_ffn_in = {k: v for k, v in _L0_ffn_all.items() if k in ('U_i', 'V_i', 'b_i', 'U_f', 'V_f', 'b_f', 'U_c', 'V_c', 'b_c', 'U_o', 'V_o', 'b_o')}
    del _L0_ffn_all

    def _L1_gnn_setup():
        import jax, jax.numpy as jnp
        import numpy as np
        EPS_LN = 1e-05

        def _layernorm(x, g, b):
            mu = x.mean(-1, keepdims=True)
            var = ((x - mu) ** 2).mean(-1, keepdims=True)
            return (x - mu) / jnp.sqrt(var + EPS_LN) * g + b
        key = jax.random.key(seed)
        B, N, D, H = (4, 1024, 128, 4)
        hid = int(D * 2.0)
        ks = jax.random.split(key, 12)
        x = jax.random.normal(ks[0], (B, N, D), jnp.float32)
        Au = jax.random.uniform(ks[1], (N, N)) < 0.004
        A = jnp.logical_or(Au, Au.T)
        A = A.at[jnp.arange(N), jnp.arange(N)].set(False)
        Af = A.astype(jnp.float32)
        deg = Af.sum(axis=1)
        L = jnp.diag(deg) - Af
        adjacency = Af + jnp.eye(N, dtype=jnp.float32)
        s = lambda k, sh, f: jax.random.normal(k, sh, jnp.float32) * f
        sc = 1.0 / np.sqrt(D)
        Wc = s(ks[2], (D, D), sc)
        bc = jnp.zeros((D,), jnp.float32)
        Wq = s(ks[3], (D, D), sc)
        Wk = s(ks[4], (D, D), sc)
        Wv = s(ks[5], (D, D), sc)
        Wo = s(ks[6], (D, D), sc)
        bo = jnp.zeros((D,), jnp.float32)
        W1 = s(ks[7], (D, hid), sc)
        b1 = jnp.zeros((hid,), jnp.float32)
        W2 = s(ks[8], (hid, D), 1.0 / np.sqrt(hid))
        b2 = jnp.zeros((D,), jnp.float32)
        g1 = jnp.ones((D,), jnp.float32)
        be1 = jnp.zeros((D,), jnp.float32)
        g2 = jnp.ones((D,), jnp.float32)
        be2 = jnp.zeros((D,), jnp.float32)
        g3 = jnp.ones((D,), jnp.float32)
        be3 = jnp.zeros((D,), jnp.float32)
        return dict(x=x, L=L, adjacency=adjacency, Wc=Wc, bc=bc, g1=g1, be1=be1, Wq=Wq, Wk=Wk, Wv=Wv, Wo=Wo, bo=bo, g2=g2, be2=be2, W1=W1, b1=b1, W2=W2, b2=b2, g3=g3, be3=be3)
    _L1_gnn_all = _L1_gnn_setup()
    _L1_gnn_in = {k: v for k, v in _L1_gnn_all.items() if k in ('Wc', 'bc', 'g1', 'be1', 'Wq', 'Wk', 'Wv', 'Wo', 'bo', 'g2', 'be2', 'W1', 'b1', 'W2', 'b2', 'g3', 'be3')}
    del _L1_gnn_all

    def _L1_ffn_setup():
        import jax, jax.numpy as jnp
        import numpy as np
        B, S, D, F, E, K = (8, 1024, 128, 512, 8, 2)
        key = jax.random.key(seed)
        ks = jax.random.split(key, 10)
        s = 0.02
        return {'x': jax.random.normal(ks[0], (B, S, D), dtype=jnp.float32), 'Wr': jax.random.normal(ks[1], (D, E), dtype=jnp.float32) * s, 'W1s': jax.random.normal(ks[2], (D, F), dtype=jnp.float32) * s, 'b1s': jnp.zeros((F,), dtype=jnp.float32), 'W2s': jax.random.normal(ks[3], (F, D), dtype=jnp.float32) * s, 'b2s': jnp.zeros((D,), dtype=jnp.float32), 'W1p': jax.random.normal(ks[4], (E, D, F), dtype=jnp.float32) * s, 'b1p': jnp.zeros((E, F), dtype=jnp.float32), 'W2p': jax.random.normal(ks[5], (E, F, D), dtype=jnp.float32) * s, 'b2p': jnp.zeros((E, D), dtype=jnp.float32)}
    _L1_ffn_all = _L1_ffn_setup()
    _L1_ffn_in = {k: v for k, v in _L1_ffn_all.items() if k in ('Wr', 'W1s', 'b1s', 'W2s', 'b2s', 'W1p', 'b1p', 'W2p', 'b2p')}
    del _L1_ffn_all
    return {'x': x, 'adj': adj, 'L0_gnn_w1_loop': _L0_gnn_in['w1_loop'], 'L0_gnn_w1_neigh': _L0_gnn_in['w1_neigh'], 'L0_gnn_b1': _L0_gnn_in['b1'], 'L0_gnn_w2_loop': _L0_gnn_in['w2_loop'], 'L0_gnn_w2_neigh': _L0_gnn_in['w2_neigh'], 'L0_gnn_b2': _L0_gnn_in['b2'], 'L0_ffn_U_i': _L0_ffn_in['U_i'], 'L0_ffn_V_i': _L0_ffn_in['V_i'], 'L0_ffn_b_i': _L0_ffn_in['b_i'], 'L0_ffn_U_f': _L0_ffn_in['U_f'], 'L0_ffn_V_f': _L0_ffn_in['V_f'], 'L0_ffn_b_f': _L0_ffn_in['b_f'], 'L0_ffn_U_c': _L0_ffn_in['U_c'], 'L0_ffn_V_c': _L0_ffn_in['V_c'], 'L0_ffn_b_c': _L0_ffn_in['b_c'], 'L0_ffn_U_o': _L0_ffn_in['U_o'], 'L0_ffn_V_o': _L0_ffn_in['V_o'], 'L0_ffn_b_o': _L0_ffn_in['b_o'], 'L1_gnn_Wc': _L1_gnn_in['Wc'], 'L1_gnn_bc': _L1_gnn_in['bc'], 'L1_gnn_g1': _L1_gnn_in['g1'], 'L1_gnn_be1': _L1_gnn_in['be1'], 'L1_gnn_Wq': _L1_gnn_in['Wq'], 'L1_gnn_Wk': _L1_gnn_in['Wk'], 'L1_gnn_Wv': _L1_gnn_in['Wv'], 'L1_gnn_Wo': _L1_gnn_in['Wo'], 'L1_gnn_bo': _L1_gnn_in['bo'], 'L1_gnn_g2': _L1_gnn_in['g2'], 'L1_gnn_be2': _L1_gnn_in['be2'], 'L1_gnn_W1': _L1_gnn_in['W1'], 'L1_gnn_b1': _L1_gnn_in['b1'], 'L1_gnn_W2': _L1_gnn_in['W2'], 'L1_gnn_b2': _L1_gnn_in['b2'], 'L1_gnn_g3': _L1_gnn_in['g3'], 'L1_gnn_be3': _L1_gnn_in['be3'], 'L1_ffn_Wr': _L1_ffn_in['Wr'], 'L1_ffn_W1s': _L1_ffn_in['W1s'], 'L1_ffn_b1s': _L1_ffn_in['b1s'], 'L1_ffn_W2s': _L1_ffn_in['W2s'], 'L1_ffn_b2s': _L1_ffn_in['b2s'], 'L1_ffn_W1p': _L1_ffn_in['W1p'], 'L1_ffn_b1p': _L1_ffn_in['b1p'], 'L1_ffn_W2p': _L1_ffn_in['W2p'], 'L1_ffn_b2p': _L1_ffn_in['b2p']}

def reference(x, adj, L0_gnn_w1_loop, L0_gnn_w1_neigh, L0_gnn_b1, L0_gnn_w2_loop, L0_gnn_w2_neigh, L0_gnn_b2, L0_ffn_U_i, L0_ffn_V_i, L0_ffn_b_i, L0_ffn_U_f, L0_ffn_V_f, L0_ffn_b_f, L0_ffn_U_c, L0_ffn_V_c, L0_ffn_b_c, L0_ffn_U_o, L0_ffn_V_o, L0_ffn_b_o, L1_gnn_Wc, L1_gnn_bc, L1_gnn_g1, L1_gnn_be1, L1_gnn_Wq, L1_gnn_Wk, L1_gnn_Wv, L1_gnn_Wo, L1_gnn_bo, L1_gnn_g2, L1_gnn_be2, L1_gnn_W1, L1_gnn_b1, L1_gnn_W2, L1_gnn_b2, L1_gnn_g3, L1_gnn_be3, L1_ffn_Wr, L1_ffn_W1s, L1_ffn_b1s, L1_ffn_W2s, L1_ffn_b2s, L1_ffn_W1p, L1_ffn_b1p, L1_ffn_W2p, L1_ffn_b2p):
    import jax
    import jax.numpy as jnp

    def _L0_gnn_ref(x, adj, w1_loop, w1_neigh, b1, w2_loop, w2_neigh, b2):
        import jax, jax.numpy as jnp
        import numpy as np
        N = 3445
        B = 32
        IN_DIM = 128
        HID_DIM = 128

        def _make_adj(key):
            a = jax.random.uniform(key, (N, N), dtype=jnp.float32)
            a = (a < 0.001).astype(jnp.float32)
            a = jnp.maximum(a, a.T)
            deg = jnp.sum(a, axis=1, keepdims=True)
            return a / jnp.maximum(deg, 1.0)

        def _graph_conv(x, adj, w_loop, w_neigh, b):
            loop = jnp.einsum('bnd,dh->bnh', x, w_loop)
            neigh = jnp.einsum('nm,bmh->bnh', adj, jnp.einsum('bnd,dh->bnh', x, w_neigh))
            return loop + neigh + b
        h = jax.nn.relu(_graph_conv(x, adj, w1_loop, w1_neigh, b1))
        h = jax.nn.relu(_graph_conv(h, adj, w2_loop, w2_neigh, b2))
        return (x + h) * 0.5

    def _L0_ffn_ref(x, U_i, V_i, b_i, U_f, V_f, b_f, U_c, V_c, b_c, U_o, V_o, b_o):
        import jax, jax.numpy as jnp
        import numpy as np
        from jax import lax
        B, T, _ = x.shape
        H = U_i.shape[1]
        xt = jnp.swapaxes(x, 0, 1)
        xi = xt @ U_i + b_i
        xf = xt @ U_f + b_f
        xg = xt @ U_c + b_c
        xo = xt @ U_o + b_o
        h0 = jnp.zeros((B, H), x.dtype)
        c0 = jnp.zeros((B, H), x.dtype)

        def step(carry, xs):
            h, c = carry
            xi_t, xf_t, xg_t, xo_t = xs
            i_t = jax.nn.sigmoid(xi_t + h @ V_i)
            f_t = jax.nn.sigmoid(xf_t + h @ V_f)
            g_t = jnp.tanh(xg_t + h @ V_c)
            o_t = jax.nn.sigmoid(xo_t + h @ V_o)
            c_new = h * c + i_t * g_t
            h_new = o_t * jnp.tanh(c_new)
            return ((h_new, c_new), h_new)
        (_, _), hs = lax.scan(step, (h0, c0), (xi, xf, xg, xo))
        return jnp.swapaxes(hs, 0, 1)

    def _L1_gnn_ref(x, L, adjacency, Wc, bc, g1, be1, Wq, Wk, Wv, Wo, bo, g2, be2, W1, b1, W2, b2, g3, be3):
        import jax, jax.numpy as jnp
        import numpy as np
        EPS_LN = 1e-05

        def _layernorm(x, g, b):
            mu = x.mean(-1, keepdims=True)
            var = ((x - mu) ** 2).mean(-1, keepdims=True)
            return (x - mu) / jnp.sqrt(var + EPS_LN) * g + b
        B, N, D = x.shape
        H = 4
        hd = D // H
        eig = jnp.linalg.eigvalsh(L)
        lam_max = eig[-1] + 1e-08
        L_norm = 2.0 * L / lam_max - jnp.eye(N, dtype=L.dtype)
        xp = jnp.einsum('mn,bnf->bmf', L_norm, x)
        h = xp @ Wc + bc
        h = _layernorm(h, g1, be1)
        h = jax.nn.relu(h)
        x1 = h + x
        q = (x1 @ Wq).reshape(B, N, H, hd).transpose(0, 2, 1, 3)
        k = (x1 @ Wk).reshape(B, N, H, hd).transpose(0, 2, 1, 3)
        v = (x1 @ Wv).reshape(B, N, H, hd).transpose(0, 2, 1, 3)
        scores = jnp.einsum('bhnd,bhmd->bhnm', q, k) / np.sqrt(hd).astype(np.float32)
        scores = jnp.where(adjacency[None, None] > 0, scores, jnp.float32(-1000000000.0))
        attn = jax.nn.softmax(scores, axis=-1)
        o = jnp.einsum('bhnm,bhmd->bhnd', attn, v)
        o = o.transpose(0, 2, 1, 3).reshape(B, N, D)
        o = o @ Wo + bo
        x2 = _layernorm(x1 + o, g2, be2)
        m = jax.nn.gelu(x2 @ W1 + b1, approximate=False) @ W2 + b2
        return _layernorm(x2 + m, g3, be3)

    def _L1_ffn_ref(x, Wr, W1s, b1s, W2s, b2s, W1p, b1p, W2p, b2p):
        import jax, jax.numpy as jnp
        import numpy as np
        B, S, D, F, E, K = (8, 1024, 128, 512, 8, 2)
        gelu = lambda t: jax.nn.gelu(t, approximate=False)
        shared = gelu(x @ W1s + b1s) @ W2s + b2s
        rw = jax.nn.softmax(x @ Wr, axis=-1)
        topw, topi = jax.lax.top_k(rw, K)
        topw = topw / jnp.sum(topw, axis=-1, keepdims=True)
        mask = jnp.sum(jax.nn.one_hot(topi, E, dtype=topw.dtype) * topw[..., None], axis=-2)
        h = gelu(jnp.einsum('bsd,edf->bsef', x, W1p) + b1p)
        priv = jnp.einsum('bsef,efd->bsed', h, W2p) + b2p
        routed = jnp.einsum('bsed,bse->bsd', priv, mask)
        return shared + routed
    x = x + _L0_gnn_ref(_layernorm(x, axis=-1), adj, L0_gnn_w1_loop, L0_gnn_w1_neigh, L0_gnn_b1, L0_gnn_w2_loop, L0_gnn_w2_neigh, L0_gnn_b2)
    x = x + _L0_ffn_ref(_layernorm(x, axis=-1), L0_ffn_U_i, L0_ffn_V_i, L0_ffn_b_i, L0_ffn_U_f, L0_ffn_V_f, L0_ffn_b_f, L0_ffn_U_c, L0_ffn_V_c, L0_ffn_b_c, L0_ffn_U_o, L0_ffn_V_o, L0_ffn_b_o)
    x = x + _L1_gnn_ref(_layernorm(x, axis=-1), adj, adj, L1_gnn_Wc, L1_gnn_bc, L1_gnn_g1, L1_gnn_be1, L1_gnn_Wq, L1_gnn_Wk, L1_gnn_Wv, L1_gnn_Wo, L1_gnn_bo, L1_gnn_g2, L1_gnn_be2, L1_gnn_W1, L1_gnn_b1, L1_gnn_W2, L1_gnn_b2, L1_gnn_g3, L1_gnn_be3)
    x = x + _L1_ffn_ref(_layernorm(x, axis=-1), L1_ffn_Wr, L1_ffn_W1s, L1_ffn_b1s, L1_ffn_W2s, L1_ffn_b2s, L1_ffn_W1p, L1_ffn_b1p, L1_ffn_W2p, L1_ffn_b2p)
    return x

_drawn_inputs = setup_inputs


def setup_inputs(seed=0):
    import zlib

    import numpy as np

    out = dict(_drawn_inputs(seed))
    spreads = {'L0_gnn_b1': (0.0, 0.376),
     'L0_gnn_b2': (0.0, 0.362),
     'L1_gnn_bc': (0.0, 0.1),
     'L1_gnn_g1': (1.0, 0.2),
     'L1_gnn_be1': (0.0, 0.272),
     'L1_gnn_bo': (0.0, 0.278),
     'L1_gnn_g2': (1.0, 0.2),
     'L1_gnn_be2': (0.0, 0.1),
     'L1_gnn_b1': (0.0, 0.335),
     'L1_gnn_b2': (0.0, 0.1),
     'L1_gnn_g3': (1.0, 0.2),
     'L1_gnn_be3': (0.0, 0.1),
     'L1_ffn_b1s': (0.0, 0.794),
     'L1_ffn_b2s': (0.0, 0.1),
     'L1_ffn_b1p': (0.0, 0.8),
     'L1_ffn_b2p': (0.0, 0.27)}
    factors = {'L0_ffn_V_i': 8.0,
     'L0_ffn_b_i': 8.0,
     'L0_ffn_V_c': 5.349,
     'L0_ffn_b_c': 5.918,
     'L0_ffn_V_o': 8.0,
     'L0_ffn_b_o': 8.0,
     'L1_ffn_W1p': 3.416,
     'L1_ffn_W2p': 3.094}
    for name, (base, spread) in spreads.items():
        noise = np.random.default_rng([zlib.crc32(name.encode()), seed]).standard_normal(out[name].shape)
        drawn = base * np.exp(spread * noise) if base else spread * noise
        out[name] = jnp.asarray(drawn.astype(out[name].dtype))
    for name, factor in factors.items():
        out[name] = (out[name] * factor).astype(out[name].dtype)
    return out
```

```python
from contextlib import ExitStack

import concourse.bass as bass
from concourse import mybir

P = 128
G = 4
BANK = G * P
SLOTS = 2
HEADS = 4
HD = P // HEADS
EXPERTS = 8
FF = 512
FC = FF // P
SQUARINGS = 28
EPS = 1e-5
L1_LOADS = 16 * (7 + 1 + 1 + 1 + 1 + EXPERTS + 2 + 2 + 2 + 9)
F32 = mybir.dt.float32
BF16 = mybir.dt.bfloat16
U32 = mybir.dt.uint32
ALU = mybir.AluOpType
ACT = mybir.ActivationFunctionType
AX = mybir.AxisListType


def build(nc, t):
    B, N, D = t["x"].shape
    assert B == N == D == P
    J = B // (G * SLOTS)
    ctx = ExitStack()
    with ctx:
        def sb(name, shape, dt=F32):
            return ctx.enter_context(nc.sbuf_tensor(name, shape, dt))

        sems = {}

        def sem(name, *which):
            key = "_".join([name, *map(str, which)])
            if key not in sems:
                sems[key] = ctx.enter_context(nc.semaphore(key))
            return sems[key]

        psum = ctx.enter_context(nc.psum_tensor("psum", [P, 8, BANK], F32))

        def early(eng, *values):
            for v in values:
                eng.compute_val(v)
            return values

        def nth(n, per_pass, k):
            return n * per_pass + (k + 1 - per_pass)

        SHARED = {
            "a_rows_psum": ("a_z1_psum", "a_h1_psum", "a_h2_psum"),
            "a_rows": ("a_z1", "a_h1", "a_x_half"),
            "r_parts": ("r_hc", "r_ic"),
            "c_rows_psum": ("c_hs_psum", "c_h_psum", "c_wo_psum", "c_ff_psum"),
            "c_qkv_psum": ("c_q_psum", "c_k_psum", "c_v_psum"),
            "c_sums": ("c_x1_bo", "c_x2_b2"),
            "a_cols_psum": ("a_xt_psum", "a_h1t_psum", "a_z2_psum", "a_h2t_psum", "a_x1t_psum"),
            "a_cols": ("a_xt", "a_h1t", "a_z2", "a_h2t", "a_x1t"),
            "c_cols_psum": ("c_xp_psum", "c_x1t_psum", "c_ot_psum", "c_x2t_psum", "c_x4t_psum"),
            "c_cols": ("c_xp", "c_x1t", "c_ot", "c_x2t", "c_x4t"),
            "c_rows": ("c_x2", "c_h", "c_res2", "c_res3", "c_x3"),
            "c_gains": ("c2_gained", "c2_shifted", "c3_gained", "c_x2n", "c4_gained", "c4_shifted"),
            "d_route": ("d_max", "d_sub", "d_top", "d_idx", "d_den", "d_inv", "d_w", "d_idxf", "d_eq0", "d_part0",
                        "d_eq1", "d_part1"),
        }
        AHEAD = {"a_cols": 1, "c_rows": 1, "y_done": 1, "x1_stored": 1, "out_stored": 1}
        PLACE = {step: (name, len(steps), k) for name, steps in SHARED.items() for k, step in enumerate(steps)}

        def rises(step, s):
            return sem(PLACE[step][0], s)

        def at(step, s, n):
            name, per_pass, k = PLACE[step]
            return sem(name, s), nth(n, per_pass, k) + AHEAD.get(name, 0)

        NORMS = {"a1": (2, 0), "a2": (2, 1), **{f"c{k + 1}": (5, k) for k in range(5)}}

        def norm(tag, what, s, n):
            return sem(f"{tag[0]}_norm_{what}", s), nth(n, *NORMS[tag])

        def bank(s, k):
            return psum[:, 4 * s + k, :]

        def squares(ap):
            return ap.rearrange("p (b f) -> p b f", b=G)

        def attended(s, half):
            return bank(s, 2 + half)[:, 0:2 * HEADS * (HD + 1)].rearrange("p (b h d) -> p b h d", b=2, h=HEADS)

        states = sb("states", [P, N + 1, B])
        room = sb("room", [P, SLOTS, 17, BANK])
        v_ones = sb("v_ones", [P, SLOTS, G, HEADS, HD + 1])

        def tile(s, k, n=1):
            return room[:, s, k:k + n, :].rearrange("p a f -> p (a f)")

        W = {}
        for name, cols in (("L0_gnn_w1_loop", P), ("L0_gnn_w1_neigh", P), ("L0_gnn_w2_loop", P),
                           ("L0_gnn_w2_neigh", P), ("L1_gnn_Wc", P), ("L1_gnn_Wq", P),
                           ("L1_gnn_Wk", P), ("L1_gnn_Wv", P), ("L1_gnn_Wo", P), ("L1_gnn_W1", 2 * P),
                           ("L1_ffn_Wr", EXPERTS)):
            W[name] = sb("w_" + name, [P, cols])
        gate_u = sb("gate_u", [P, 3, P])
        gate_v = sb("gate_v", [P, 3, P])
        w2_gnn = sb("w2_gnn", [P, 2, P])
        up_w = sb("up_w", [P, 1 + EXPERTS, FF])
        down_w = sb("down_w", [P, 1 + EXPERTS, FC, P])
        up_b = sb("up_b", [P, 1 + EXPERTS, FC])
        down_b = sb("down_b", [EXPERTS + 1, P])
        col_b = sb("col_b", [P, 8])
        gate_b = sb("gate_b", [P, 3])
        ROWS = ("L1_gnn_bc", "L1_gnn_g1", "L1_gnn_be1", "L1_gnn_bo", "L1_gnn_g2", "L1_gnn_be2",
                "L1_gnn_b2", "L1_gnn_g3", "L1_gnn_be3")
        row_b = sb("row_b", [P, len(ROWS), P])

        def row(name):
            return row_b[:, ROWS.index("L1_gnn_" + name), :].unsqueeze(1).to_broadcast([P, G, P])

        adj = sb("adj", [P, P])
        adj_t = sb("adj_t", [P, P])
        lap_t = sb("lap_t", [P, P])
        sym = sb("sym", [P, P])
        power = sb("power", [P, P])
        ident = sb("ident", [P, P])
        ident_h = sb("ident_h", [P, P], BF16)
        ones = sb("ones", [P, P])
        mask_add = sb("mask_add", [P, HEADS, P], BF16)
        row_any = sb("row_any", [P, P])
        tmp = sb("tmp", [P, P])
        tmp2 = sb("tmp2", [P, P])
        sc = sb("sc", [P, 16])
        expert_no = sb("expert_no", [P, G, EXPERTS])
        half_neg = sb("half_neg", [P, G])
        eps_tile = sb("eps_tile", [P, G])
        starts = sb("starts", [P, 16])
        waiting = sb("waiting", [P, 1])
        cell = sb("cell", [P, B])
        state_cell = sb("state_cell", [P, B])
        in_cand = sb("in_cand", [P, B])
        gates = sb("gates", [P, 2, 3, B])
        cell_tanh = sb("cell_tanh", [P, B])
        stats = sb("stats", [P, SLOTS, G, 6])
        moments = sb("moments", [P, SLOTS, G, 2])
        rstd = sb("rstd", [P, SLOTS, G])
        top = sb("top", [P, SLOTS, HEADS * G])
        inv_sum = sb("inv_sum", [P, SLOTS, 2, 2, HEADS])
        router = sb("router", [P, SLOTS, 8, G, EXPERTS])
        best_idx = sb("best_idx", [P, SLOTS, G, 8], U32)
        mask_t = sb("mask_t", [EXPERTS + 1, SLOTS, BANK])

        x1_dram = nc.dram_tensor("x1_scratch", [N, B, D], F32, kind="Internal").ap()
        x_rows = t["x"].rearrange("b n d -> n b d")
        out_rows = t["out"].rearrange("b n d -> n b d")

        block = ctx.enter_context(nc.Block())

        @block.sync
        def _(sp):
            sp.dma_start(adj[:], t["adj"]).then_inc(sem("adj_loaded"), 16)
            for name in ("L0_gnn_w1_loop", "L0_gnn_w1_neigh", "L0_gnn_w2_loop", "L0_gnn_w2_neigh"):
                sp.dma_start(W[name][:], t[name]).then_inc(sem("l0_loaded"), 16)
            for k, name in enumerate(("L0_gnn_b1", "L0_gnn_b2")):
                sp.dma_start(col_b[:, k:k + 1], t[name].unsqueeze(1)).then_inc(sem("l0_loaded"), 16)
            with sp.Fori(0, J) as j:
                batch = early(sp, *((j * SLOTS + s) * G for s in range(SLOTS)))
                stored, normed = early(sp, 16 * j + 1, norm("a2", "normed", 0, j + 1)[1])
                for s in range(SLOTS):
                    sp.wait_ge(sem("x1_stored", s), stored)
                    sp.dma_start(squares(tile(s, 0)), x_rows[:, bass.ds(batch[s], G), :]).then_inc(sem("x_in", s), 16)
                for s in range(SLOTS):
                    sp.wait_ge(norm("a2", "normed", s, 1)[0], normed)
                    sp.dma_start(x1_dram[:, bass.ds(batch[s], G), :], squares(tile(s, 0))).then_inc(sem("x1_stored", s), 16)
            for s in range(SLOTS):
                sp.wait_ge(sem("x1_stored", s), 16 * J + 1)
            with sp.Fori(0, J) as j:
                batch = early(sp, *((j * SLOTS + s) * G for s in range(SLOTS)))
                added, done = early(sp, at("c_x3", 0, j)[1], j + 2)
                for s in range(SLOTS):
                    sp.wait_ge(rises("c_x3", s), added)
                    sp.dma_start(squares(tile(s, 0)), x1_dram[:, bass.ds(batch[s], G), :]).then_inc(sem("c_x1_in", s), 16)
                for s in range(SLOTS):
                    sp.wait_ge(sem("y_done", s), done)
                    sp.dma_start(out_rows[:, bass.ds(batch[s], G), :], squares(tile(s, 12))).then_inc(sem("out_stored", s), 16)
            for s in range(SLOTS):
                sp.wait_ge(sem("out_stored", s), 16 * J + 1)

        @block.gpsimd
        def _(pool):
            nc.gpsimd.memset(ident[:], 0.0).then_inc(sem("p_zero"), 1)
            nc.gpsimd.memset(ones[:], 1.0)
            nc.gpsimd.memset(half_neg[:], -0.5)
            nc.gpsimd.memset(eps_tile[:], EPS)
            nc.gpsimd.memset(mask_t[:], 1.0)
            nc.gpsimd.memset(states[:, 0, :], 0.0)
            nc.gpsimd.memset(cell[:], 0.0)
            nc.gpsimd.memset(v_ones[:], 1.0)
            nc.gpsimd.iota(expert_no[:], pattern=[[0, G], [1, EXPERTS]], base=0, channel_multiplier=0,
                           allow_small_or_imprecise_dtypes=True)
            for k, name in enumerate(AHEAD):
                for s in range(SLOTS):
                    nc.gpsimd.memset(starts[:, SLOTS * k + s:SLOTS * k + s + 1], 0.0).then_inc(sem(name, s), 1)
            pool.wait_ge(sem("p_zero"), 1)
            nc.gpsimd.affine_select(out=ident[:], in_=ident[:], compare_op=ALU.not_equal, fill=1.0, base=0,
                                    pattern=[[-1, P]], channel_multiplier=1).then_inc(sem("ident"), 1)
            pool.wait_ge(sem("ident"), 1)
            nc.gpsimd.tensor_copy(ident_h[:], ident[:]).then_inc(sem("consts"), 1)

            def inverse_deviation(tag, s, n):
                pool.wait_ge(*norm(tag, "moments", s, n))
                nc.gpsimd.tensor_tensor(rstd[:, s, :], moments[:, s, :, 1], eps_tile[:], ALU.add).then_inc(norm(tag, "var", s, n)[0], 1)
                pool.wait_ge(*norm(tag, "var", s, n))
                nc.gpsimd.tensor_tensor(rstd[:, s, :], rstd[:, s, :], half_neg[:], ALU.pow).then_inc(norm(tag, "rstd", s, n)[0], 1)

            def vector_sum(tag, s, n, ready, out, a, b):
                pool.wait_ge(*ready)
                nc.gpsimd.tensor_tensor(squares(out), squares(a), b, ALU.add).then_inc(rises(tag, s), 1)

            with pool.Fori(0, J) as j:
                for tag in ("a1", "a2"):
                    for s in range(SLOTS):
                        inverse_deviation(tag, s, j + 1)
            for name in ("L1_gnn_Wc", "L1_gnn_Wq", "L1_gnn_Wk", "L1_gnn_Wv", "L1_gnn_Wo", "L1_gnn_W1", "L1_ffn_Wr"):
                pool.dma_start(W[name][:], t[name]).then_inc(sem("l1_loaded"), 16)
            pool.dma_start(w2_gnn[:], t["L1_gnn_W2"].rearrange("(c p) d -> p c d", p=P)).then_inc(sem("l1_loaded"), 16)
            pool.dma_start(up_w[:, 0, :], t["L1_ffn_W1s"]).then_inc(sem("l1_loaded"), 16)
            pool.dma_start(up_w[:, 1:, :], t["L1_ffn_W1p"].rearrange("e p f -> p e f")).then_inc(sem("l1_loaded"), 16)
            pool.dma_start(down_w[:, 0, :, :], t["L1_ffn_W2s"].rearrange("(c p) d -> p c d", p=P)).then_inc(sem("l1_loaded"), 16)
            for e in range(EXPERTS):
                pool.dma_start(down_w[:, 1 + e, :, :], t["L1_ffn_W2p"][e].rearrange("(c p) d -> p c d", p=P)).then_inc(sem("l1_loaded"), 16)
            with nc.allow_non_contiguous_dma(reason="small bias columns"):
                pool.dma_start(up_b[:, 0, :], t["L1_ffn_b1s"].rearrange("(c p) -> p c", p=P)).then_inc(sem("l1_loaded"), 16)
                pool.dma_start(up_b[:, 1:, :], t["L1_ffn_b1p"].rearrange("e (c p) -> p e c", p=P)).then_inc(sem("l1_loaded"), 16)
                for k in range(2):
                    pool.dma_start(col_b[:, 5 + k:6 + k], t["L1_gnn_b1"][k * P:(k + 1) * P].unsqueeze(1)).then_inc(sem("l1_loaded"), 16)
            pool.dma_start(down_b[0:EXPERTS, :], t["L1_ffn_b2p"]).then_inc(sem("l1_loaded"), 16)
            pool.dma_start(down_b[EXPERTS:EXPERTS + 1, :], t["L1_ffn_b2s"].unsqueeze(0)).then_inc(sem("l1_loaded"), 16)
            for k, name in enumerate(ROWS):
                pool.dma_start(row_b[:, k, :], t[name].partition_broadcast(P)).then_inc(sem("l1_loaded"), 16)
            pool.wait_ge(sem("l1_loaded"), L1_LOADS)
            pool.wait_ge(sem("recurrence_done"), 1)
            with pool.Fori(0, J) as j:
                n = j + 1
                for s in range(SLOTS):
                    pool.wait_ge(sem("y_done", s), n)
                    b0 = (j * SLOTS + s) * G
                    nc.gpsimd.tensor_copy(squares(tile(s, 11)),
                                          states[:, 1:, bass.ds(b0, G)].rearrange("p n b -> p b n")).then_inc(sem("c_hs", s), 1)
                for tag in ("c1", "c2"):
                    for s in range(SLOTS):
                        inverse_deviation(tag, s, n)
                for s in range(SLOTS):
                    vector_sum("c_x1_bo", s, n, (sem("c_block_x1", s), n), tile(s, 3), tile(s, 4), row("bo"))
                for s in range(SLOTS):
                    inverse_deviation("c3", s, n)
                for s in range(SLOTS):
                    vector_sum("c_x2_b2", s, n, at("c_x2n", s, n), tile(s, 3), tile(s, 5), row("b2"))
                for tag in ("c4", "c5"):
                    for s in range(SLOTS):
                        inverse_deviation(tag, s, n)

        @block.vector
        def _(dve):
            V = nc.vector

            def carry_wait():
                V.tensor_copy(waiting[:], ones[:, 0:1])

            def layer_norm(tag, s, n, src, dst):
                for b in range(G):
                    last = V.bn_stats(stats[:, s, b, :], squares(src)[:, b, :])
                last.then_inc(norm(tag, "stats", s, n)[0], 1)
                dve.wait_ge(*norm(tag, "stats", s, n))
                carry_wait()
                for b in range(G):
                    last = V.bn_aggr(moments[:, s, b, :], stats[:, s, b, :])
                last.then_inc(norm(tag, "moments", s, n)[0], 1)

            def normalize(tag, s, n, src, dst):
                dve.wait_ge(*norm(tag, "rstd", s, n))
                for b in range(G):
                    last = V.tensor_scalar(squares(dst)[:, b, :], squares(src)[:, b, :], moments[:, s, b, 0:1],
                                           rstd[:, s, b:b + 1], ALU.subtract, ALU.mult)
                last.then_inc(norm(tag, "normed", s, n)[0], 1)

            def gain_and_shift(tag, s, n, ap, gain, shift):
                dve.wait_ge(*norm(tag, "normed", s, n))
                V.tensor_tensor(squares(ap), squares(ap), row(gain), ALU.mult).then_inc(rises(tag + "_gained", s), 1)
                dve.wait_ge(*at(tag + "_gained", s, n))
                V.tensor_tensor(squares(ap), squares(ap), row(shift), ALU.add).then_inc(rises(tag + "_shifted", s), 1)
                dve.wait_ge(*at(tag + "_shifted", s, n))

            dve.wait_ge(sem("adj_t_psum"), 1)
            V.tensor_copy(adj_t[:], bank(0, 0)[:, 0:P]).then_inc(sem("adj_t"), 1)
            dve.wait_ge(sem("l0_loaded"), 16 * 6)
            V.tensor_scalar(col_b[:, 2:3], col_b[:, 1:2], 0.5, None, ALU.mult).then_inc(sem("b2_half"), 1)

            with dve.Fori(0, J) as j:
                n = j + 1
                for s in range(SLOTS):
                    dve.wait_ge(sem("x_in", s), 16 * n)
                    layer_norm("a1", s, n, tile(s, 0), None)
                for s in range(SLOTS):
                    normalize("a1", s, n, tile(s, 0), tile(s, 1))
                for s in range(SLOTS):
                    dve.wait_ge(*at("a_z1_psum", s, n))
                    V.tensor_copy(tile(s, 3), bank(s, 1)).then_inc(rises("a_z1", s), 1)
                for s in range(SLOTS):
                    dve.wait_ge(*at("a_h1_psum", s, n))
                    V.tensor_copy(tile(s, 5), bank(s, 0)).then_inc(rises("a_h1", s), 1)
                for s in range(SLOTS):
                    dve.wait_ge(*norm("a1", "normed", s, n))
                    V.scalar_tensor_tensor(tile(s, 0), tile(s, 1), 0.5, tile(s, 0), ALU.mult, ALU.add).then_inc(rises("a_x_half", s), 1)
                for s in range(SLOTS):
                    dve.wait_ge(*at("a_h2_psum", s, n))
                    dve.wait_ge(*at("a_x_half", s, n))
                    V.tensor_tensor(tile(s, 0), tile(s, 0), bank(s, 1), ALU.add).then_inc(sem("x1_done", s), 1)
                    dve.wait_ge(sem("x1_done", s), n)
                    layer_norm("a2", s, n, tile(s, 0), None)
                for s in range(SLOTS):
                    normalize("a2", s, n, tile(s, 0), tile(s, 8))

            dve.wait_ge(sem("gates_loaded"), 16 * 9)
            for k in (0, 2):
                V.tensor_scalar(gate_u[:, k, :], gate_u[:, k, :], 0.5, None, ALU.mult)
                V.tensor_scalar(gate_v[:, k, :], gate_v[:, k, :], 0.25, None, ALU.mult)
                V.tensor_scalar(gate_b[:, k:k + 1], gate_b[:, k:k + 1], 0.5, None, ALU.mult)
            V.tensor_scalar(gate_v[:, 1, :], gate_v[:, 1, :], 0.5, None, ALU.mult).then_inc(sem("gates_scaled"), 1)

            V.tensor_tensor(tmp[:], adj[:], adj_t[:], ALU.add).then_inc(sem("one_shot"), 1)
            dve.wait_ge(sem("one_shot"), 1)
            V.tensor_scalar(sym[:], tmp[:], 0.5, None, ALU.mult).then_inc(sem("one_shot"), 1)
            dve.wait_ge(sem("one_shot"), 2)
            V.tensor_reduce(sc[:, 0:1], sym[:], AX.X, ALU.add, apply_absolute_value=True).then_inc(sem("one_shot"), 1)
            dve.wait_ge(sem("one_shot"), 3)
            V.tensor_scalar(tmp2[:], ones[:], sc[:, 0:1], None, ALU.mult).then_inc(sem("e_spread"), 1)
            dve.wait_ge(sem("e_bound_psum"), 1)
            V.tensor_reduce(sc[:, 1:2], bank(0, 0)[:, 0:P], AX.X, ALU.max).then_inc(sem("one_shot"), 1)
            dve.wait_ge(sem("one_shot"), 4)
            V.scalar_tensor_tensor(power[:], ident[:], sc[:, 1:2], sym[:], ALU.mult, ALU.add).then_inc(sem("e_power"), 1)

            def trace_of(ap, count):
                V.tensor_tensor_reduce(tmp[:], ap, ident[:], 1.0, 0.0, ALU.mult, ALU.add, sc[:, 2:3]).then_inc(sem("e_diag"), 1)

            dve.wait_ge(sem("e_power"), 1)
            trace_of(power[:], 1)
            dve.wait_ge(sem("e_trace_psum"), 1)
            V.reciprocal(sc[:, 3:4], bank(0, 1)[:, 0:1]).then_inc(sem("e_inv"), 1)
            dve.wait_ge(sem("e_inv"), 1)
            V.tensor_scalar(power[:], power[:], sc[:, 3:4], None, ALU.mult).then_inc(sem("e_power"), 1)
            with dve.Fori(0, SQUARINGS) as q:
                dve.wait_ge(sem("e_square_psum"), q + 1)
                dve.wait_ge(sem("e_power"), q + 2)
                V.tensor_copy(tmp2[:], bank(0, 0)[:, 0:P]).then_inc(sem("e_copied"), 1)
                dve.wait_ge(sem("e_copied"), q + 1)
                trace_of(tmp2[:], q + 2)
                dve.wait_ge(sem("e_trace_psum"), q + 2)
                V.reciprocal(sc[:, 3:4], bank(0, 1)[:, 0:1]).then_inc(sem("e_inv"), 1)
                dve.wait_ge(sem("e_inv"), q + 2)
                V.tensor_scalar(power[:], tmp2[:], sc[:, 3:4], None, ALU.mult).then_inc(sem("e_power"), 1)
            dve.wait_ge(sem("e_power"), SQUARINGS + 2)
            trace_of(power[:], SQUARINGS + 2)
            dve.wait_ge(sem("e_diag"), SQUARINGS + 2)
            V.tensor_tensor_reduce(tmp[:], power[:], sym[:], 1.0, 0.0, ALU.mult, ALU.add, sc[:, 4:5]).then_inc(sem("e_rayleigh"), 1)
            dve.wait_ge(sem("e_trace_psum"), SQUARINGS + 2)
            V.tensor_copy(sc[:, 5:7], bank(0, 1)[:, 0:2]).then_inc(sem("one_shot"), 1)
            dve.wait_ge(sem("one_shot"), 5)
            V.reciprocal(sc[:, 7:8], sc[:, 5:6]).then_inc(sem("e_inv"), 1)
            dve.wait_ge(sem("e_inv"), SQUARINGS + 2)
            V.tensor_scalar(sc[:, 8:9], sc[:, 6:7], sc[:, 7:8], 1e-8, ALU.mult, ALU.add).then_inc(sem("one_shot"), 1)
            dve.wait_ge(sem("one_shot"), 6)
            V.reciprocal(sc[:, 9:10], sc[:, 8:9]).then_inc(sem("e_inv"), 1)
            dve.wait_ge(sem("e_inv"), SQUARINGS + 3)
            V.tensor_scalar(tmp2[:], adj_t[:], sc[:, 9:10], 2.0, ALU.mult, ALU.mult).then_inc(sem("one_shot"), 1)
            dve.wait_ge(sem("one_shot"), 7)
            V.tensor_tensor(lap_t[:], tmp2[:], ident[:], ALU.subtract).then_inc(sem("lap_t"), 1)
            V.tensor_scalar(tmp[:], adj[:], 0.0, None, ALU.is_gt).then_inc(sem("one_shot"), 1)
            dve.wait_ge(sem("one_shot"), 8)
            V.tensor_reduce(sc[:, 10:11], tmp[:], AX.X, ALU.max).then_inc(sem("one_shot"), 1)
            dve.wait_ge(sem("one_shot"), 9)
            V.tensor_scalar(tmp[:], tmp[:], sc[:, 10:11], 1e9, ALU.subtract, ALU.mult).then_inc(sem("one_shot"), 1)
            V.tensor_scalar(power[:], ident[:], sc[:, 10:11], None, ALU.mult).then_inc(sem("m_diag"), 1)
            dve.wait_ge(sem("one_shot"), 10)
            V.tensor_copy(mask_add[:], tmp[:].unsqueeze(1).to_broadcast([P, HEADS, P])).then_inc(sem("mask"), 1)
            dve.wait_ge(sem("m_any_psum"), 1)
            V.tensor_scalar(row_any[:], bank(0, 0)[:, 0:P], HD ** -0.5, None, ALU.mult).then_inc(sem("row_any"), 1)
            dve.wait_ge(sem("row_any"), 1)

            def recur(pair, n, k):
                now = pair * 2 + k
                V.scalar_tensor_tensor(state_cell[:], states[:, now, :], 0.5, cell[:], ALU.mult, ALU.mult).then_inc(rises("r_hc", k), 1)
                dve.wait_ge(sem("r_gates", k), n)
                V.scalar_tensor_tensor(in_cand[:], gates[:, k, 0, :], 1.0, gates[:, k, 1, :], ALU.add, ALU.mult).then_inc(rises("r_ic", k), 1)
                dve.wait_ge(*at("r_ic", k, n))
                dve.wait_ge(*at("r_hc", k, n))
                V.tensor_tensor(cell[:], state_cell[:], in_cand[:], ALU.add).then_inc(sem("r_cell", k), 1)
                dve.wait_ge(sem("r_cell", k), n)
                dve.wait_ge(sem("r_tanh", k), n)
                V.scalar_tensor_tensor(states[:, now + 1, :], gates[:, k, 2, :], 1.0, cell_tanh[:], ALU.add, ALU.mult).then_inc(sem("r_state", k), 1)
                dve.wait_ge(sem("r_state", k), n)

            with dve.Fori(0, N // 2) as pair:
                for k in range(2):
                    recur(pair, pair + 1, k)
            dve.wait_ge(sem("r_state", 1), N // 2)
            V.tensor_copy(sc[:, 12:13], ones[:, 0:1]).then_inc(sem("recurrence_done"), 1)
            dve.wait_ge(sem("l1_loaded"), L1_LOADS)

            def scores_of(s):
                return psum[:, 4 * s:4 * s + HEADS, :].rearrange("p h (b m) -> p (h b) m", b=G)

            with dve.Fori(0, J) as j:
                n = j + 1
                for s in range(SLOTS):
                    dve.wait_ge(sem("c_x1_in", s), 16 * n)
                    dve.wait_ge(*at("c_hs_psum", s, n))
                    V.scalar_tensor_tensor(tile(s, 0), bank(s, 0), 0.5, tile(s, 0), ALU.mult, ALU.add).then_inc(rises("c_x2", s), 1)
                    dve.wait_ge(*at("c_x2", s, n))
                    layer_norm("c1", s, n, tile(s, 0), None)
                for s in range(SLOTS):
                    normalize("c1", s, n, tile(s, 0), tile(s, 1))
                for s in range(SLOTS):
                    dve.wait_ge(*at("c_h_psum", s, n))
                    V.tensor_tensor(squares(tile(s, 3)), squares(bank(s, 0)), row("bc"), ALU.add).then_inc(rises("c_h", s), 1)
                    dve.wait_ge(*at("c_h", s, n))
                    layer_norm("c2", s, n, tile(s, 3), None)
                for s in range(SLOTS):
                    normalize("c2", s, n, tile(s, 3), tile(s, 3))
                    gain_and_shift("c2", s, n, tile(s, 3), "g1", "be1")
                    V.scalar_tensor_tensor(tile(s, 4), tile(s, 3), 0.0, tile(s, 1), ALU.max, ALU.add).then_inc(sem("c_block_x1", s), 1)
                for s in range(SLOTS):
                    dve.wait_ge(*at("c_q_psum", s, n))
                    dve.wait_ge(*at("c_x1_bo", s, n))
                    V.tensor_tensor(squares(tile(s, 4)), squares(bank(s, 0)), row_any[:].unsqueeze(1).to_broadcast([P, G, P]), ALU.mult).then_inc(sem("c_q", s), 1)
                for s in range(SLOTS):
                    dve.wait_ge(*at("c_v_psum", s, n))
                    V.tensor_copy(v_ones[:, s, :, :, 0:HD].rearrange("p b h d -> p (b h) d"),
                                  bank(s, 2).rearrange("p (c d) -> p c d", d=HD)).then_inc(sem("c_v", s), 1)
                for s in range(SLOTS):
                    dve.wait_ge(sem("c_s_psum", s), n)
                    V.tensor_reduce(top[:, s, :], scores_of(s), AX.X, ALU.max).then_inc(sem("c_max", s), 1)
                    dve.wait_ge(sem("c_max", s), n)
                    V.tensor_tensor(tile(s, 7, HEADS).rearrange("p (c m) -> p c m", m=P), scores_of(s),
                                    top[:, s, :].unsqueeze(2).to_broadcast([P, HEADS * G, P]),
                                    ALU.subtract).then_inc(sem("c_sub", s), 1)
                for s in range(SLOTS):
                    dve.wait_ge(sem("c_o_psum", s), n)
                    for half in range(2):
                        o = attended(s, half)
                        V.reciprocal(inv_sum[:, s, half], o[:, :, :, HD]).then_inc(sem("c_inv", s), 1)
                    for half in range(2):
                        dve.wait_ge(sem("c_inv", s), nth(n, 2, half))
                        out = squares(tile(s, 1))[:, 2 * half:2 * half + 2, :].rearrange("p b (h d) -> p b h d", h=HEADS)
                        last = V.tensor_tensor(out, attended(s, half)[:, :, :, 0:HD],
                                               inv_sum[:, s, half].unsqueeze(3).to_broadcast([P, 2, HEADS, HD]), ALU.mult)
                    last.then_inc(sem("c_o", s), 1)
                for s in range(SLOTS):
                    dve.wait_ge(*at("c_wo_psum", s, n))
                    dve.wait_ge(*at("c_x1_bo", s, n))
                    V.tensor_tensor(tile(s, 5), bank(s, 1), tile(s, 3), ALU.add).then_inc(rises("c_res2", s), 1)
                    dve.wait_ge(*at("c_res2", s, n))
                    layer_norm("c3", s, n, tile(s, 5), None)
                for s in range(SLOTS):
                    normalize("c3", s, n, tile(s, 5), tile(s, 5))
                    dve.wait_ge(*norm("c3", "normed", s, n))
                    V.tensor_tensor(squares(tile(s, 5)), squares(tile(s, 5)), row("g2"), ALU.mult).then_inc(rises("c3_gained", s), 1)
                    dve.wait_ge(*at("c3_gained", s, n))
                    V.tensor_tensor(squares(tile(s, 5)), squares(tile(s, 5)), row("be2"), ALU.add).then_inc(rises("c_x2n", s), 1)
                for s in range(SLOTS):
                    dve.wait_ge(*at("c_ff_psum", s, n))
                    dve.wait_ge(*at("c_x2_b2", s, n))
                    V.tensor_tensor(tile(s, 1), bank(s, 0), tile(s, 3), ALU.add).then_inc(rises("c_res3", s), 1)
                    dve.wait_ge(*at("c_res3", s, n))
                    layer_norm("c4", s, n, tile(s, 1), None)
                for s in range(SLOTS):
                    normalize("c4", s, n, tile(s, 1), tile(s, 1))
                    gain_and_shift("c4", s, n, tile(s, 1), "g3", "be3")
                    dve.wait_ge(sem("out_stored", s), 16 * j + 1)
                    V.tensor_tensor(tile(s, 12), tile(s, 0), tile(s, 1), ALU.add).then_inc(rises("c_x3", s), 1)
                    dve.wait_ge(*at("c_x3", s, n))
                    layer_norm("c5", s, n, tile(s, 12), None)
                for s in range(SLOTS):
                    normalize("c5", s, n, tile(s, 12), tile(s, 1))
                for s in range(SLOTS):
                    logits = bank(s, 0)[:, 0:G * EXPERTS].rearrange("p (b e) -> p b e", b=G)
                    R = [router[:, s, k] for k in range(7)]
                    dve.wait_ge(sem("d_logits_psum", s), n)
                    V.tensor_reduce(R[0][:, :, 0], logits, AX.X, ALU.max).then_inc(rises("d_max", s), 1)
                    dve.wait_ge(*at("d_max", s, n))
                    V.tensor_tensor(R[1], logits, R[0][:, :, 0:1].to_broadcast([P, G, EXPERTS]), ALU.subtract).then_inc(rises("d_sub", s), 1)
                for s in range(SLOTS):
                    R = [router[:, s, k] for k in range(7)]
                    dve.wait_ge(sem("d_exp", s), n)
                    carry_wait()
                    for b in range(G):
                        last = V.max(R[3][:, b, :], R[2][:, b, :])
                    last.then_inc(rises("d_top", s), 1)
                    dve.wait_ge(*at("d_top", s, n))
                    carry_wait()
                    for b in range(G):
                        last = V.max_index(best_idx[:, s, b, :], R[3][:, b, :], R[2][:, b, :])
                    last.then_inc(rises("d_idx", s), 1)
                    V.tensor_tensor(R[0][:, :, 0], R[3][:, :, 0], R[3][:, :, 1], ALU.add).then_inc(rises("d_den", s), 1)
                    dve.wait_ge(*at("d_den", s, n))
                    V.reciprocal(R[0][:, :, 1], R[0][:, :, 0]).then_inc(rises("d_inv", s), 1)
                    dve.wait_ge(*at("d_inv", s, n))
                    V.tensor_tensor(R[0][:, :, 2:4], R[3][:, :, 0:2], R[0][:, :, 1:2].to_broadcast([P, G, 2]), ALU.mult).then_inc(rises("d_w", s), 1)
                    dve.wait_ge(*at("d_idx", s, n))
                    V.tensor_copy(R[0][:, :, 4:6], best_idx[:, s, :, 0:2]).then_inc(rises("d_idxf", s), 1)
                    dve.wait_ge(*at("d_w", s, n))
                    dve.wait_ge(*at("d_idxf", s, n))
                    for k in range(2):
                        V.tensor_tensor(R[4 + k], expert_no[:], R[0][:, :, 4 + k:5 + k].to_broadcast([P, G, EXPERTS]), ALU.is_equal).then_inc(rises(f"d_eq{k}", s), 1)
                        dve.wait_ge(*at(f"d_eq{k}", s, n))
                        V.tensor_tensor(R[4 + k], R[4 + k], R[0][:, :, 2 + k:3 + k].to_broadcast([P, G, EXPERTS]), ALU.mult).then_inc(rises(f"d_part{k}", s), 1)
                        dve.wait_ge(*at(f"d_part{k}", s, n))
                    V.tensor_tensor(R[6], R[4], R[5], ALU.add).then_inc(sem("d_mask", s), 1)
                    dve.wait_ge(sem("d_mask", s), n)
                for e in range(1 + EXPERTS):
                    for s in range(SLOTS):
                        y = tile(s, 12)
                        dve.wait_ge(sem("d_down_psum", s), nth(n, 1 + EXPERTS, e))
                        if e == 0:
                            V.tensor_tensor(y, y, bank(s, 2), ALU.add).then_inc(sem("d_y", s), 1)
                            dve.wait_ge(sem("d_y", s), nth(n, EXPERTS, e))
                            continue
                        dve.wait_ge(sem("d_y", s), nth(n, EXPERTS, e - 1))
                        for b in range(G):
                            last = V.scalar_tensor_tensor(squares(y)[:, b, :], squares(bank(s, 2 + e % 2))[:, b, :],
                                                          router[:, s, 6, b, e - 1:e], squares(y)[:, b, :], ALU.mult, ALU.add)
                        last.then_inc(sem("d_y", s) if e < EXPERTS else sem("y_done", s), 1)

        @block.scalar
        def _(act):
            A = nc.scalar
            for k, name in enumerate("ico"):
                act.dma_start(gate_u[:, k, :], t["L0_ffn_U_" + name]).then_inc(sem("gates_loaded"), 16)
                act.dma_start(gate_v[:, k, :], t["L0_ffn_V_" + name]).then_inc(sem("gates_loaded"), 16)
                act.dma_start(gate_b[:, k:k + 1], t["L0_ffn_b_" + name].unsqueeze(1)).then_inc(sem("gates_loaded"), 16)
            act.wait_ge(sem("l0_loaded"), 16 * 6)
            act.wait_ge(sem("b2_half"), 1)
            with act.Fori(0, J) as j:
                n = j + 1
                for s in range(SLOTS):
                    act.wait_ge(*at("a_xt_psum", s, n))
                    A.copy(tile(s, 2), bank(s, 0)).then_inc(rises("a_xt", s), 1)
                for s in range(SLOTS):
                    act.wait_ge(*at("a_h1t_psum", s, n))
                    A.activation(tile(s, 4), bank(s, 2), ACT.Relu, bias=col_b[:, 0:1]).then_inc(rises("a_h1t", s), 1)
                for s in range(SLOTS):
                    act.wait_ge(*at("a_z2_psum", s, n))
                    A.copy(tile(s, 6), bank(s, 1)).then_inc(rises("a_z2", s), 1)
                for s in range(SLOTS):
                    act.wait_ge(*at("a_h2t_psum", s, n))
                    A.activation(tile(s, 7), bank(s, 2), ACT.Relu, bias=col_b[:, 2:3], scale=0.5).then_inc(rises("a_h2t", s), 1)
                for s in range(SLOTS):
                    act.wait_ge(*at("a_x1t_psum", s, n))
                    b0 = (j * SLOTS + s) * G
                    A.copy(states[:, 1:, bass.ds(b0, G)].rearrange("p n b -> p b n"), squares(bank(s, 3))).then_inc(rises("a_x1t", s), 1)

            act.wait_ge(sem("gates_scaled"), 1)
            with act.Fori(0, N // 2) as pair:
                for k in range(2):
                    n = pair + 1
                    act.wait_ge(sem("r_zic_psum", k), n)
                    A.activation(gates[:, k, 0, :], psum[:, 2 * k, 0:B], ACT.Tanh, bias=gate_b[:, 0:1])
                    A.activation(gates[:, k, 1, :], psum[:, 2 * k, B:2 * B], ACT.Tanh, bias=gate_b[:, 1:2]).then_inc(sem("r_gates", k), 1)
                    act.wait_ge(sem("r_zo_psum", k), n)
                    A.activation(gates[:, k, 2, :], psum[:, 2 * k + 1, 0:B], ACT.Tanh, bias=gate_b[:, 2:3]).then_inc(sem("r_out_gate", k), 1)
                    act.wait_ge(sem("r_cell", k), n)
                    A.activation(cell_tanh[:], cell[:], ACT.Tanh, scale=0.5).then_inc(sem("r_tanh", k), 1)

            act.wait_ge(sem("l1_loaded"), L1_LOADS)
            with act.Fori(0, J) as j:
                n = j + 1
                for s in range(SLOTS):
                    act.wait_ge(*at("c_xp_psum", s, n))
                    A.copy(tile(s, 2), bank(s, 1)).then_inc(rises("c_xp", s), 1)
                for s in range(SLOTS):
                    act.wait_ge(*at("c_x1t_psum", s, n))
                    A.copy(tile(s, 2), bank(s, 1)).then_inc(rises("c_x1t", s), 1)
                for s in range(SLOTS):
                    act.wait_ge(*at("c_k_psum", s, n))
                    A.copy(tile(s, 5), bank(s, 1)).then_inc(sem("c_k", s), 1)

                for s in range(SLOTS):
                    act.wait_ge(sem("c_sub", s), n)
                    A.activation(tile(s, 7, HEADS), tile(s, 7, HEADS), ACT.Exp).then_inc(sem("c_exp", s), 1)
                for h in range(HEADS):
                    for s in range(SLOTS):
                        act.wait_ge(sem("c_pt_psum", s), nth(n, HEADS, h))
                        A.copy(tile(s, 13 + h), bank(s, h % 2)).then_inc(sem("c_pt", s), 1)
                for s in range(SLOTS):
                    act.wait_ge(*at("c_ot_psum", s, n))
                    A.copy(tile(s, 2), bank(s, 0)).then_inc(rises("c_ot", s), 1)
                for s in range(SLOTS):
                    act.wait_ge(*at("c_x2t_psum", s, n))
                    A.copy(tile(s, 2), bank(s, 0)).then_inc(rises("c_x2t", s), 1)
                for k in range(2):
                    for s in range(SLOTS):
                        act.wait_ge(sem("c_up_psum", s), nth(n, 2, k))
                        A.activation(tile(s, 7 + k), bank(s, 1 + k), ACT.Gelu, bias=col_b[:, 5 + k:6 + k]).then_inc(sem("c_up", s), 1)
                for s in range(SLOTS):
                    act.wait_ge(*at("c_x4t_psum", s, n))
                    A.copy(tile(s, 2), bank(s, 1)).then_inc(rises("c_x4t", s), 1)
                for s in range(SLOTS):
                    act.wait_ge(*at("d_sub", s, n))
                    A.activation(router[:, s, 2], router[:, s, 1], ACT.Exp).then_inc(sem("d_exp", s), 1)
                for s in range(SLOTS):
                    act.wait_ge(sem("d_maskt_psum", s), n)
                    A.copy(mask_t[0:EXPERTS, s, :], bank(s, 1)[0:EXPERTS, :]).then_inc(sem("d_maskt", s), 1)
                for e in range(1 + EXPERTS):
                    for c in range(FC):
                        for s in range(SLOTS):
                            act.wait_ge(sem("d_up_psum", s), nth(n, FC * (1 + EXPERTS), FC * e + c))
                            A.activation(tile(s, 13 + c), bank(s, c % 2), ACT.Gelu, bias=up_b[:, e, c:c + 1]).then_inc(sem("d_up", s), 1)

        @block.tensor
        def _(pe):
            T = nc.tensor

            def transposes(s, src, k, done, rows=P):
                for b in range(G):
                    last = T.transpose(squares(bank(s, k))[:rows, b, :], src[:, b, :], ident[:])
                last.then_inc(done, 1)

            def by_square(s, k, left, right, done, start=True, stop=True):
                for b in range(G):
                    last = T.matmul(squares(bank(s, k))[:, b, :], left[:, b, :], right, start=start and b == 0,
                                    stop=stop, skip_group_check=True)
                if done is not None:
                    last.then_inc(done, 1)

            pe.wait_ge(sem("adj_loaded"), 16)
            pe.wait_ge(sem("consts"), 1)
            T.transpose(bank(0, 0)[:, 0:P], adj[:], ident[:]).then_inc(sem("adj_t_psum"), 1)
            pe.wait_ge(sem("adj_t"), 1)
            pe.wait_ge(sem("l0_loaded"), 16 * 6)
            with pe.Fori(0, J) as j:
                n = j + 1
                for s in range(SLOTS):
                    pe.wait_ge(*norm("a1", "normed", s, n))
                    transposes(s, squares(tile(s, 1)), 0, rises("a_xt_psum", s))
                    by_square(s, 1, squares(tile(s, 1)), adj_t[:], rises("a_z1_psum", s))
                for s in range(SLOTS):
                    pe.wait_ge(*at("a_xt", s, n))
                    T.matmul(bank(s, 2), W["L0_gnn_w1_loop"][:], tile(s, 2), start=True, stop=False)
                    pe.wait_ge(*at("a_z1", s, n))
                    T.matmul(bank(s, 2), W["L0_gnn_w1_neigh"][:], tile(s, 3), start=False, stop=True).then_inc(rises("a_h1t_psum", s), 1)
                for s in range(SLOTS):
                    pe.wait_ge(*at("a_h1t", s, n))
                    transposes(s, squares(tile(s, 4)), 0, rises("a_h1_psum", s))
                for s in range(SLOTS):
                    pe.wait_ge(*at("a_h1", s, n))
                    by_square(s, 1, squares(tile(s, 5)), adj_t[:], rises("a_z2_psum", s))
                for s in range(SLOTS):
                    T.matmul(bank(s, 2), W["L0_gnn_w2_loop"][:], tile(s, 4), start=True, stop=False)
                    pe.wait_ge(*at("a_z2", s, n))
                    T.matmul(bank(s, 2), W["L0_gnn_w2_neigh"][:], tile(s, 6), start=False, stop=True).then_inc(rises("a_h2t_psum", s), 1)
                for s in range(SLOTS):
                    pe.wait_ge(*at("a_h2t", s, n))
                    transposes(s, squares(tile(s, 7)), 1, rises("a_h2_psum", s))
                for s in range(SLOTS):
                    pe.wait_ge(*norm("a2", "normed", s, n))
                    pe.wait_ge(*at("a_x1t", s, j))
                    transposes(s, squares(tile(s, 8)), 3, rises("a_x1t_psum", s))

            pe.wait_ge(sem("e_spread"), 1)
            T.transpose(bank(0, 0)[:, 0:P], tmp2[:], ident[:]).then_inc(sem("e_bound_psum"), 1)
            pe.wait_ge(sem("e_diag"), 1)
            T.matmul(bank(0, 1)[:, 0:1], ones[:], sc[:, 2:3], start=True, stop=True).then_inc(sem("e_trace_psum"), 1)
            with pe.Fori(0, SQUARINGS) as q:
                pe.wait_ge(sem("e_power"), q + 2)
                T.matmul(bank(0, 0)[:, 0:P], power[:], power[:], start=True, stop=True).then_inc(sem("e_square_psum"), 1)
                pe.wait_ge(sem("e_diag"), q + 2)
                T.matmul(bank(0, 1)[:, 0:1], ones[:], sc[:, 2:3], start=True, stop=True).then_inc(sem("e_trace_psum"), 1)
            pe.wait_ge(sem("e_rayleigh"), 1)
            T.matmul(bank(0, 1)[:, 0:1], ones[:], sc[:, 2:3], start=True, stop=True)
            T.matmul(bank(0, 1)[:, 1:2], ones[:], sc[:, 4:5], start=True, stop=True).then_inc(sem("e_trace_psum"), 1)
            pe.wait_ge(sem("m_diag"), 1)
            T.matmul(bank(0, 0)[:, 0:P], ones[:], power[:], start=True, stop=True).then_inc(sem("m_any_psum"), 1)
            pe.wait_ge(sem("row_any"), 1)

            pe.wait_ge(sem("gates_scaled"), 1)
            for s in range(SLOTS):
                pe.wait_ge(*at("a_x1t", s, J))

            def gate_bank(k, g):
                return psum[:, 2 * k + (g == 2), (g % 2) * B:(g % 2 + 1) * B]

            def input_part(now, k):
                for g in range(3):
                    T.matmul(gate_bank(k, g), gate_u[:, g, :], states[:, now, :], start=(g != 1), stop=False, skip_group_check=True)

            def state_part(now, k):
                for g in range(3):
                    last = T.matmul(gate_bank(k, g), gate_v[:, g, :], states[:, now, :], start=False, stop=True, skip_group_check=True)
                    if g == 1:
                        last.then_inc(sem("r_zic_psum", k), 1)
                last.then_inc(sem("r_zo_psum", k), 1)

            input_part(1, 0)
            state_part(0, 0)
            input_part(2, 1)
            with pe.Fori(0, N // 2 - 1) as pair:
                pe.wait_ge(sem("r_state", 0), pair + 1)
                state_part(pair * 2 + 1, 1)
                input_part(pair * 2 + 3, 0)
                pe.wait_ge(sem("r_state", 1), pair + 1)
                state_part(pair * 2 + 2, 0)
                input_part(pair * 2 + 4, 1)
            pe.wait_ge(sem("r_state", 0), N // 2)
            state_part(N - 1, 1)

            pe.wait_ge(sem("l1_loaded"), L1_LOADS)
            pe.wait_ge(sem("lap_t"), 1)
            pe.wait_ge(sem("mask"), 1)
            pe.wait_ge(sem("recurrence_done"), 1)

            def scores(s):
                for h in range(HEADS):
                    T.matmul(bank(s, h), ident_h[:], mask_add[:].rearrange("p b m -> p (b m)"), start=True,
                             stop=False, skip_group_check=True)
                for b in range(G):
                    for h in range(HEADS):
                        rows = slice(h * HD, (h + 1) * HD)
                        last = T.matmul(squares(bank(s, h))[:, b, :], tile(s, 4)[rows, b * P:(b + 1) * P],
                                        tile(s, 5)[rows, b * P:(b + 1) * P], start=False, stop=True, skip_group_check=True)
                last.then_inc(sem("c_s_psum", s), 1)

            def weighted_values(s, n, h):
                pe.wait_ge(sem("c_pt", s), nth(n, HEADS, h))
                for b in range(G):
                    last = T.matmul(attended(s, b // 2)[:, b % 2, h, :], squares(tile(s, 13 + h))[:, b, :],
                                    v_ones[:, s, b, h, :], start=(h == 0 and b % 2 == 0), stop=True, skip_group_check=True)
                if h == HEADS - 1:
                    last.then_inc(sem("c_o_psum", s), 1)

            with pe.Fori(0, J) as j:
                n = j + 1
                for s in range(SLOTS):
                    pe.wait_ge(sem("c_hs", s), n)
                    transposes(s, squares(tile(s, 11)), 0, rises("c_hs_psum", s))
                for s in range(SLOTS):
                    pe.wait_ge(*norm("c1", "normed", s, n))
                    by_square(s, 1, squares(tile(s, 1)), lap_t[:], rises("c_xp_psum", s))
                for s in range(SLOTS):
                    pe.wait_ge(*at("c_xp", s, n))
                    by_square(s, 0, squares(tile(s, 2)), W["L1_gnn_Wc"][:], rises("c_h_psum", s))
                for s in range(SLOTS):
                    pe.wait_ge(sem("c_block_x1", s), n)
                    transposes(s, squares(tile(s, 4)), 1, rises("c_x1t_psum", s))
                for s in range(SLOTS):
                    pe.wait_ge(*at("c_x1t", s, n))
                    T.matmul(bank(s, 0), W["L1_gnn_Wq"][:], tile(s, 2), start=True, stop=True).then_inc(rises("c_q_psum", s), 1)
                    T.matmul(bank(s, 1), W["L1_gnn_Wk"][:], tile(s, 2), start=True, stop=True).then_inc(rises("c_k_psum", s), 1)
                    by_square(s, 2, squares(tile(s, 2)), W["L1_gnn_Wv"][:], rises("c_v_psum", s))
                for s in range(SLOTS):
                    pe.wait_ge(sem("c_q", s), n)
                    pe.wait_ge(sem("c_k", s), n)
                    pe.wait_ge(sem("c_v", s), n)
                    scores(s)
                for h in range(HEADS):
                    for s in range(SLOTS):
                        if h == 0:
                            pe.wait_ge(sem("c_exp", s), n)
                        if h >= 2:
                            pe.wait_ge(sem("c_pt", s), nth(n, HEADS, h - 2))
                        transposes(s, squares(tile(s, 7 + h)), h % 2, sem("c_pt_psum", s))
                    if h > 0:
                        for s in range(SLOTS):
                            weighted_values(s, n, h - 1)
                for s in range(SLOTS):
                    weighted_values(s, n, HEADS - 1)
                for s in range(SLOTS):
                    pe.wait_ge(sem("c_o", s), n)
                    transposes(s, squares(tile(s, 1)), 0, rises("c_ot_psum", s))
                for s in range(SLOTS):
                    pe.wait_ge(*at("c_ot", s, n))
                    by_square(s, 1, squares(tile(s, 2)), W["L1_gnn_Wo"][:], rises("c_wo_psum", s))
                for s in range(SLOTS):
                    pe.wait_ge(*at("c_x2n", s, n))
                    transposes(s, squares(tile(s, 5)), 0, rises("c_x2t_psum", s))
                for s in range(SLOTS):
                    pe.wait_ge(*at("c_x2t", s, n))
                    for k in range(2):
                        T.matmul(bank(s, 1 + k), W["L1_gnn_W1"][:, k * P:(k + 1) * P], tile(s, 2), start=True, stop=True).then_inc(sem("c_up_psum", s), 1)
                for s in range(SLOTS):
                    for b in range(G):
                        for k in range(2):
                            if b == 0:
                                pe.wait_ge(sem("c_up", s), nth(n, 2, k))
                            last = T.matmul(squares(bank(s, 0))[:, b, :], squares(tile(s, 7 + k))[:, b, :], w2_gnn[:, k, :],
                                            start=(b == 0 and k == 0), stop=(k == 1), skip_group_check=True)
                    last.then_inc(rises("c_ff_psum", s), 1)
                for s in range(SLOTS):
                    pe.wait_ge(*norm("c5", "normed", s, n))
                    transposes(s, squares(tile(s, 1)), 1, rises("c_x4t_psum", s))
                for s in range(SLOTS):
                    pe.wait_ge(*at("c_x4t", s, n))
                    for b in range(G):
                        last = T.matmul(bank(s, 0)[:, b * EXPERTS:(b + 1) * EXPERTS], squares(tile(s, 2))[:, b, :],
                                        W["L1_ffn_Wr"][:], start=(b == 0), stop=True, skip_group_check=True)
                    last.then_inc(sem("d_logits_psum", s), 1)
                for s in range(SLOTS):
                    pe.wait_ge(sem("d_mask", s), n)
                    for b in range(G):
                        last = T.transpose(squares(bank(s, 1))[0:EXPERTS, b, :], router[:, s, 6, b, :], ident[:])
                    last.then_inc(sem("d_maskt_psum", s), 1)
                for e in range(1 + EXPERTS):
                    for c in range(FC):
                        for s in range(SLOTS):
                            if e == 0 and c == 1:
                                pe.wait_ge(sem("d_maskt", s), n)
                            if c >= 2:
                                pe.wait_ge(sem("d_up", s), nth(n, FC * (1 + EXPERTS), FC * e + c - 2))
                            T.matmul(bank(s, c % 2), up_w[:, e, c * P:(c + 1) * P], tile(s, 2), start=True, stop=True).then_inc(sem("d_up_psum", s), 1)
                    for s in range(SLOTS):
                        k = 2 + e % 2
                        if e >= 2:
                            pe.wait_ge(sem("d_y", s), nth(n, EXPERTS, e - 2))
                        for b in range(G):
                            for c in range(FC):
                                if b == 0:
                                    pe.wait_ge(sem("d_up", s), nth(n, FC * (1 + EXPERTS), FC * e + c))
                                last = T.matmul(squares(bank(s, k))[:, b, :], squares(tile(s, 13 + c))[:, b, :], down_w[:, e, c, :],
                                                start=(b == 0 and c == 0), stop=(c == FC - 1), skip_group_check=True)
                            if e == 0:
                                last = T.matmul(squares(bank(s, k))[:, b, :], mask_t[:, s, b * P:(b + 1) * P], down_b[:],
                                                start=False, stop=True, skip_group_check=True)
                        last.then_inc(sem("d_down_psum", s), 1)
    return nc


_IN = ("x", "adj", "L0_gnn_w1_loop", "L0_gnn_w1_neigh", "L0_gnn_b1", "L0_gnn_w2_loop", "L0_gnn_w2_neigh",
       "L0_gnn_b2", "L0_ffn_U_i", "L0_ffn_V_i", "L0_ffn_b_i", "L0_ffn_U_c", "L0_ffn_V_c", "L0_ffn_b_c",
       "L0_ffn_U_o", "L0_ffn_V_o", "L0_ffn_b_o", "L1_gnn_Wc", "L1_gnn_bc", "L1_gnn_g1", "L1_gnn_be1",
       "L1_gnn_Wq", "L1_gnn_Wk", "L1_gnn_Wv", "L1_gnn_Wo", "L1_gnn_bo", "L1_gnn_g2", "L1_gnn_be2", "L1_gnn_W1",
       "L1_gnn_b1", "L1_gnn_W2", "L1_gnn_b2", "L1_gnn_g3", "L1_gnn_be3", "L1_ffn_Wr", "L1_ffn_W1s", "L1_ffn_b1s",
       "L1_ffn_W2s", "L1_ffn_b2s", "L1_ffn_W1p", "L1_ffn_b1p", "L1_ffn_W2p", "L1_ffn_b2p")


def kernel(**inputs):
    import numpy as _np
    import concourse.bacc as _bacc
    from concourse import mybir as _mybir
    from concourse.bass_utils import run_bass_kernel_spmd as _run

    nc = _bacc.Bacc("TRN2", target_bir_lowering=False, num_devices=1)
    arrays, tensors = {}, {}
    for name in _IN:
        a = _np.ascontiguousarray(inputs[name])
        arrays[f"in_{name}"] = a
        tensors[name] = nc.dram_tensor(f"in_{name}", a.shape, _mybir.dt.from_np(a.dtype), kind="ExternalInput").ap()
    tensors["out"] = nc.dram_tensor("out_0", (128, 128, 128), _mybir.dt.float32, kind="ExternalOutput").ap()
    build(nc, tensors)
    r = _run(nc, [arrays], core_ids=[0])
    return r.results[0]["out_0"]
```

```python
from contextlib import ExitStack

import concourse.bass as bass
from concourse import mybir

P = 128
G = 2
GROUP = G * P
BANK = 512
LANES = 4
SLOTS = 2
PAIR = LANES // SLOTS * G
HEADS = 4
HD = P // HEADS
EXPERTS = 8
FF = 512
FC = FF // P
TOP = 2
ROW = P + 4
TILE = 512
SUB = TILE // P
TOKENS = P * P
REGION = TOKENS + TILE
TILES = (TOP * TOKENS + EXPERTS * (TILE - 1)) // TILE
TILES += TILES % 2
SQUARINGS = 28
EPS = 1e-5
L1_LOADS = 16 * (7 + 1 + 1 + 1 + 1 + EXPERTS + 2 + 2 + 2 + 9)
F32 = mybir.dt.float32
BF16 = mybir.dt.bfloat16
U32 = mybir.dt.uint32
I32 = mybir.dt.int32
ALU = mybir.AluOpType
ACT = mybir.ActivationFunctionType
AX = mybir.AxisListType


def build(nc, t):
    B, N, D = t["x"].shape
    assert B == N == D == P
    J = B // (G * LANES)
    ctx = ExitStack()
    with ctx:
        def sb(name, shape, dt=F32):
            return ctx.enter_context(nc.sbuf_tensor(name, shape, dt))

        sems = {}

        def sem(name, *which):
            key = "_".join([name, *map(str, which)])
            if key not in sems:
                sems[key] = ctx.enter_context(nc.semaphore(key))
            return sems[key]

        psum = ctx.enter_context(nc.psum_tensor("psum", [P, 8, BANK], F32))

        def early(eng, *values):
            for v in values:
                eng.compute_val(v)
            return values

        def nth(n, per_pass, k):
            return n * per_pass + (k + 1 - per_pass)

        SHARED = {
            "a_psum": ("a_xt_psum", "a_z1_psum", "a_h1t_psum", "a_h1_psum", "a_z2_psum", "a_h2t_psum", "a_h2_psum",
                       "a_x1t_psum"),
            "a_dve": ("a1_stats", "a1_moments", "a1_normed", "a_z1", "a_h1", "a_x_half", "a_x1", "a2_stats",
                      "a2_moments", "a2_normed"),
            "a_act": ("a_xt", "a_h1t", "a_z2", "a_h2t", "a_x1t"),
            "a_pool": ("a1_var", "a1_rstd", "a2_var", "a2_rstd"),
            "r_cells": ("r_hc", "r_ic", "r_cell", "r_state"),
            "r_z_psum": ("r_zic_psum", "r_zo_psum"),
            "r_tanhs": ("r_gates", "r_out_gate", "r_tanh"),
            "c_psum": ("c_hs_psum", "c_xp_psum", "c_h_psum", "c_x1t_psum", "c_q_psum", "c_kv_psum", "c_s_psum",
                       "c_pt0_psum", "c_pt1_psum", "c_o_psum", "c_ot_psum", "c_wo_psum", "c_x2t_psum", "c_up0_psum",
                       "c_up1_psum", "c_ff_psum", "c_x4t_psum", "d_up0_psum", "d_up1_psum", "d_up2_psum",
                       "d_up3_psum", "d_down_psum"),
            "c_act": ("c_xp", "c_x1t", "c_k", "c_v", "c_exp", "c_pt0", "c_pt1", "c_ot", "c_x2t", "c_up0", "c_up1",
                      "c_x4t", "d_up0", "d_up1", "d_up2", "d_up3"),
            "c_dve": ("c_x2", "c1_stats", "c1_moments", "c1_normed", "c_h", "c2_stats", "c2_moments", "c2_gained",
                      "c2_shifted", "c_block_x1", "c_q", "c_max", "c_negmax", "c_inv", "c_o", "c_res2", "c3_stats",
                      "c3_moments", "c3_gained", "c_x2n", "c_res3", "c4_stats", "c4_moments", "c4_gained", "c_x3",
                      "c5_stats", "c5_moments", "c5_normed", "d_y"),
            "c_pool": ("c1_var", "c1_rstd", "c2_var", "c2_rstd", "c_x1_bo", "c_x_be3", "c3_var", "c3_rstd", "c_x2_b2",
                       "c4_var", "c4_rstd", "c5_var", "c5_rstd"),
            "d_psum": ("d_logits_psum", "d_places_psum", "d_maskt_psum"),
            "d_act": ("d_exp", "d_maskt"),
            "d_route": ("d_max", "d_sub", "d_top", "d_idx", "d_den", "d_inv", "d_w", "d_idxf", "d_eq0", "d_eq1",
                        "d_chosen", "d_part0", "d_part1", "d_mask", "d_place", "d_prod0", "d_prod1",
                        "d_slot0", "d_slot1", "d_slots"),
            "m_psum": ("m_xt_psum", "m_up0_psum", "m_up1_psum", "m_up2_psum", "m_up3_psum", "m_down_psum"),
            "m_act": ("m_xt", "m_h0", "m_h1", "m_h2", "m_h3"),
            "m_weights": ("m_is_first", "m_diff", "m_part", "m_weight", "m_ids"),
        }
        AHEAD = {"a_act": LANES, "x1_stored": LANES, "out_stored": LANES, "rows_free": SLOTS, "m_psum": SLOTS,
                 "m_y": SLOTS, "m_free": SLOTS, "m_weights": SLOTS}
        PLACE = {step: (name, len(steps), k) for name, steps in SHARED.items() for k, step in enumerate(steps)}

        def rises(step, s):
            return sem(PLACE[step][0], s)

        def at(step, s, n):
            name, per_pass, k = PLACE[step]
            return sem(name, s), nth(n, per_pass, k) + (1 if name in AHEAD else 0)

        def bank(s, k):
            return psum[:, 4 * s + k, :]

        def lane_bank(s, k):
            return psum[:, 2 * s + k % 2, k // 2 * GROUP:(k // 2 + 1) * GROUP]

        def lane_banks(s):
            return psum[:, 2 * s:2 * s + 2, :]

        def lane(s, k, n=1):
            at_col = (s * 16 + k) * GROUP
            return room[:, at_col:at_col + n * GROUP]

        def lanes_of(pair):
            return range(PAIR // G * pair, PAIR // G * (pair + 1))

        def tokens_of(s):
            return slice(s % (PAIR // G) * G, (s % (PAIR // G) + 1) * G)

        def squares(ap):
            return ap.rearrange("p (b f) -> p b f", f=P)

        def attended(s):
            return lane_banks(s)[:, :, 0:HEADS * (HD + 1)].rearrange("p b (h d) -> p b h d", h=HEADS)

        states = sb("states", [P, N + 1, B])
        room = sb("room", [P, LANES * 16 * GROUP])
        v_ones = sb("v_ones", [P, LANES, G, HEADS, HD + 1])

        def tile(s, k, n=1):
            at_col = (s * 16 + k) * BANK
            return room[:, at_col:at_col + n * BANK]

        W = {}
        for name, cols in (("L0_gnn_w1_loop", P), ("L0_gnn_w1_neigh", P), ("L0_gnn_w2_loop", P),
                           ("L0_gnn_w2_neigh", P), ("L1_gnn_Wc", P), ("L1_gnn_Wq", P),
                           ("L1_gnn_Wk", P), ("L1_gnn_Wv", P), ("L1_gnn_Wo", P), ("L1_gnn_W1", 2 * P),
                           ("L1_ffn_Wr", EXPERTS)):
            W[name] = sb("w_" + name, [P, cols])
        gate_u = sb("gate_u", [P, 3, P])
        gate_v = sb("gate_v", [P, 3, P])
        w2_gnn = sb("w2_gnn", [P, 2, P])
        up_w = sb("up_w", [P, 1 + EXPERTS, FF])
        down_w = sb("down_w", [P, 1 + EXPERTS, FC, P])
        up_b = sb("up_b", [P, 1 + EXPERTS, FC])
        down_b = sb("down_b", [EXPERTS + 1, P])
        col_b = sb("col_b", [P, 8])
        gate_b = sb("gate_b", [P, 3])
        ROWS = ("L1_gnn_bc", "L1_gnn_g1", "L1_gnn_be1", "L1_gnn_bo", "L1_gnn_g2", "L1_gnn_be2",
                "L1_gnn_b2", "L1_gnn_g3", "L1_gnn_be3")
        row_b = sb("row_b", [P, len(ROWS), P])

        def row(name):
            return row_b[:, ROWS.index("L1_gnn_" + name), :].unsqueeze(1).to_broadcast([P, G, P])

        adj = sb("adj", [P, P])
        adj_t = sb("adj_t", [P, P])
        lap_t = sb("lap_t", [P, P])
        ident = sb("ident", [P, P])
        ident_h = sb("ident_h", [P, P], BF16)
        ones = sb("ones", [P, P])
        mask_add = sb("mask_add", [P, HEADS, P], BF16)
        row_any = sb("row_any", [P, P])
        sc = sb("sc", [P, 16])
        expert_no = sb("expert_no", [P, PAIR, EXPERTS])
        head_col = sb("head_col", [P, HEADS])
        half_neg = sb("half_neg", [P, G])
        eps_tile = sb("eps_tile", [P, G])
        starts = sb("starts", [P, 64])
        waiting = sb("waiting", [P, 1])
        sym, power, tmp, tmp2 = (lane(1, 9, 2)[:, k * P:(k + 1) * P] for k in range(4))
        cell, state_cell, in_cand, cell_tanh = (lane(0, 9, 2)[:, k * B:(k + 1) * B] for k in range(4))
        gates = lane(0, 11, 3)[:, 0:6 * B].rearrange("p (k g b) -> p k g b", k=2, g=3)
        stats = sb("stats", [P, LANES, G, 6])
        moments = sb("moments", [P, LANES, G, 2])
        rstd = sb("rstd", [P, LANES, G])
        top = sb("top", [P, LANES, 2, G * HEADS])
        inv_sum = sb("inv_sum", [P, LANES, G, HEADS])
        router = sb("router", [P, SLOTS, 12, PAIR, EXPERTS])
        best_idx = sb("best_idx", [P, SLOTS, PAIR, 8], U32)
        routed = sb("routed", [P, SLOTS, SUB, ROW])
        assert PAIR == SUB
        padding = sb("padding", [P, SUB, ROW])
        token_no = sb("token_no", [P, B], I32)
        before = sb("before", [P, P])
        region_at = sb("region_at", [P, EXPERTS])
        next_row = sb("next_row", [P, EXPERTS])
        row_idx = sb("row_idx", [P, SLOTS, PAIR, TOP], U32)
        row_weight = sb("row_weight", [P, SLOTS, 4, SUB])
        row_token = sb("row_token", [P, SLOTS, SUB], U32)
        tile_at = sb("tile_at", [P, TILES], I32)
        tile_expert = sb("tile_expert", [P, TILES], I32)
        next_row_i = sb("next_row_i", [P, EXPERTS], I32)
        mask_t = sb("mask_t", [EXPERTS + 1, SLOTS, BANK])

        x1_dram = nc.dram_tensor("x1_scratch", [N, B, D], F32, kind="Internal").ap()
        x_rows = t["x"].rearrange("b n d -> n b d")
        out_rows = t["out"][0:TOKENS, :].rearrange("(b n) d -> n b d", n=N)
        routed_dram = nc.dram_tensor("routed_rows", [EXPERTS * REGION + TILE, ROW], F32, kind="Internal").ap()

        block = ctx.enter_context(nc.Block())

        @block.sync
        def _(sp):
            sp.dma_start(adj[:], t["adj"]).then_inc(sem("adj_loaded"), 16)
            for name in ("L0_gnn_w1_loop", "L0_gnn_w1_neigh", "L0_gnn_w2_loop", "L0_gnn_w2_neigh"):
                sp.dma_start(W[name][:], t[name]).then_inc(sem("l0_loaded"), 16)
            for k, name in enumerate(("L0_gnn_b1", "L0_gnn_b2")):
                sp.dma_start(col_b[:, k:k + 1], t[name].unsqueeze(1)).then_inc(sem("l0_loaded"), 16)
            with sp.Fori(0, J) as j:
                batch = early(sp, *((j * LANES + s) * G for s in range(LANES)))
                stored, normed = early(sp, 16 * j + 1, at("a2_normed", 0, j + 1)[1])
                for s in range(LANES):
                    sp.wait_ge(sem("x1_stored", s), stored)
                    sp.dma_start(squares(lane(s, 0)), x_rows[:, bass.ds(batch[s], G), :]).then_inc(sem("x_in", s), 16)
                for s in range(LANES):
                    sp.wait_ge(rises("a2_normed", s), normed)
                    sp.dma_start(x1_dram[:, bass.ds(batch[s], G), :], squares(lane(s, 0))).then_inc(sem("x1_stored", s), 16)
            for s in range(LANES):
                sp.wait_ge(sem("x1_stored", s), 16 * J + 1)

            def load_x1(s, b):
                sp.dma_start(squares(lane(s, 0)), x1_dram[:, b, :]).then_inc(sem("c_x1_in", s), 16)

            def store_y(s, b, count):
                sp.wait_ge(rises("d_y", s), count)
                sp.dma_start(out_rows[:, b, :], squares(lane(s, 11))).then_inc(sem("out_stored", s), 16)

            for s in range(LANES):
                load_x1(s, bass.ds(s * G, G))
            with sp.Fori(0, J - 1) as j:
                batch = early(sp, *((j * LANES + s) * G for s in range(LANES)))
                following = early(sp, *((j * LANES + LANES + s) * G for s in range(LANES)))
                added, done = early(sp, at("c_x3", 0, j + 1)[1], at("d_y", 0, j + 1)[1])
                for pair in range(SLOTS):
                    for s in lanes_of(pair):
                        sp.wait_ge(rises("c_x3", s), added)
                        load_x1(s, bass.ds(following[s], G))
                    for s in lanes_of(pair):
                        store_y(s, bass.ds(batch[s], G), done)
            for s in range(LANES):
                store_y(s, bass.ds(((J - 1) * LANES + s) * G, G), at("d_y", s, J)[1])
            sp.dma_start(t["out"][TOKENS:, :].rearrange("(a p) d -> p a d", p=P), padding[:, :, 0:P]).then_inc(sem("padded"), 16)
            for s in range(SLOTS):
                sp.wait_ge(sem("scattered", s), 16 * PAIR * TOP * J)
            sp.wait_ge(sem("tables"), 1)
            for e in range(EXPERTS + 1):
                at_row = EXPERTS * REGION if e == EXPERTS else sp.value_load(
                    next_row_i[0:1, e:e + 1], min_val=e * REGION, max_val=e * REGION + TOKENS)
                sp.dma_start(routed_dram[bass.ds(at_row, TILE), :].rearrange("(a p) d -> p a d", p=P),
                             padding[:]).then_inc(sem("padded"), 16)
            sp.wait_ge(sem("padded"), 16 * (EXPERTS + 2))
            for s in range(LANES):
                sp.wait_ge(sem("out_stored", s), 16 * J + 1)
            with sp.Fori(0, TILES // SLOTS) as j:
                (read,) = early(sp, at("m_ids", 0, j)[1])
                for s in range(SLOTS):
                    at_row = sp.value_load(tile_at[0:1, bass.ds(j * SLOTS + s, 1)], min_val=0, max_val=EXPERTS * REGION)
                    sp.wait_ge(rises("m_ids", s), read)
                    sp.dma_start(routed[:, s, :, :], routed_dram[bass.ds(at_row, TILE), :].rearrange(
                        "(a p) d -> p a d", p=P)).then_inc(sem("m_rows_in", s), 16)

        @block.gpsimd
        def _(pool):
            nc.gpsimd.memset(ident[:], 0.0).then_inc(sem("p_zero"), 1)
            nc.gpsimd.memset(ones[:], 1.0)
            nc.gpsimd.memset(half_neg[:], -0.5)
            nc.gpsimd.memset(eps_tile[:], EPS)
            nc.gpsimd.memset(mask_t[:], 1.0)
            nc.gpsimd.memset(states[:, 0, :], 0.0)
            nc.gpsimd.memset(cell[:], 0.0)
            nc.gpsimd.memset(v_ones[:], 1.0)
            nc.gpsimd.iota(expert_no[:], pattern=[[0, PAIR], [1, EXPERTS]], base=0, channel_multiplier=0,
                           allow_small_or_imprecise_dtypes=True)
            spots = iter(range(64))
            for name, count in AHEAD.items():
                for s in range(count):
                    spot = next(spots)
                    nc.gpsimd.memset(starts[:, spot:spot + 1], 0.0).then_inc(sem(name, s), 1)
            nc.gpsimd.memset(padding[:], 0.0).then_inc(sem("p_zero"), 1)
            nc.gpsimd.iota(token_no[:], pattern=[[P, B]], base=0, channel_multiplier=1)
            nc.gpsimd.iota(region_at[:], pattern=[[REGION, EXPERTS]], base=0, channel_multiplier=0,
                           allow_small_or_imprecise_dtypes=True)
            nc.gpsimd.iota(next_row[:], pattern=[[REGION, EXPERTS]], base=0, channel_multiplier=0,
                           allow_small_or_imprecise_dtypes=True).then_inc(sem("d_counted"), 1)
            pool.wait_ge(sem("p_zero"), 2)
            nc.gpsimd.affine_select(out=head_col[:], in_=ones[:, 0:HEADS], compare_op=ALU.is_gt, fill=0.0, base=1,
                                    pattern=[[-HD, HEADS]], channel_multiplier=1)
            nc.gpsimd.iota(padding[:, :, ROW - 1].bitcast(I32), pattern=[[P, SUB]], base=TOKENS, channel_multiplier=1)
            nc.gpsimd.affine_select(out=before[:], in_=ones[:], compare_op=ALU.is_gt, fill=0.0, base=0,
                                    pattern=[[1, P]], channel_multiplier=-1)
            nc.gpsimd.affine_select(out=ident[:], in_=ident[:], compare_op=ALU.not_equal, fill=1.0, base=0,
                                    pattern=[[-1, P]], channel_multiplier=1).then_inc(sem("ident"), 1)
            pool.wait_ge(sem("ident"), 1)
            nc.gpsimd.affine_select(out=head_col[:], in_=head_col[:], compare_op=ALU.is_gt, fill=0.0, base=HD,
                                    pattern=[[HD, HEADS]], channel_multiplier=-1)
            nc.gpsimd.tensor_copy(ident_h[:], ident[:]).then_inc(sem("consts"), 1)

            def inverse_deviation(tag, s, n):
                pool.wait_ge(*at(tag + "_moments", s, n))
                nc.gpsimd.tensor_tensor(rstd[:, s, :], moments[:, s, :, 1], eps_tile[:], ALU.add).then_inc(rises(tag + "_var", s), 1)
                pool.wait_ge(*at(tag + "_var", s, n))
                nc.gpsimd.tensor_tensor(rstd[:, s, :], rstd[:, s, :], half_neg[:], ALU.pow).then_inc(rises(tag + "_rstd", s), 1)

            def vector_sum(tag, s, n, ready, out, a, b):
                pool.wait_ge(*ready)
                nc.gpsimd.tensor_tensor(squares(out), squares(a), b, ALU.add).then_inc(rises(tag, s), 1)

            def carry_wait_pool(k):
                return nc.gpsimd.tensor_tensor(starts[:, k:k + 1], ones[:, 0:1], ones[:, 0:1], ALU.mult)

            with pool.Fori(0, J) as j:
                for tag in ("a1", "a2"):
                    for s in range(LANES):
                        inverse_deviation(tag, s, j + 1)
            for name in ("L1_gnn_Wc", "L1_gnn_Wq", "L1_gnn_Wk", "L1_gnn_Wv", "L1_gnn_Wo", "L1_gnn_W1", "L1_ffn_Wr"):
                pool.dma_start(W[name][:], t[name]).then_inc(sem("l1_loaded"), 16)
            pool.dma_start(w2_gnn[:], t["L1_gnn_W2"].rearrange("(c p) d -> p c d", p=P)).then_inc(sem("l1_loaded"), 16)
            pool.dma_start(up_w[:, 0, :], t["L1_ffn_W1s"]).then_inc(sem("l1_loaded"), 16)
            pool.dma_start(up_w[:, 1:, :], t["L1_ffn_W1p"].rearrange("e p f -> p e f")).then_inc(sem("l1_loaded"), 16)
            pool.dma_start(down_w[:, 0, :, :], t["L1_ffn_W2s"].rearrange("(c p) d -> p c d", p=P)).then_inc(sem("l1_loaded"), 16)
            for e in range(EXPERTS):
                pool.dma_start(down_w[:, 1 + e, :, :], t["L1_ffn_W2p"][e].rearrange("(c p) d -> p c d", p=P)).then_inc(sem("l1_loaded"), 16)
            with nc.allow_non_contiguous_dma(reason="small bias columns"):
                pool.dma_start(up_b[:, 0, :], t["L1_ffn_b1s"].rearrange("(c p) -> p c", p=P)).then_inc(sem("l1_loaded"), 16)
                pool.dma_start(up_b[:, 1:, :], t["L1_ffn_b1p"].rearrange("e (c p) -> p e c", p=P)).then_inc(sem("l1_loaded"), 16)
                for k in range(2):
                    pool.dma_start(col_b[:, 5 + k:6 + k], t["L1_gnn_b1"][k * P:(k + 1) * P].unsqueeze(1)).then_inc(sem("l1_loaded"), 16)
            pool.dma_start(down_b[0:EXPERTS, :], t["L1_ffn_b2p"]).then_inc(sem("l1_loaded"), 16)
            pool.dma_start(down_b[EXPERTS:EXPERTS + 1, :], t["L1_ffn_b2s"].unsqueeze(0)).then_inc(sem("l1_loaded"), 16)
            for k, name in enumerate(ROWS):
                pool.dma_start(row_b[:, k, :], t[name].partition_broadcast(P)).then_inc(sem("l1_loaded"), 16)
            pool.wait_ge(sem("l1_loaded"), L1_LOADS)
            pool.wait_ge(sem("recurrence_done"), 1)

            def hidden_columns(s, b0):
                nc.gpsimd.tensor_copy(squares(lane(s, 6)),
                                      states[:, 1:, bass.ds(b0, G)].rearrange("p n b -> p b n")).then_inc(sem("c_hs", s), 1)

            def both_halves(first, n1, second, n2, more):
                pairs_of = lambda p: () if p is None else lanes_of(p)
                one, two = pairs_of(first), pairs_of(second)
                for s in one:
                    inverse_deviation("c1", s, n1)
                for s in two:
                    vector_sum("c_x_be3", s, n2, at("c1_normed", s, n2), lane(s, 0), lane(s, 0), row("be3"))
                for s in two:
                    inverse_deviation("c3", s, n2)
                for s in one:
                    inverse_deviation("c2", s, n1)
                for s in two:
                    vector_sum("c_x2_b2", s, n2, at("c_x2n", s, n2), lane(s, 3), lane(s, 5), row("b2"))
                if more:
                    for s in two:
                        pool.wait_ge(*at("c_hs_psum", s, n2))
                        hidden_columns(s, (n2 * LANES + s) * G)
                for s in one:
                    vector_sum("c_x1_bo", s, n1, at("c_block_x1", s, n1), lane(s, 3), lane(s, 4), row("bo"))
                for tag in ("c4", "c5"):
                    for s in two:
                        inverse_deviation(tag, s, n2)
                if second is not None:
                    pool.wait_ge(*at("d_slots", second, n2))
                    carry_wait_pool(56 + second)
                    for b in range(PAIR):
                        for k in range(TOP):
                            pool.indirect_dma_start(
                                routed_dram, bass.IndirectOffsetOnAxis(ap=row_idx[:, second, b, k:k + 1], axis=0),
                                routed[:, second, b, :], None).then_inc(sem("scattered", second), 16)
                    pool.wait_ge(sem("scattered", second), 16 * PAIR * TOP * n2)
                    carry_wait_pool(58 + second).then_inc(sem("rows_free", second), 1)

            for s in range(LANES):
                hidden_columns(s, s * G)
            both_halves(0, 1, None, None, True)
            with pool.Fori(0, J - 1) as j:
                both_halves(1, j + 1, 0, j + 1, True)
                both_halves(0, j + 2, 1, j + 1, True)
            both_halves(1, J, 0, J, False)
            both_halves(None, None, 1, J, False)
            for s in range(LANES):
                pool.wait_ge(*at("d_y", s, J))
                pool.wait_ge(sem("out_stored", s), 16 * J + 1)
            nc.gpsimd.iota(tile(0, 3)[:, 0:EXPERTS * (TOKENS // TILE)], pattern=[[0, EXPERTS], [TILE, TOKENS // TILE]],
                           base=0, channel_multiplier=0, allow_small_or_imprecise_dtypes=True)
            nc.gpsimd.iota(tile(0, 9)[:, 0:TILES], pattern=[[1, TILES]], base=0, channel_multiplier=0,
                           allow_small_or_imprecise_dtypes=True).then_inc(sem("table_consts"), 1)
            pool.wait_ge(sem("padded"), 16 * (EXPERTS + 2))
            with pool.Fori(0, TILES // SLOTS) as j:
                for s in range(SLOTS):
                    pool.wait_ge(sem("m_y", s), j + 2)
                    carry_wait_pool(60 + s)
                    for a in range(SUB):
                        pool.indirect_dma_start(
                            t["out"], bass.IndirectOffsetOnAxis(ap=row_token[:, s, a:a + 1], axis=0),
                            squares(tile(s, 11))[:, a, :], None, compute_op=ALU.add).then_inc(sem("m_added", s), 16)
                    pool.wait_ge(sem("m_added", s), 16 * SUB * (j + 1))
                    carry_wait_pool(62 + s).then_inc(sem("m_free", s), 1)

        @block.vector
        def _(dve):
            V = nc.vector

            def carry_wait():
                V.tensor_copy(waiting[:], ones[:, 0:1])

            def measure(tag, s, n, src):
                for b in range(G):
                    last = V.bn_stats(stats[:, s, b, :], src[:, b, :])
                last.then_inc(rises(tag + "_stats", s), 1)
                dve.wait_ge(*at(tag + "_stats", s, n))
                carry_wait()
                for b in range(G):
                    last = V.bn_aggr(moments[:, s, b, :], stats[:, s, b, :])
                last.then_inc(rises(tag + "_moments", s), 1)

            def normalize(tag, s, n, src, dst):
                dve.wait_ge(*at(tag + "_rstd", s, n))
                for b in range(G):
                    last = V.tensor_scalar(dst[:, b, :], src[:, b, :], moments[:, s, b, 0:1], rstd[:, s, b:b + 1],
                                           ALU.subtract, ALU.mult)
                last.then_inc(rises(tag + "_normed", s), 1)

            def gain(tag, s, n, src, vector):
                dve.wait_ge(*at(tag + "_moments", s, n))
                for b in range(G):
                    last = V.scalar_tensor_tensor(src[:, b, :], src[:, b, :], moments[:, s, b, 0:1], row(vector)[:, 0, :],
                                                  ALU.subtract, ALU.mult)
                last.then_inc(rises(tag + "_gained", s), 1)

            def shift(tag, s, n, src, dst, added, done):
                dve.wait_ge(*at(tag + "_gained", s, n))
                dve.wait_ge(*at(tag + "_rstd", s, n))
                for b in range(G):
                    last = V.scalar_tensor_tensor(dst[:, b, :], src[:, b, :], rstd[:, s, b:b + 1], added[:, b, :],
                                                  ALU.mult, ALU.add)
                last.then_inc(rises(done, s), 1)

            dve.wait_ge(sem("adj_t_psum"), 1)
            V.tensor_copy(adj_t[:], bank(0, 0)[:, 0:P]).then_inc(sem("adj_t"), 1)
            dve.wait_ge(sem("l0_loaded"), 16 * 6)
            V.tensor_scalar(col_b[:, 2:3], col_b[:, 1:2], 0.5, None, ALU.mult).then_inc(sem("b2_half"), 1)

            with dve.Fori(0, J) as j:
                n = j + 1
                for s in range(LANES):
                    dve.wait_ge(sem("x_in", s), 16 * n)
                    measure("a1", s, n, squares(lane(s, 0)))
                for s in range(LANES):
                    normalize("a1", s, n, squares(lane(s, 0)), squares(lane(s, 1)))
                for s in range(LANES):
                    dve.wait_ge(*at("a_z1_psum", s, n))
                    V.tensor_copy(lane(s, 3), lane_bank(s, 1)).then_inc(rises("a_z1", s), 1)
                for s in range(LANES):
                    dve.wait_ge(*at("a_h1_psum", s, n))
                    V.tensor_copy(lane(s, 5), lane_bank(s, 0)).then_inc(rises("a_h1", s), 1)
                for s in range(LANES):
                    dve.wait_ge(*at("a1_normed", s, n))
                    V.scalar_tensor_tensor(lane(s, 0), lane(s, 1), 0.5, lane(s, 0), ALU.mult, ALU.add).then_inc(rises("a_x_half", s), 1)
                for s in range(LANES):
                    dve.wait_ge(*at("a_h2_psum", s, n))
                    dve.wait_ge(*at("a_x_half", s, n))
                    V.tensor_tensor(lane(s, 0), lane(s, 0), lane_bank(s, 1), ALU.add).then_inc(rises("a_x1", s), 1)
                    dve.wait_ge(*at("a_x1", s, n))
                    measure("a2", s, n, squares(lane(s, 0)))
                for s in range(LANES):
                    normalize("a2", s, n, squares(lane(s, 0)), squares(lane(s, 8)))

            dve.wait_ge(sem("gates_loaded"), 16 * 9)
            for k in (0, 2):
                V.tensor_scalar(gate_u[:, k, :], gate_u[:, k, :], 0.5, None, ALU.mult)
                V.tensor_scalar(gate_v[:, k, :], gate_v[:, k, :], 0.25, None, ALU.mult)
                V.tensor_scalar(gate_b[:, k:k + 1], gate_b[:, k:k + 1], 0.5, None, ALU.mult)
            V.tensor_scalar(gate_v[:, 1, :], gate_v[:, 1, :], 0.5, None, ALU.mult).then_inc(sem("gates_scaled"), 1)

            V.tensor_tensor(tmp[:], adj[:], adj_t[:], ALU.add).then_inc(sem("one_shot"), 1)
            dve.wait_ge(sem("one_shot"), 1)
            V.tensor_scalar(sym[:], tmp[:], 0.5, None, ALU.mult).then_inc(sem("one_shot"), 1)
            dve.wait_ge(sem("one_shot"), 2)
            V.tensor_reduce(sc[:, 0:1], sym[:], AX.X, ALU.add, apply_absolute_value=True).then_inc(sem("one_shot"), 1)
            dve.wait_ge(sem("one_shot"), 3)
            V.tensor_scalar(tmp2[:], ones[:], sc[:, 0:1], None, ALU.mult).then_inc(sem("e_spread"), 1)
            dve.wait_ge(sem("e_bound_psum"), 1)
            V.tensor_reduce(sc[:, 1:2], bank(0, 0)[:, 0:P], AX.X, ALU.max).then_inc(sem("one_shot"), 1)
            dve.wait_ge(sem("one_shot"), 4)
            V.scalar_tensor_tensor(power[:], ident[:], sc[:, 1:2], sym[:], ALU.mult, ALU.add).then_inc(sem("e_power"), 1)

            def trace_of(ap, count):
                V.tensor_tensor_reduce(tmp[:], ap, ident[:], 1.0, 0.0, ALU.mult, ALU.add, sc[:, 2:3]).then_inc(sem("e_diag"), 1)

            dve.wait_ge(sem("e_power"), 1)
            trace_of(power[:], 1)
            dve.wait_ge(sem("e_trace_psum"), 1)
            V.reciprocal(sc[:, 3:4], bank(0, 1)[:, 0:1]).then_inc(sem("e_inv"), 1)
            dve.wait_ge(sem("e_inv"), 1)
            V.tensor_scalar(power[:], power[:], sc[:, 3:4], None, ALU.mult).then_inc(sem("e_power"), 1)
            with dve.Fori(0, SQUARINGS) as q:
                dve.wait_ge(sem("e_square_psum"), q + 1)
                dve.wait_ge(sem("e_power"), q + 2)
                V.tensor_copy(tmp2[:], bank(0, 0)[:, 0:P]).then_inc(sem("e_copied"), 1)
                dve.wait_ge(sem("e_copied"), q + 1)
                trace_of(tmp2[:], q + 2)
                dve.wait_ge(sem("e_trace_psum"), q + 2)
                V.reciprocal(sc[:, 3:4], bank(0, 1)[:, 0:1]).then_inc(sem("e_inv"), 1)
                dve.wait_ge(sem("e_inv"), q + 2)
                V.tensor_scalar(power[:], tmp2[:], sc[:, 3:4], None, ALU.mult).then_inc(sem("e_power"), 1)
            dve.wait_ge(sem("e_power"), SQUARINGS + 2)
            trace_of(power[:], SQUARINGS + 2)
            dve.wait_ge(sem("e_diag"), SQUARINGS + 2)
            V.tensor_tensor_reduce(tmp[:], power[:], sym[:], 1.0, 0.0, ALU.mult, ALU.add, sc[:, 4:5]).then_inc(sem("e_rayleigh"), 1)
            dve.wait_ge(sem("e_trace_psum"), SQUARINGS + 2)
            V.tensor_copy(sc[:, 5:7], bank(0, 1)[:, 0:2]).then_inc(sem("one_shot"), 1)
            dve.wait_ge(sem("one_shot"), 5)
            V.reciprocal(sc[:, 7:8], sc[:, 5:6]).then_inc(sem("e_inv"), 1)
            dve.wait_ge(sem("e_inv"), SQUARINGS + 2)
            V.tensor_scalar(sc[:, 8:9], sc[:, 6:7], sc[:, 7:8], 1e-8, ALU.mult, ALU.add).then_inc(sem("one_shot"), 1)
            dve.wait_ge(sem("one_shot"), 6)
            V.reciprocal(sc[:, 9:10], sc[:, 8:9]).then_inc(sem("e_inv"), 1)
            dve.wait_ge(sem("e_inv"), SQUARINGS + 3)
            V.tensor_scalar(tmp2[:], adj_t[:], sc[:, 9:10], 2.0, ALU.mult, ALU.mult).then_inc(sem("one_shot"), 1)
            dve.wait_ge(sem("one_shot"), 7)
            V.tensor_tensor(lap_t[:], tmp2[:], ident[:], ALU.subtract).then_inc(sem("lap_t"), 1)
            V.tensor_scalar(tmp[:], adj[:], 0.0, None, ALU.is_gt).then_inc(sem("one_shot"), 1)
            dve.wait_ge(sem("one_shot"), 8)
            V.tensor_reduce(sc[:, 10:11], tmp[:], AX.X, ALU.max).then_inc(sem("one_shot"), 1)
            dve.wait_ge(sem("one_shot"), 9)
            V.tensor_scalar(tmp[:], tmp[:], sc[:, 10:11], 1e9, ALU.subtract, ALU.mult).then_inc(sem("one_shot"), 1)
            V.tensor_scalar(power[:], ident[:], sc[:, 10:11], None, ALU.mult).then_inc(sem("m_diag"), 1)
            dve.wait_ge(sem("one_shot"), 10)
            V.tensor_copy(mask_add[:], tmp[:].unsqueeze(1).to_broadcast([P, HEADS, P])).then_inc(sem("mask"), 1)
            dve.wait_ge(sem("m_any_psum"), 1)
            V.tensor_scalar(row_any[:], bank(0, 0)[:, 0:P], HD ** -0.5, None, ALU.mult).then_inc(sem("row_any"), 1)
            dve.wait_ge(sem("row_any"), 1)

            def recur(pair, n, k):
                now = pair * 2 + k
                V.scalar_tensor_tensor(state_cell[:], states[:, now, :], 0.5, cell[:], ALU.mult, ALU.mult).then_inc(rises("r_hc", k), 1)
                dve.wait_ge(*at("r_gates", k, n))
                V.scalar_tensor_tensor(in_cand[:], gates[:, k, 0, :], 1.0, gates[:, k, 1, :], ALU.add, ALU.mult).then_inc(rises("r_ic", k), 1)
                dve.wait_ge(*at("r_ic", k, n))
                dve.wait_ge(*at("r_hc", k, n))
                V.tensor_tensor(cell[:], state_cell[:], in_cand[:], ALU.add).then_inc(rises("r_cell", k), 1)
                dve.wait_ge(*at("r_cell", k, n))
                dve.wait_ge(*at("r_tanh", k, n))
                V.scalar_tensor_tensor(states[:, now + 1, :], gates[:, k, 2, :], 1.0, cell_tanh[:], ALU.add, ALU.mult).then_inc(rises("r_state", k), 1)
                dve.wait_ge(*at("r_state", k, n))

            with dve.Fori(0, N // 2) as pair:
                for k in range(2):
                    recur(pair, pair + 1, k)
            dve.wait_ge(*at("r_state", 1, N // 2))
            V.tensor_copy(sc[:, 12:13], ones[:, 0:1]).then_inc(sem("recurrence_done"), 1)
            dve.wait_ge(sem("l1_loaded"), L1_LOADS)

            def both_halves(first, n1, second, n2):
                pairs_of = lambda p: () if p is None else lanes_of(p)
                one, two = pairs_of(first), pairs_of(second)
                for s in one:
                    dve.wait_ge(sem("c_x1_in", s), 16 * n1)
                    dve.wait_ge(*at("c_hs_psum", s, n1))
                    V.scalar_tensor_tensor(lane(s, 0), lane_bank(s, 0), 0.5, lane(s, 0), ALU.mult, ALU.add).then_inc(rises("c_x2", s), 1)
                    dve.wait_ge(*at("c_x2", s, n1))
                    measure("c1", s, n1, squares(lane(s, 0)))
                for s in two:
                    dve.wait_ge(*at("c_wo_psum", s, n2))
                    dve.wait_ge(*at("c_x1_bo", s, n2))
                    V.tensor_tensor(lane(s, 5), lane_bank(s, 1), lane(s, 3), ALU.add).then_inc(rises("c_res2", s), 1)
                    dve.wait_ge(*at("c_res2", s, n2))
                    measure("c3", s, n2, squares(lane(s, 5)))
                for s in one:
                    normalize("c1", s, n1, squares(lane(s, 0)), squares(lane(s, 1)))
                for s in two:
                    gain("c3", s, n2, squares(lane(s, 5)), "g2")
                for s in two:
                    shift("c3", s, n2, squares(lane(s, 5)), squares(lane(s, 5)), row("be2"), "c_x2n")
                for s in one:
                    dve.wait_ge(*at("c_h_psum", s, n1))
                    V.tensor_tensor(squares(lane(s, 3)), squares(lane_bank(s, 0)), row("bc"), ALU.add).then_inc(rises("c_h", s), 1)
                    dve.wait_ge(*at("c_h", s, n1))
                    measure("c2", s, n1, squares(lane(s, 3)))
                for s in one:
                    gain("c2", s, n1, squares(lane(s, 3)), "g1")
                for s in one:
                    shift("c2", s, n1, squares(lane(s, 3)), squares(lane(s, 3)), row("be1"), "c2_shifted")
                    dve.wait_ge(*at("c2_shifted", s, n1))
                    V.scalar_tensor_tensor(lane(s, 4), lane(s, 3), 0.0, lane(s, 1), ALU.max, ALU.add).then_inc(rises("c_block_x1", s), 1)
                for s in two:
                    dve.wait_ge(*at("c_ff_psum", s, n2))
                    dve.wait_ge(*at("c_x2_b2", s, n2))
                    V.tensor_tensor(lane(s, 1), lane_bank(s, 1), lane(s, 3), ALU.add).then_inc(rises("c_res3", s), 1)
                    dve.wait_ge(*at("c_res3", s, n2))
                    measure("c4", s, n2, squares(lane(s, 1)))
                for s in one:
                    dve.wait_ge(*at("c_q_psum", s, n1))
                    dve.wait_ge(*at("c_x1_bo", s, n1))
                    V.tensor_tensor(squares(lane(s, 4)), squares(lane_bank(s, 0)),
                                    row_any[:].unsqueeze(1).to_broadcast([P, G, P]), ALU.mult).then_inc(rises("c_q", s), 1)
                for s in two:
                    gain("c4", s, n2, squares(lane(s, 1)), "g3")
                for s in two:
                    dve.wait_ge(*at("c_x_be3", s, n2))
                    dve.wait_ge(sem("out_stored", s), 16 * n2 - 15)
                    shift("c4", s, n2, squares(lane(s, 1)), squares(lane(s, 11)), squares(lane(s, 0)), "c_x3")
                    dve.wait_ge(*at("c_x3", s, n2))
                    measure("c5", s, n2, squares(lane(s, 11)))
                for s in one:
                    dve.wait_ge(*at("c_s_psum", s, n1))
                    V.tensor_reduce(top[:, s, 0, :], lane_banks(s).rearrange("p b (h m) -> p (b h) m", h=HEADS), AX.X, ALU.max).then_inc(rises("c_max", s), 1)
                    dve.wait_ge(*at("c_max", s, n1))
                    V.tensor_scalar(top[:, s, 1, :], top[:, s, 0, :], -1.0, None, ALU.mult).then_inc(rises("c_negmax", s), 1)
                for s in two:
                    dve.wait_ge(sem("rows_free", second), n2)
                    normalize("c5", s, n2, squares(lane(s, 11)), routed[:, second, tokens_of(s), 0:P])
                if second is not None:
                    route(second, n2)
                for s in one:
                    dve.wait_ge(*at("c_o_psum", s, n1))
                    V.reciprocal(inv_sum[:, s], attended(s)[:, :, :, HD]).then_inc(rises("c_inv", s), 1)
                    dve.wait_ge(*at("c_inv", s, n1))
                    V.tensor_tensor(squares(lane(s, 1)).rearrange("p b (h d) -> p b h d", h=HEADS),
                                    attended(s)[:, :, :, 0:HD], inv_sum[:, s].unsqueeze(3).to_broadcast([P, G, HEADS, HD]),
                                    ALU.mult).then_inc(rises("c_o", s), 1)
                for s in two:
                    dve.wait_ge(*at("d_down_psum", s, n2))
                    V.tensor_tensor(lane(s, 11), lane(s, 11), lane_bank(s, 3), ALU.add).then_inc(rises("d_y", s), 1)

            def route(s, n):
                R = [router[:, s, k] for k in range(12)]
                wide = [P, PAIR, EXPERTS]
                logits = bank(s, 1)[:, 0:PAIR * EXPERTS].rearrange("p (b e) -> p b e", b=PAIR)
                dve.wait_ge(*at("d_logits_psum", s, n))
                V.tensor_reduce(R[0][:, :, 0], logits, AX.X, ALU.max).then_inc(rises("d_max", s), 1)
                dve.wait_ge(*at("d_max", s, n))
                V.tensor_tensor(R[1], logits, R[0][:, :, 0:1].to_broadcast(wide), ALU.subtract).then_inc(rises("d_sub", s), 1)
                dve.wait_ge(*at("d_exp", s, n))
                carry_wait()
                for b in range(PAIR):
                    last = V.max(R[3][:, b, :], R[2][:, b, :])
                last.then_inc(rises("d_top", s), 1)
                dve.wait_ge(*at("d_top", s, n))
                carry_wait()
                for b in range(PAIR):
                    last = V.max_index(best_idx[:, s, b, :], R[3][:, b, :], R[2][:, b, :])
                last.then_inc(rises("d_idx", s), 1)
                V.tensor_tensor(R[0][:, :, 0], R[3][:, :, 0], R[3][:, :, 1], ALU.add).then_inc(rises("d_den", s), 1)
                dve.wait_ge(*at("d_den", s, n))
                V.reciprocal(R[0][:, :, 1], R[0][:, :, 0]).then_inc(rises("d_inv", s), 1)
                dve.wait_ge(*at("d_inv", s, n))
                V.tensor_tensor(routed[:, s, :, P:P + TOP], R[3][:, :, 0:2], R[0][:, :, 1:2].to_broadcast([P, PAIR, 2]), ALU.mult).then_inc(rises("d_w", s), 1)
                dve.wait_ge(*at("d_idx", s, n))
                V.tensor_copy(R[0][:, :, 4:6], best_idx[:, s, :, 0:2]).then_inc(rises("d_idxf", s), 1)
                dve.wait_ge(*at("d_w", s, n))
                dve.wait_ge(*at("d_idxf", s, n))
                for k in range(TOP):
                    V.tensor_tensor(R[4 + k], expert_no[:], R[0][:, :, 4 + k:5 + k].to_broadcast(wide),
                                    ALU.is_equal).then_inc(rises(f"d_eq{k}", s), 1)
                dve.wait_ge(*at("d_eq1", s, n))
                V.tensor_tensor(R[8], R[4], R[5], ALU.add).then_inc(rises("d_chosen", s), 1)
                for k in range(TOP):
                    V.tensor_tensor(R[10 + k], R[4 + k], routed[:, s, :, P + k:P + k + 1].to_broadcast(wide),
                                    ALU.mult).then_inc(rises(f"d_part{k}", s), 1)
                V.tensor_copy(routed[:, s, :, P + 2], best_idx[:, s, :, 0])
                V.tensor_copy(routed[:, s, :, P + 3].bitcast(I32), token_no[:, bass.ds((n * SLOTS + s - SLOTS) * PAIR, PAIR)])
                dve.wait_ge(*at("d_part1", s, n))
                V.tensor_tensor(R[6], R[10], R[11], ALU.add).then_inc(rises("d_mask", s), 1)
                dve.wait_ge(*at("d_places_psum", s, n))
                dve.wait_ge(sem("d_counted"), n * SLOTS + s + 1 - SLOTS)
                V.tensor_tensor(R[9], logits, next_row[:].unsqueeze(1).to_broadcast(wide), ALU.add).then_inc(rises("d_place", s), 1)
                dve.wait_ge(*at("d_place", s, n))
                V.tensor_tensor(next_row[:], next_row[:], bank(s, 1)[:, PAIR * EXPERTS:(PAIR + 1) * EXPERTS],
                                ALU.add).then_inc(sem("d_counted"), 1)
                for k in range(TOP):
                    V.tensor_tensor(R[10 + k], R[4 + k], R[9], ALU.mult).then_inc(rises(f"d_prod{k}", s), 1)
                for k in range(TOP):
                    dve.wait_ge(*at(f"d_prod{k}", s, n))
                    V.tensor_reduce(R[0][:, :, 6 + k], R[10 + k], AX.X, ALU.add).then_inc(rises(f"d_slot{k}", s), 1)
                dve.wait_ge(*at("d_slot1", s, n))
                V.tensor_copy(row_idx[:, s, :, :], R[0][:, :, 6:8]).then_inc(rises("d_slots", s), 1)

            both_halves(0, 1, None, None)
            with dve.Fori(0, J - 1) as j:
                both_halves(1, j + 1, 0, j + 1)
                both_halves(0, j + 2, 1, j + 1)
            both_halves(1, J, 0, J)
            both_halves(None, None, 1, J)

            dve.wait_ge(sem("d_counted"), J * SLOTS + 1)
            for s in range(LANES):
                dve.wait_ge(sem("out_stored", s), 16 * J + 1)
            wide = lambda s, k: tile(s, k, 2)[:, 0:TILES * EXPERTS].rearrange("p (i e) -> p i e", e=EXPERTS)
            steps, ge, part = tile(0, 3)[:, 0:EXPERTS * (TOKENS // TILE)], wide(0, 5), wide(0, 7)
            tile_no, cells = tile(0, 9)[:, 0:TILES], tile(0, 10)
            count, tiles_of, upto = (cells[:, 8 * k:8 * k + EXPERTS] for k in range(3))
            expert_f, first_f, within, live, at_f = (cells[:, 32 + TILES * k:32 + TILES * (k + 1)] for k in range(5))
            made = [0]

            def then(op):
                op.then_inc(sem("table_step"), 1)
                made[0] += 1
                dve.wait_ge(sem("table_step"), made[0])

            dve.wait_ge(sem("table_consts"), 1)
            then(V.tensor_tensor(count, next_row[:], region_at[:], ALU.subtract))
            then(V.tensor_tensor(steps.rearrange("p (e m) -> p e m", e=EXPERTS), count.unsqueeze(2).to_broadcast(
                [P, EXPERTS, TOKENS // TILE]), steps.rearrange("p (e m) -> p e m", e=EXPERTS), ALU.is_gt))
            then(V.tensor_reduce(tiles_of, steps.rearrange("p (e m) -> p e m", e=EXPERTS), AX.X, ALU.add))
            then(V.tensor_copy(upto, tiles_of))
            for e in range(1, EXPERTS):
                then(V.tensor_tensor(upto[:, e:e + 1], upto[:, e - 1:e], tiles_of[:, e:e + 1], ALU.add))
            then(V.tensor_tensor(ge, tile_no.unsqueeze(2).to_broadcast([P, TILES, EXPERTS]),
                                 upto.unsqueeze(1).to_broadcast([P, TILES, EXPERTS]), ALU.is_ge))
            then(V.tensor_reduce(expert_f, ge, AX.X, ALU.add))
            then(V.tensor_tensor(part, ge, tiles_of.unsqueeze(1).to_broadcast([P, TILES, EXPERTS]), ALU.mult))
            then(V.tensor_reduce(first_f, part, AX.X, ALU.add))
            then(V.tensor_tensor(within, tile_no, first_f, ALU.subtract))
            then(V.tensor_scalar(live, expert_f, EXPERTS - 0.5, float(TILE), ALU.is_lt, ALU.mult))
            then(V.tensor_tensor(within, within, live, ALU.mult))
            then(V.tensor_scalar(at_f, expert_f, float(REGION), None, ALU.mult))
            then(V.tensor_tensor(at_f, at_f, within, ALU.add))
            then(V.tensor_scalar(expert_f, expert_f, EXPERTS - 1.0, None, ALU.min))
            then(V.tensor_copy(tile_at[:], at_f))
            then(V.tensor_copy(tile_expert[:], expert_f))
            V.tensor_copy(next_row_i[:], next_row[:]).then_inc(sem("tables"), 1)
            dve.wait_ge(sem("tables"), 1)

            with dve.Fori(0, TILES // SLOTS) as j:
                n = j + 1
                for s in range(SLOTS):
                    e = dve.value_load(tile_expert[0:1, bass.ds(j * SLOTS + s, 1)], min_val=0, max_val=EXPERTS - 1)
                    dve.wait_ge(*at("m_down_psum", s, j))
                    V.tensor_copy(tile(s, 5), up_w[:, bass.ds(e + 1, 1), :].rearrange("p a f -> p (a f)"))
                    V.tensor_copy(tile(s, 7)[:, 0:FC], up_b[:, bass.ds(e + 1, 1), :].rearrange("p a f -> p (a f)"))
                    V.tensor_copy(tile(s, 6), down_w[:, bass.ds(e + 1, 1), :, :].rearrange("p a c d -> p (a c d)")).then_inc(sem("m_staged", s), 1)
                    first, diff, part_w, weight = (row_weight[:, s, k, :] for k in range(4))
                    dve.wait_ge(sem("m_rows_in", s), 16 * n)
                    V.tensor_scalar(first, routed[:, s, :, P + 2], expert_no[:, 0, bass.ds(e, 1)], None, ALU.is_equal).then_inc(rises("m_is_first", s), 1)
                    V.tensor_tensor(diff, routed[:, s, :, P], routed[:, s, :, P + 1], ALU.subtract).then_inc(rises("m_diff", s), 1)
                    dve.wait_ge(*at("m_diff", s, n))
                    V.tensor_tensor(part_w, first, diff, ALU.mult).then_inc(rises("m_part", s), 1)
                    dve.wait_ge(*at("m_part", s, n))
                    V.tensor_tensor(weight, part_w, routed[:, s, :, P + 1], ALU.add).then_inc(rises("m_weight", s), 1)
                for s in range(SLOTS):
                    dve.wait_ge(sem("m_free", s), n)
                    dve.wait_ge(*at("m_weight", s, n))
                    dve.wait_ge(*at("m_xt_psum", s, n))
                    V.tensor_copy(row_token[:, s, :], routed[:, s, :, ROW - 1].bitcast(U32)).then_inc(rises("m_ids", s), 1)
                for s in range(SLOTS):
                    dve.wait_ge(*at("m_down_psum", s, n))
                    V.tensor_tensor(squares(tile(s, 11)), squares(bank(s, 1)),
                                    row_weight[:, s, 3, :].unsqueeze(2).to_broadcast([P, SUB, P]), ALU.mult).then_inc(sem("m_y", s), 1)

        @block.scalar
        def _(act):
            A = nc.scalar
            for k, name in enumerate("ico"):
                act.dma_start(gate_u[:, k, :], t["L0_ffn_U_" + name]).then_inc(sem("gates_loaded"), 16)
                act.dma_start(gate_v[:, k, :], t["L0_ffn_V_" + name]).then_inc(sem("gates_loaded"), 16)
                act.dma_start(gate_b[:, k:k + 1], t["L0_ffn_b_" + name].unsqueeze(1)).then_inc(sem("gates_loaded"), 16)
            act.wait_ge(sem("l0_loaded"), 16 * 6)
            act.wait_ge(sem("b2_half"), 1)
            with act.Fori(0, J) as j:
                n = j + 1
                for s in range(LANES):
                    act.wait_ge(*at("a_xt_psum", s, n))
                    A.copy(lane(s, 2), lane_bank(s, 0)).then_inc(rises("a_xt", s), 1)
                for s in range(LANES):
                    act.wait_ge(*at("a_h1t_psum", s, n))
                    A.activation(lane(s, 4), lane_bank(s, 2), ACT.Relu, bias=col_b[:, 0:1]).then_inc(rises("a_h1t", s), 1)
                for s in range(LANES):
                    act.wait_ge(*at("a_z2_psum", s, n))
                    A.copy(lane(s, 6), lane_bank(s, 1)).then_inc(rises("a_z2", s), 1)
                for s in range(LANES):
                    act.wait_ge(*at("a_h2t_psum", s, n))
                    A.activation(lane(s, 7), lane_bank(s, 2), ACT.Relu, bias=col_b[:, 2:3], scale=0.5).then_inc(rises("a_h2t", s), 1)
                for s in range(LANES):
                    act.wait_ge(*at("a_x1t_psum", s, n))
                    b0 = (j * LANES + s) * G
                    A.copy(states[:, 1:, bass.ds(b0, G)].rearrange("p n b -> p b n"), squares(lane_bank(s, 2))).then_inc(rises("a_x1t", s), 1)

            act.wait_ge(sem("gates_scaled"), 1)
            with act.Fori(0, N // 2) as pair:
                for k in range(2):
                    n = pair + 1
                    act.wait_ge(*at("r_zic_psum", k, n))
                    A.activation(gates[:, k, 0, :], psum[:, 2 * k, 0:B], ACT.Tanh, bias=gate_b[:, 0:1])
                    A.activation(gates[:, k, 1, :], psum[:, 2 * k, B:2 * B], ACT.Tanh, bias=gate_b[:, 1:2]).then_inc(rises("r_gates", k), 1)
                    act.wait_ge(*at("r_zo_psum", k, n))
                    A.activation(gates[:, k, 2, :], psum[:, 2 * k + 1, 0:B], ACT.Tanh, bias=gate_b[:, 2:3]).then_inc(rises("r_out_gate", k), 1)
                    act.wait_ge(*at("r_cell", k, n))
                    A.activation(cell_tanh[:], cell[:], ACT.Tanh, scale=0.5).then_inc(rises("r_tanh", k), 1)

            act.wait_ge(sem("l1_loaded"), L1_LOADS)

            def both_halves(first, n1, second, n2):
                pairs_of = lambda p: () if p is None else lanes_of(p)
                one, two = pairs_of(first), pairs_of(second)
                for s in two:
                    act.wait_ge(*at("c_ot_psum", s, n2))
                    A.copy(lane(s, 2), lane_bank(s, 0)).then_inc(rises("c_ot", s), 1)
                for s in one:
                    act.wait_ge(*at("c_xp_psum", s, n1))
                    A.copy(lane(s, 2), lane_bank(s, 1)).then_inc(rises("c_xp", s), 1)
                for s in two:
                    act.wait_ge(*at("c_x2t_psum", s, n2))
                    A.copy(lane(s, 2), lane_bank(s, 0)).then_inc(rises("c_x2t", s), 1)
                for k in range(2):
                    for s in two:
                        act.wait_ge(*at(f"c_up{k}_psum", s, n2))
                        A.activation(lane(s, 7 + k), lane_bank(s, 1 + k), ACT.Gelu, bias=col_b[:, 5 + k:6 + k]).then_inc(rises(f"c_up{k}", s), 1)
                for s in one:
                    act.wait_ge(*at("c_x1t_psum", s, n1))
                    A.copy(lane(s, 2), lane_bank(s, 1)).then_inc(rises("c_x1t", s), 1)
                for s in one:
                    act.wait_ge(*at("c_kv_psum", s, n1))
                    for h in range(HEADS):
                        last = A.activation(lane(s, 7, 4)[:, h * GROUP:(h + 1) * GROUP], lane_bank(s, 1), ACT.Copy, scale=head_col[:, h:h + 1])
                    last.then_inc(rises("c_k", s), 1)
                    A.copy(v_ones[:, s, :, :, 0:HD].rearrange("p b h d -> p (b h) d"),
                           lane_bank(s, 3).rearrange("p (c d) -> p c d", d=HD)).then_inc(rises("c_v", s), 1)
                for s in one:
                    act.wait_ge(*at("c_negmax", s, n1))
                    for b in range(G):
                        for h in range(HEADS):
                            c = b * HEADS + h
                            last = A.activation(lane(s, 7, 4)[:, c * P:(c + 1) * P], lane_banks(s)[:, b, h * P:(h + 1) * P], ACT.Exp,
                                                bias=top[:, s, 1, c:c + 1])
                    last.then_inc(rises("c_exp", s), 1)
                for s in two:
                    act.wait_ge(*at("c_x4t_psum", s, n2))
                    A.copy(lane(s, 2), lane_bank(s, 0)).then_inc(rises("c_x4t", s), 1)
                if second is not None:
                    act.wait_ge(*at("d_sub", second, n2))
                    A.activation(router[:, second, 2], router[:, second, 1], ACT.Exp).then_inc(rises("d_exp", second), 1)
                for b in range(G):
                    for s in one:
                        act.wait_ge(*at(f"c_pt{b}_psum", s, n1))
                        A.copy(lane(s, 12 + 2 * b, 2), lane_banks(s)[:, b, :]).then_inc(rises(f"c_pt{b}", s), 1)
                if second is not None:
                    act.wait_ge(*at("d_maskt_psum", second, n2))
                    A.copy(mask_t[0:EXPERTS, second, :], bank(second, 0)[0:EXPERTS, :]).then_inc(rises("d_maskt", second), 1)
                for c in range(FC):
                    for s in two:
                        act.wait_ge(*at(f"d_up{c}_psum", s, n2))
                        A.activation(lane(s, 12 + c), lane_bank(s, (1 + c) % 2), ACT.Gelu, bias=up_b[:, 0, c:c + 1]).then_inc(rises(f"d_up{c}", s), 1)

            both_halves(0, 1, None, None)
            with act.Fori(0, J - 1) as j:
                both_halves(1, j + 1, 0, j + 1)
                both_halves(0, j + 2, 1, j + 1)
            both_halves(1, J, 0, J)
            both_halves(None, None, 1, J)

            with act.Fori(0, TILES // SLOTS) as j:
                n = j + 1
                for s in range(SLOTS):
                    act.wait_ge(*at("m_xt_psum", s, n))
                    A.copy(tile(s, 2), bank(s, 0)).then_inc(rises("m_xt", s), 1)
                for s in range(SLOTS):
                    for c in range(FC):
                        act.wait_ge(*at(f"m_up{c}_psum", s, n))
                        A.activation(tile(s, 12 + c), bank(s, (1 + c) % 4), ACT.Gelu, bias=tile(s, 7)[:, c:c + 1]).then_inc(rises(f"m_h{c}", s), 1)

        @block.tensor
        def _(pe):
            T = nc.tensor

            def transposes(out, src, done, rows=P):
                for b in range(src.shape[1]):
                    last = T.transpose(squares(out)[:rows, b, :], src[:, b, :], ident[:])
                last.then_inc(done, 1)

            def by_square(out, left, right, done):
                for b in range(G):
                    last = T.matmul(squares(out)[:, b, :], left[:, b, :], right, start=(b == 0), stop=True, skip_group_check=True)
                last.then_inc(done, 1)

            pe.wait_ge(sem("adj_loaded"), 16)
            pe.wait_ge(sem("consts"), 1)
            T.transpose(bank(0, 0)[:, 0:P], adj[:], ident[:]).then_inc(sem("adj_t_psum"), 1)
            pe.wait_ge(sem("adj_t"), 1)
            pe.wait_ge(sem("l0_loaded"), 16 * 6)
            with pe.Fori(0, J) as j:
                n = j + 1
                for s in range(LANES):
                    pe.wait_ge(*at("a1_normed", s, n))
                    pe.wait_ge(*at("a_x1t", s, j))
                    transposes(lane_bank(s, 0), squares(lane(s, 1)), rises("a_xt_psum", s))
                    by_square(lane_bank(s, 1), squares(lane(s, 1)), adj_t[:], rises("a_z1_psum", s))
                for s in range(LANES):
                    pe.wait_ge(*at("a_xt", s, n))
                    T.matmul(lane_bank(s, 2), W["L0_gnn_w1_loop"][:], lane(s, 2), start=True, stop=False)
                    pe.wait_ge(*at("a_z1", s, n))
                    T.matmul(lane_bank(s, 2), W["L0_gnn_w1_neigh"][:], lane(s, 3), start=False, stop=True).then_inc(rises("a_h1t_psum", s), 1)
                for s in range(LANES):
                    pe.wait_ge(*at("a_h1t", s, n))
                    transposes(lane_bank(s, 0), squares(lane(s, 4)), rises("a_h1_psum", s))
                for s in range(LANES):
                    pe.wait_ge(*at("a_h1", s, n))
                    by_square(lane_bank(s, 1), squares(lane(s, 5)), adj_t[:], rises("a_z2_psum", s))
                for s in range(LANES):
                    T.matmul(lane_bank(s, 2), W["L0_gnn_w2_loop"][:], lane(s, 4), start=True, stop=False)
                    pe.wait_ge(*at("a_z2", s, n))
                    T.matmul(lane_bank(s, 2), W["L0_gnn_w2_neigh"][:], lane(s, 6), start=False, stop=True).then_inc(rises("a_h2t_psum", s), 1)
                for s in range(LANES):
                    pe.wait_ge(*at("a_h2t", s, n))
                    transposes(lane_bank(s, 1), squares(lane(s, 7)), rises("a_h2_psum", s))
                for s in range(LANES):
                    pe.wait_ge(*at("a2_normed", s, n))
                    transposes(lane_bank(s, 2), squares(lane(s, 8)), rises("a_x1t_psum", s))

            for s in range(LANES):
                pe.wait_ge(*at("a_x1t", s, J))
            pe.wait_ge(sem("e_spread"), 1)
            T.transpose(bank(0, 0)[:, 0:P], tmp2[:], ident[:]).then_inc(sem("e_bound_psum"), 1)
            pe.wait_ge(sem("e_diag"), 1)
            T.matmul(bank(0, 1)[:, 0:1], ones[:], sc[:, 2:3], start=True, stop=True).then_inc(sem("e_trace_psum"), 1)
            with pe.Fori(0, SQUARINGS) as q:
                pe.wait_ge(sem("e_power"), q + 2)
                T.matmul(bank(0, 0)[:, 0:P], power[:], power[:], start=True, stop=True).then_inc(sem("e_square_psum"), 1)
                pe.wait_ge(sem("e_diag"), q + 2)
                T.matmul(bank(0, 1)[:, 0:1], ones[:], sc[:, 2:3], start=True, stop=True).then_inc(sem("e_trace_psum"), 1)
            pe.wait_ge(sem("e_rayleigh"), 1)
            T.matmul(bank(0, 1)[:, 0:1], ones[:], sc[:, 2:3], start=True, stop=True)
            T.matmul(bank(0, 1)[:, 1:2], ones[:], sc[:, 4:5], start=True, stop=True).then_inc(sem("e_trace_psum"), 1)
            pe.wait_ge(sem("m_diag"), 1)
            T.matmul(bank(0, 0)[:, 0:P], ones[:], power[:], start=True, stop=True).then_inc(sem("m_any_psum"), 1)
            pe.wait_ge(sem("row_any"), 1)

            pe.wait_ge(sem("gates_scaled"), 1)

            def gate_bank(k, g):
                return psum[:, 2 * k + (g == 2), (g % 2) * B:(g % 2 + 1) * B]

            def input_part(now, k):
                for g in range(3):
                    T.matmul(gate_bank(k, g), gate_u[:, g, :], states[:, now, :], start=(g != 1), stop=False, skip_group_check=True)

            def state_part(now, k):
                for g in range(3):
                    last = T.matmul(gate_bank(k, g), gate_v[:, g, :], states[:, now, :], start=False, stop=True, skip_group_check=True)
                    if g == 1:
                        last.then_inc(rises("r_zic_psum", k), 1)
                last.then_inc(rises("r_zo_psum", k), 1)

            input_part(1, 0)
            state_part(0, 0)
            input_part(2, 1)
            with pe.Fori(0, N // 2 - 1) as pair:
                pe.wait_ge(*at("r_state", 0, pair + 1))
                state_part(pair * 2 + 1, 1)
                input_part(pair * 2 + 3, 0)
                pe.wait_ge(*at("r_state", 1, pair + 1))
                state_part(pair * 2 + 2, 0)
                input_part(pair * 2 + 4, 1)
            pe.wait_ge(*at("r_state", 0, N // 2))
            state_part(N - 1, 1)

            pe.wait_ge(sem("l1_loaded"), L1_LOADS)
            pe.wait_ge(sem("lap_t"), 1)
            pe.wait_ge(sem("mask"), 1)
            pe.wait_ge(sem("recurrence_done"), 1)

            def both_halves(first, n1, second, n2):
                pairs_of = lambda p: () if p is None else lanes_of(p)
                one, two = pairs_of(first), pairs_of(second)
                for s in one:
                    pe.wait_ge(sem("c_hs", s), n1)
                    transposes(lane_bank(s, 0), squares(lane(s, 6)), rises("c_hs_psum", s))
                for s in two:
                    pe.wait_ge(*at("c_o", s, n2))
                    transposes(lane_bank(s, 0), squares(lane(s, 1)), rises("c_ot_psum", s))
                for s in two:
                    pe.wait_ge(*at("c_ot", s, n2))
                    by_square(lane_bank(s, 1), squares(lane(s, 2)), W["L1_gnn_Wo"][:], rises("c_wo_psum", s))
                for s in one:
                    pe.wait_ge(*at("c1_normed", s, n1))
                    by_square(lane_bank(s, 1), squares(lane(s, 1)), lap_t[:], rises("c_xp_psum", s))
                for s in one:
                    pe.wait_ge(*at("c_xp", s, n1))
                    by_square(lane_bank(s, 0), squares(lane(s, 2)), W["L1_gnn_Wc"][:], rises("c_h_psum", s))
                for s in two:
                    pe.wait_ge(*at("c_x2n", s, n2))
                    transposes(lane_bank(s, 0), squares(lane(s, 5)), rises("c_x2t_psum", s))
                for s in two:
                    pe.wait_ge(*at("c_x2t", s, n2))
                    for k in range(2):
                        T.matmul(lane_bank(s, 1 + k), W["L1_gnn_W1"][:, k * P:(k + 1) * P], lane(s, 2), start=True, stop=True).then_inc(rises(f"c_up{k}_psum", s), 1)
                for s in two:
                    for b in range(G):
                        for k in range(2):
                            if b == 0:
                                pe.wait_ge(*at(f"c_up{k}", s, n2))
                            last = T.matmul(squares(lane_bank(s, 1))[:, b, :], squares(lane(s, 7 + k))[:, b, :], w2_gnn[:, k, :],
                                            start=(b == 0 and k == 0), stop=(k == 1), skip_group_check=True)
                    last.then_inc(rises("c_ff_psum", s), 1)
                for s in one:
                    pe.wait_ge(*at("c_block_x1", s, n1))
                    transposes(lane_bank(s, 1), squares(lane(s, 4)), rises("c_x1t_psum", s))
                for s in one:
                    pe.wait_ge(*at("c_x1t", s, n1))
                    T.matmul(lane_bank(s, 0), W["L1_gnn_Wq"][:], lane(s, 2), start=True, stop=True).then_inc(rises("c_q_psum", s), 1)
                    T.matmul(lane_bank(s, 1), W["L1_gnn_Wk"][:], lane(s, 2), start=True, stop=True)
                    by_square(lane_bank(s, 3), squares(lane(s, 2)), W["L1_gnn_Wv"][:], rises("c_kv_psum", s))
                for s in one:
                    pe.wait_ge(*at("c_q", s, n1))
                    pe.wait_ge(*at("c_v", s, n1))
                    for b in range(G):
                        T.matmul(lane_banks(s)[:, b, :], ident_h[:], mask_add[:].rearrange("p b m -> p (b m)"), start=True,
                                 stop=False, skip_group_check=True)
                        last = T.matmul(lane_banks(s)[:, b, :], squares(lane(s, 4))[:, b, :],
                                        lane(s, 7, 4).rearrange("p (h b m) -> p h b m", h=HEADS, b=G)[:, :, b, :],
                                        start=False, stop=True, skip_group_check=True)
                    last.then_inc(rises("c_s_psum", s), 1)
                for s in two:
                    pe.wait_ge(*at("c5_normed", s, n2))
                    transposes(lane_bank(s, 0), routed[:, second, tokens_of(s), 0:P], rises("c_x4t_psum", s))
                if second is not None:
                    last = None
                    for s in two:
                        pe.wait_ge(*at("c_x4t", s, n2))
                        for b in range(G):
                            c = s % (PAIR // G) * G + b
                            last = T.matmul(bank(second, 1)[:, c * EXPERTS:(c + 1) * EXPERTS], squares(lane(s, 2))[:, b, :],
                                            W["L1_ffn_Wr"][:], start=(c == 0), stop=True, skip_group_check=True)
                    last.then_inc(rises("d_logits_psum", second), 1)
                for b in range(G):
                    for s in one:
                        if b == 0:
                            pe.wait_ge(*at("c_exp", s, n1))
                        transposes(lane_banks(s)[:, b, :], squares(lane(s, 7 + 2 * b, 2)), rises(f"c_pt{b}_psum", s))
                if second is not None:
                    pe.wait_ge(*at("d_chosen", second, n2))
                    chosen = router[:, second, 8]
                    places = bank(second, 1)[:, 0:(PAIR + 1) * EXPERTS].rearrange("p (b e) -> p b e", b=PAIR + 1)
                    T.matmul(bank(second, 1)[:, 0:PAIR * EXPERTS], before[:], chosen.rearrange("p b e -> p (b e)"), start=True, stop=False, skip_group_check=True)
                    for b in range(PAIR):
                        last = T.matmul(places[:, b + 1:, :], ones[:], chosen[:, b:b + 1, :].to_broadcast([P, PAIR - b, EXPERTS]),
                                        start=False, stop=(b == PAIR - 1), skip_group_check=True)
                    last.then_inc(rises("d_places_psum", second), 1)
                    pe.wait_ge(*at("d_mask", second, n2))
                    transposes(bank(second, 0), router[:, second, 6], rises("d_maskt_psum", second), rows=EXPERTS)
                for b in range(G):
                    for s in one:
                        pe.wait_ge(*at(f"c_pt{b}", s, n1))
                        for h in range(HEADS):
                            last = T.matmul(attended(s)[:, b, h, :], squares(lane(s, 12 + 2 * b, 2))[:, h, :],
                                            v_ones[:, s, b, h, :], start=(h == 0), stop=True, skip_group_check=True)
                        if b == G - 1:
                            last.then_inc(rises("c_o_psum", s), 1)
                for c in range(FC):
                    for s in two:
                        if c == 0:
                            pe.wait_ge(*at("d_place", second, n2))
                            pe.wait_ge(sem("d_counted"), n2 * SLOTS + second + 2 - SLOTS)
                        if c == 1:
                            pe.wait_ge(*at("d_maskt", second, n2))
                        if c >= 2:
                            pe.wait_ge(*at(f"d_up{c - 2}", s, n2))
                        T.matmul(lane_bank(s, (1 + c) % 2), up_w[:, 0, c * P:(c + 1) * P], lane(s, 2), start=True, stop=True).then_inc(rises(f"d_up{c}_psum", s), 1)
                for s in two:
                    pe.wait_ge(*at("d_up2", s, n2))
                    for b in range(G):
                        for c in range(FC):
                            if b == 0 and c == FC - 1:
                                pe.wait_ge(*at("d_up3", s, n2))
                            last = T.matmul(squares(lane_bank(s, 3))[:, b, :], squares(lane(s, 12 + c))[:, b, :], down_w[:, 0, c, :],
                                            start=(b == 0 and c == 0), stop=False, skip_group_check=True)
                        c = s % (PAIR // G) * G + b
                        last = T.matmul(squares(lane_bank(s, 3))[:, b, :], mask_t[:, second, c * P:(c + 1) * P], down_b[:],
                                        start=False, stop=True, skip_group_check=True)
                    last.then_inc(rises("d_down_psum", s), 1)

            both_halves(0, 1, None, None)
            with pe.Fori(0, J - 1) as j:
                both_halves(1, j + 1, 0, j + 1)
                both_halves(0, j + 2, 1, j + 1)
            both_halves(1, J, 0, J)
            both_halves(None, None, 1, J)

            for s in range(LANES):
                pe.wait_ge(*at("d_y", s, J))
            with pe.Fori(0, TILES // SLOTS) as j:
                n = j + 1
                for s in range(SLOTS):
                    pe.wait_ge(sem("m_rows_in", s), 16 * n)
                    transposes(bank(s, 0), routed[:, s, :, 0:P], rises("m_xt_psum", s))
                for s in range(SLOTS):
                    pe.wait_ge(*at("m_xt", s, n))
                    pe.wait_ge(sem("m_staged", s), n)
                    pe.wait_ge(sem("m_y", s), n)
                    for c in range(FC):
                        T.matmul(bank(s, (1 + c) % 4), tile(s, 5)[:, c * P:(c + 1) * P], tile(s, 2), start=True, stop=True).then_inc(rises(f"m_up{c}_psum", s), 1)
                for s in range(SLOTS):
                    for a in range(SUB):
                        for c in range(FC):
                            if a == 0:
                                pe.wait_ge(*at(f"m_h{c}", s, n))
                            last = T.matmul(squares(bank(s, 1))[:, a, :], squares(tile(s, 12 + c))[:, a, :],
                                            tile(s, 6)[:, c * P:(c + 1) * P], start=(a == 0 and c == 0), stop=(c == FC - 1),
                                            skip_group_check=True)
                    last.then_inc(rises("m_down_psum", s), 1)
    return nc


_IN = ("x", "adj", "L0_gnn_w1_loop", "L0_gnn_w1_neigh", "L0_gnn_b1", "L0_gnn_w2_loop", "L0_gnn_w2_neigh",
       "L0_gnn_b2", "L0_ffn_U_i", "L0_ffn_V_i", "L0_ffn_b_i", "L0_ffn_U_c", "L0_ffn_V_c", "L0_ffn_b_c",
       "L0_ffn_U_o", "L0_ffn_V_o", "L0_ffn_b_o", "L1_gnn_Wc", "L1_gnn_bc", "L1_gnn_g1", "L1_gnn_be1",
       "L1_gnn_Wq", "L1_gnn_Wk", "L1_gnn_Wv", "L1_gnn_Wo", "L1_gnn_bo", "L1_gnn_g2", "L1_gnn_be2", "L1_gnn_W1",
       "L1_gnn_b1", "L1_gnn_W2", "L1_gnn_b2", "L1_gnn_g3", "L1_gnn_be3", "L1_ffn_Wr", "L1_ffn_W1s", "L1_ffn_b1s",
       "L1_ffn_W2s", "L1_ffn_b2s", "L1_ffn_W1p", "L1_ffn_b1p", "L1_ffn_W2p", "L1_ffn_b2p")


def kernel(**inputs):
    import numpy as _np
    import concourse.bacc as _bacc
    from concourse import mybir as _mybir
    from concourse.bass_utils import run_bass_kernel_spmd as _run

    nc = _bacc.Bacc("TRN2", target_bir_lowering=False, num_devices=1)
    arrays, tensors = {}, {}
    for name in _IN:
        a = _np.ascontiguousarray(inputs[name])
        arrays[f"in_{name}"] = a
        tensors[name] = nc.dram_tensor(f"in_{name}", a.shape, _mybir.dt.from_np(a.dtype), kind="ExternalInput").ap()
    tensors["out"] = nc.dram_tensor("out_0", (128 * 128 + TILE, 128), _mybir.dt.float32, kind="ExternalOutput").ap()
    build(nc, tensors)
    r = _run(nc, [arrays], core_ids=[0])
    return r.results[0]["out_0"][:128 * 128].reshape(128, 128, 128)
```

```python
from contextlib import ExitStack

import concourse.bass as bass
from concourse import mybir

P = 128
G = 2
GROUP = G * P
BANK = 512
LANES = 4
SLOTS = 2
PAIR = LANES // SLOTS * G
HEADS = 4
HD = P // HEADS
EXPERTS = 8
FF = 512
FC = FF // P
TOP = 2
ROW = P + 4
TILE = 512
SUB = TILE // P
TOKENS = P * P
REGION = TOKENS + TILE
TILES = (TOP * TOKENS + EXPERTS * (TILE - 1)) // TILE
TILES += TILES % 2
STEPS = 4
SQUARINGS = P // STEPS - 1
EPS = 1e-5
L1_LOADS = 16 * (7 + 1 + 1 + 1 + 1 + EXPERTS + 2 + 2 + 1 + 10)
F32 = mybir.dt.float32
BF16 = mybir.dt.bfloat16
U32 = mybir.dt.uint32
I32 = mybir.dt.int32
ALU = mybir.AluOpType
ACT = mybir.ActivationFunctionType
AX = mybir.AxisListType


def build(nc, t):
    B, N, D = t["x"].shape
    assert B == N == D == P
    J = B // (G * LANES)
    ctx = ExitStack()
    with ctx:
        def sb(name, shape, dt=F32):
            return ctx.enter_context(nc.sbuf_tensor(name, shape, dt))

        sems = {}

        def sem(name, *which):
            key = "_".join([name, *map(str, which)])
            if key not in sems:
                sems[key] = ctx.enter_context(nc.semaphore(key))
            return sems[key]

        psum = ctx.enter_context(nc.psum_tensor("psum", [P, 8, BANK], F32))

        def early(eng, *values):
            for v in values:
                eng.compute_val(v)
            return values

        def nth(n, per_pass, k):
            return n * per_pass + (k + 1 - per_pass)

        SHARED = {
            "a_psum": ("a_xt_psum", "a_z1_psum", "a_h1t_psum", "a_h1_psum", "a_z2_psum", "a_h2t_psum", "a_h2_psum"),
            "a_norm1": ("a1_stats", "a1_moments", "a1_normed"),
            "a_dve": ("a_z1", "a_x_half", "a_h1", "a_x1", "a2_stats",
                      "a2_moments", "a2_normed"),
            "a_act": ("a_xt", "a_h1t", "a_z2", "a_h2t"),
            "a_pool1": ("a1_var", "a1_rstd"),
            "a_pool2": ("a2_var", "a2_rstd"),
            "r_cells": ("r_hc", "r_ic", "r_cell", "r_state"),
            "r_z_psum": ("r_zic_psum", "r_zo_psum"),
            "r_tanhs": ("r_gates", "r_out_gate", "r_tanh"),
            "c_psum": ("c_hs_psum", "c_xp_psum", "c_h_psum", "c_x1t_psum", "c_q_psum", "c_kv_psum", "c_s0_psum", "c_s1_psum",
                       "c_pt0_psum", "c_pt1_psum", "c_o_psum", "c_ot_psum", "c_wo_psum", "c_x2t_psum", "c_up0_psum",
                       "c_up1_psum", "c_ff_psum", "c_x4t_psum"),
            "c_act": ("c_xp", "c_x1t", "c_k", "c_v", "c_exp0", "c_exp1", "c_pt0", "c_pt1", "c_ot", "c_x2t", "c_up0", "c_up1",
                      "c_x4t"),
            "c_dve": ("c_x2", "c1_stats", "c1_moments", "c1_normed", "c_h", "c2_stats", "c2_moments", "c2_gained",
                      "c2_shifted", "c_block_x1", "c_q", "c_max0", "c_negmax0", "c_max1", "c_negmax1", "c_inv", "c_o", "c_res2", "c3_stats",
                      "c3_moments", "c3_gained", "c_x2n", "c_res3", "c4_stats", "c4_moments", "c4_gained", "c_x3",
                      "c5_stats", "c5_moments", "c5_normed"),
            "c_pool": ("c1_var", "c1_rstd", "c2_var", "c2_rstd", "c_x1_bo", "c_x_be3", "c3_var", "c3_rstd", "c_x2_b2",
                       "c4_var", "c4_rstd", "c5_var", "c5_rstd", "c_x3_b2s"),
            "e_psum": ("e_up0_psum", "e_up1_psum", "e_up2_psum", "e_up3_psum", "e_down_psum"),
            "e_act": ("e_up0", "e_up1", "e_up2", "e_up3"),
            "d_psum": ("d_logits_psum", "d_places_psum"),
            "d_act": ("d_exp",),
            "d_route": ("d_max", "d_sub", "d_top", "d_idx", "d_den", "d_inv", "d_w", "d_idxf", "d_eq0", "d_eq1",
                        "d_chosen", "d_place", "d_prod0", "d_prod1",
                        "d_slot0", "d_slot1", "d_slots"),
            "m_psum": ("m_xt_psum", "m_up0_psum", "m_up1_psum", "m_up2_psum", "m_up3_psum", "m_down_psum"),
            "m_act": ("m_xt", "m_h0", "m_h1", "m_h2", "m_h3"),
            "m_weights": ("m_is_first", "m_diff", "m_part", "m_weight", "m_ids"),
        }
        AHEAD = {"x1_stored": LANES, "out_stored": LANES, "rows_free": SLOTS, "m_psum": SLOTS,
                 "m_y": SLOTS, "m_free": SLOTS, "m_weights": SLOTS}
        PLACE = {step: (name, len(steps), k) for name, steps in SHARED.items() for k, step in enumerate(steps)}

        def rises(step, s):
            return sem(PLACE[step][0], s)

        def at(step, s, n):
            name, per_pass, k = PLACE[step]
            return sem(name, s), nth(n, per_pass, k) + (1 if name in AHEAD else 0)

        def bank(s, k):
            return psum[:, 4 * s + k, :]

        def lane_bank(s, k):
            return psum[:, 2 * s + k % 2, k // 2 * GROUP:(k // 2 + 1) * GROUP]

        def lane_banks(s):
            return psum[:, 2 * s:2 * s + 2, :]

        def lane(s, k, n=1):
            at_col = (s * 16 + k) * GROUP
            return room[:, at_col:at_col + n * GROUP]

        def of_norm(tag, s):
            return LANES + s if tag == "a1" else s

        def lanes_of(pair):
            return range(PAIR // G * pair, PAIR // G * (pair + 1))

        def table(k, cols):
            return states[:, 8 * k:8 * (k + 1), :].rearrange("p n b -> p (n b)")[:, 0:cols]

        def tokens_of(s):
            return slice(s % (PAIR // G) * G, (s % (PAIR // G) + 1) * G)

        def squares(ap):
            return ap.rearrange("p (b f) -> p b f", f=P)

        def attended(s):
            return lane_banks(s)[:, :, 0:HEADS * (HD + 1)].rearrange("p b (h d) -> p b h d", h=HEADS)

        states = sb("states", [P, N + 1, B])
        room = sb("room", [P, LANES * 16 * GROUP])
        v_ones = sb("v_ones", [P, LANES, G, HEADS, HD + 1])

        def tile(s, k, n=1):
            at_col = (s * 16 + k) * BANK
            return room[:, at_col:at_col + n * BANK]

        W = {}
        for name, cols in (("L0_gnn_w1_loop", P), ("L0_gnn_w1_neigh", P), ("L0_gnn_w2_loop", P),
                           ("L0_gnn_w2_neigh", P), ("L1_gnn_Wc", P), ("L1_gnn_Wq", P),
                           ("L1_gnn_Wk", P), ("L1_gnn_Wv", P), ("L1_gnn_Wo", P), ("L1_gnn_W1", 2 * P),
                           ("L1_ffn_Wr", EXPERTS)):
            W[name] = sb("w_" + name, [P, cols])
        gate_u = sb("gate_u", [P, 3, P])
        gate_v = sb("gate_v", [P, 3, P])
        w2_gnn = sb("w2_gnn", [P, 2, P])
        up_w = sb("up_w", [P, 1 + EXPERTS, FF])
        down_w = sb("down_w", [P, 1 + EXPERTS, FC, P])
        up_b = sb("up_b", [P, 1 + EXPERTS, FC])
        down_b = sb("down_b", [P, EXPERTS, P])
        col_b = sb("col_b", [P, 8])
        gate_b = sb("gate_b", [1, 3, P])
        ROWS = ("L1_gnn_bc", "L1_gnn_g1", "L1_gnn_be1", "L1_gnn_bo", "L1_gnn_g2", "L1_gnn_be2",
                "L1_gnn_b2", "L1_gnn_g3", "L1_gnn_be3", "L1_ffn_b2s")
        row_b = sb("row_b", [P, len(ROWS), P])

        def row(name):
            return row_b[:, [full.split("_", 2)[2] for full in ROWS].index(name), :].unsqueeze(1).to_broadcast([P, G, P])

        adj = sb("adj", [P, P])
        adj_t = sb("adj_t", [P, P])
        lap_t = sb("lap_t", [P, P])
        ident = sb("ident", [P, P])
        ident_h = sb("ident_h", [P, P], BF16)
        ones = sb("ones", [P, P])
        mask_add = sb("mask_add", [P, HEADS, P], BF16)
        row_any = sb("row_any", [P, P])
        sc = sb("sc", [P, 16])
        expert_no = sb("expert_no", [P, PAIR, EXPERTS])
        head_col = sb("head_col", [P, HEADS])
        half_neg = sb("half_neg", [P, G])
        eps_tile = sb("eps_tile", [P, G])
        starts = sb("starts", [P, 64])
        waiting = sb("waiting", [P, 1])
        sym, power, tmp, square = (lane(1, 9, 2)[:, k * P:(k + 1) * P] for k in range(4))
        cell, state_cell, in_cand, cell_tanh = (lane(0, 9, 2)[:, k * B:(k + 1) * B] for k in range(4))
        hidden = lane(2, 9, 2).rearrange("p (k b) -> p k b", k=STEPS)
        gates = lane(0, 11, 3)[:, 0:6 * B].rearrange("p (k g b) -> p k g b", k=2, g=3)
        stats = sb("stats", [P, 2 * LANES, G, 6])
        moments = sb("moments", [P, 2 * LANES, G, 2])
        rstd = sb("rstd", [P, 2 * LANES, G])
        top = sb("top", [P, LANES, 2, G * HEADS])
        inv_sum = sb("inv_sum", [P, LANES, G, HEADS])
        router = sb("router", [P, SLOTS, 12, PAIR, EXPERTS])
        best_idx = sb("best_idx", [P, SLOTS, PAIR, 8], U32)
        routed = sb("routed", [P, SLOTS, SUB, ROW])
        assert PAIR == SUB
        padding = sb("padding", [P, SUB, ROW])
        token_no = sb("token_no", [P, B], I32)
        before = sb("before", [P, P], BF16)
        ones_h = sb("ones_h", [P, P], BF16)
        chosen = sb("chosen", [P, SLOTS, PAIR, EXPERTS], BF16)
        region_at = sb("region_at", [P, EXPERTS])
        next_row = sb("next_row", [P, EXPERTS])
        row_idx = sb("row_idx", [P, SLOTS, PAIR, TOP], U32)
        row_weight = sb("row_weight", [P, SLOTS, 4, SUB])
        expert_now = sb("expert_now", [P, SLOTS])
        row_token = sb("row_token", [P, SLOTS, SUB], U32)
        tile_at = sb("tile_at", [P, TILES], I32)
        tile_expert = sb("tile_expert", [P, TILES], I32)
        next_row_i = sb("next_row_i", [P, EXPERTS], I32)

        x1_dram = nc.dram_tensor("x1_scratch", [N, B, D], F32, kind="Internal").ap()
        x_rows = t["x"].rearrange("b n d -> n b d")
        out_rows = t["out"][0:TOKENS, :].rearrange("(b n) d -> n b d", n=N)
        routed_dram = nc.dram_tensor("routed_rows", [EXPERTS * REGION + TILE, ROW], F32, kind="Internal").ap()

        block = ctx.enter_context(nc.Block())

        def pad_expert(eng, e):
            at_row = eng.value_load(next_row_i[0:1, e:e + 1], min_val=e * REGION, max_val=e * REGION + TOKENS)
            eng.dma_start(routed_dram[bass.ds(at_row, TILE), :].rearrange("(a p) d -> p a d", p=P),
                          padding[:]).then_inc(sem("padded"), 16)

        @block.sync
        def _(sp):
            sp.dma_start(adj[:], t["adj"]).then_inc(sem("adj_loaded"), 16)
            for name in ("L0_gnn_w1_loop", "L0_gnn_w1_neigh", "L0_gnn_w2_loop", "L0_gnn_w2_neigh"):
                sp.dma_start(W[name][:], t[name]).then_inc(sem("l0_loaded"), 16)
            for k, name in enumerate(("L0_gnn_b1", "L0_gnn_b2")):
                sp.dma_start(col_b[:, k:k + 1], t[name].unsqueeze(1)).then_inc(sem("l0_loaded"), 16)

            def load_x(s, b):
                sp.dma_start(squares(lane(s, 14)), x_rows[:, b, :]).then_inc(sem("x_in", s), 16)

            def store_x1(s, b, normed):
                sp.wait_ge(rises("a2_normed", s), normed)
                sp.dma_start(x1_dram[:, b, :], squares(lane(s, 0))).then_inc(sem("x1_stored", s), 16)

            for s in range(LANES):
                load_x(s, bass.ds(s * G, G))
            with sp.Fori(0, J - 1) as j:
                batch = early(sp, *((j * LANES + s) * G for s in range(LANES)))
                following = early(sp, *((j * LANES + LANES + s) * G for s in range(LANES)))
                read, normed = early(sp, at("a_x_half", 0, j + 1)[1], at("a2_normed", 0, j + 1)[1])
                for s in range(LANES):
                    sp.wait_ge(rises("a_x_half", s), read)
                    load_x(s, bass.ds(following[s], G))
                for s in range(LANES):
                    store_x1(s, bass.ds(batch[s], G), normed)
            for s in range(LANES):
                store_x1(s, bass.ds(((J - 1) * LANES + s) * G, G), at("a2_normed", s, J)[1])
            for s in range(LANES):
                sp.wait_ge(sem("x1_stored", s), 16 * J + 1)

            def load_x1(s, b):
                sp.dma_start(squares(lane(s, 0)), x1_dram[:, b, :]).then_inc(sem("c_x1_in", s), 16)

            def store_y(s, b, count):
                sp.wait_ge(sem("e_y", s), count)
                sp.dma_start(out_rows[:, b, :], squares(lane(s, 11))).then_inc(sem("out_stored", s), 16)

            for s in range(LANES):
                load_x1(s, bass.ds(s * G, G))
            with sp.Fori(0, J - 1) as j:
                batch = early(sp, *((j * LANES + s) * G for s in range(LANES)))
                following = early(sp, *((j * LANES + LANES + s) * G for s in range(LANES)))
                added, done = early(sp, at("c_x3", 0, j + 1)[1], j + 1)
                for pair in range(SLOTS):
                    for s in lanes_of(pair):
                        sp.wait_ge(rises("c_x3", s), added)
                        load_x1(s, bass.ds(following[s], G))
                    for s in lanes_of(pair):
                        store_y(s, bass.ds(batch[s], G), done)
            for s in lanes_of(0):
                store_y(s, bass.ds(((J - 1) * LANES + s) * G, G), J)
            sp.dma_start(t["out"][TOKENS:, :].rearrange("(a p) d -> p a d", p=P), padding[:, :, 0:P]).then_inc(sem("padded"), 16)
            sp.dma_start(routed_dram[EXPERTS * REGION:, :].rearrange("(a p) d -> p a d", p=P), padding[:]).then_inc(sem("padded"), 16)
            sp.wait_ge(sem("tables"), 1)
            for e in range(EXPERTS // 2):
                pad_expert(sp, e)
            for s in lanes_of(1):
                store_y(s, bass.ds(((J - 1) * LANES + s) * G, G), J)
            for s in range(SLOTS):
                sp.wait_ge(sem("scattered", s), 16 * PAIR * TOP * J)
            sp.wait_ge(sem("padded"), 16 * (EXPERTS + 2))
            for s in range(LANES):
                sp.wait_ge(sem("out_stored", s), 16 * J + 1)
            with sp.Fori(0, TILES // SLOTS) as j:
                (read,) = early(sp, at("m_ids", 0, j)[1])
                for s in range(SLOTS):
                    at_row = sp.value_load(tile_at[0:1, bass.ds(j * SLOTS + s, 1)], min_val=0, max_val=EXPERTS * REGION)
                    sp.wait_ge(rises("m_ids", s), read)
                    sp.dma_start(routed[:, s, :, :], routed_dram[bass.ds(at_row, TILE), :].rearrange(
                        "(a p) d -> p a d", p=P)).then_inc(sem("m_rows_in", s), 16)

        @block.gpsimd
        def _(pool):
            nc.gpsimd.memset(ident[:], 0.0).then_inc(sem("p_zero"), 1)
            nc.gpsimd.memset(ones[:], 1.0)
            nc.gpsimd.memset(ones_h[:], 1.0)
            nc.gpsimd.memset(half_neg[:], -0.5)
            nc.gpsimd.memset(eps_tile[:], EPS)
            nc.gpsimd.memset(states[:, 0, :], 0.0)
            nc.gpsimd.memset(v_ones[:], 1.0)
            nc.gpsimd.iota(expert_no[:], pattern=[[0, PAIR], [1, EXPERTS]], base=0, channel_multiplier=0,
                           allow_small_or_imprecise_dtypes=True)
            spots = iter(range(64))
            for name, count in AHEAD.items():
                for s in range(count):
                    spot = next(spots)
                    nc.gpsimd.memset(starts[:, spot:spot + 1], 0.0).then_inc(sem(name, s), 1)
            for step in range(STEPS):
                nc.gpsimd.memset(starts[:, 48 + step:49 + step], 0.0).then_inc(sem("r_kept"), 1)
            nc.gpsimd.memset(padding[:], 0.0).then_inc(sem("p_zero"), 1)
            nc.gpsimd.iota(token_no[:], pattern=[[P, B]], base=0, channel_multiplier=1)
            nc.gpsimd.iota(region_at[:], pattern=[[REGION, EXPERTS]], base=0, channel_multiplier=0,
                           allow_small_or_imprecise_dtypes=True)
            nc.gpsimd.iota(next_row[:], pattern=[[REGION, EXPERTS]], base=0, channel_multiplier=0,
                           allow_small_or_imprecise_dtypes=True).then_inc(sem("d_counted"), 1)
            pool.wait_ge(sem("p_zero"), 2)
            nc.gpsimd.affine_select(out=head_col[:], in_=ones[:, 0:HEADS], compare_op=ALU.is_gt, fill=0.0, base=1,
                                    pattern=[[-HD, HEADS]], channel_multiplier=1)
            nc.gpsimd.iota(padding[:, :, ROW - 1].bitcast(I32), pattern=[[P, SUB]], base=TOKENS, channel_multiplier=1)
            nc.gpsimd.affine_select(out=before[:], in_=ones_h[:], compare_op=ALU.is_gt, fill=0.0, base=0,
                                    pattern=[[1, P]], channel_multiplier=-1)
            nc.gpsimd.affine_select(out=ident[:], in_=ident[:], compare_op=ALU.not_equal, fill=1.0, base=0,
                                    pattern=[[-1, P]], channel_multiplier=1).then_inc(sem("ident"), 1)
            pool.wait_ge(sem("ident"), 1)
            nc.gpsimd.affine_select(out=head_col[:], in_=head_col[:], compare_op=ALU.is_gt, fill=0.0, base=HD,
                                    pattern=[[HD, HEADS]], channel_multiplier=-1)
            nc.gpsimd.tensor_copy(ident_h[:], ident[:]).then_inc(sem("consts"), 1)

            def inverse_deviation(tag, s, n):
                pool.wait_ge(*at(tag + "_moments", s, n))
                k = of_norm(tag, s)
                nc.gpsimd.tensor_tensor(rstd[:, k, :], moments[:, k, :, 1], eps_tile[:], ALU.add).then_inc(rises(tag + "_var", s), 1)
                pool.wait_ge(*at(tag + "_var", s, n))
                nc.gpsimd.tensor_tensor(rstd[:, k, :], rstd[:, k, :], half_neg[:], ALU.pow).then_inc(rises(tag + "_rstd", s), 1)

            def vector_sum(tag, s, n, ready, out, a, b):
                pool.wait_ge(*ready)
                nc.gpsimd.tensor_tensor(squares(out), squares(a), b, ALU.add).then_inc(rises(tag, s), 1)

            def carry_wait_pool(k):
                return nc.gpsimd.tensor_tensor(starts[:, k:k + 1], ones[:, 0:1], ones[:, 0:1], ALU.mult)

            for s in range(LANES):
                inverse_deviation("a1", s, 1)
            with pool.Fori(0, J - 1) as j:
                for s in range(LANES):
                    inverse_deviation("a1", s, j + 2)
                for s in range(LANES):
                    inverse_deviation("a2", s, j + 1)
            for s in range(LANES):
                inverse_deviation("a2", s, J)
            for s in range(LANES):
                pool.wait_ge(sem("a_x1t", s), J)
            nc.gpsimd.memset(cell[:], 0.0).then_inc(sem("r_zero"), 1)
            nc.gpsimd.memset(hidden[:, STEPS - 1, :], 0.0).then_inc(sem("r_zero"), 1)
            for name in ("L1_gnn_Wc", "L1_gnn_Wq", "L1_gnn_Wk", "L1_gnn_Wv", "L1_gnn_Wo", "L1_gnn_W1", "L1_ffn_Wr"):
                pool.dma_start(W[name][:], t[name]).then_inc(sem("l1_loaded"), 16)
            pool.dma_start(w2_gnn[:], t["L1_gnn_W2"].rearrange("(c p) d -> p c d", p=P)).then_inc(sem("l1_loaded"), 16)
            pool.dma_start(up_w[:, 0, :], t["L1_ffn_W1s"]).then_inc(sem("l1_loaded"), 16)
            pool.dma_start(up_w[:, 1:, :], t["L1_ffn_W1p"].rearrange("e p f -> p e f")).then_inc(sem("l1_loaded"), 16)
            pool.dma_start(down_w[:, 0, :, :], t["L1_ffn_W2s"].rearrange("(c p) d -> p c d", p=P)).then_inc(sem("l1_loaded"), 16)
            for e in range(EXPERTS):
                pool.dma_start(down_w[:, 1 + e, :, :], t["L1_ffn_W2p"][e].rearrange("(c p) d -> p c d", p=P)).then_inc(sem("l1_loaded"), 16)
            with nc.allow_non_contiguous_dma(reason="small bias columns"):
                pool.dma_start(up_b[:, 0, :], t["L1_ffn_b1s"].rearrange("(c p) -> p c", p=P)).then_inc(sem("l1_loaded"), 16)
                pool.dma_start(up_b[:, 1:, :], t["L1_ffn_b1p"].rearrange("e (c p) -> p e c", p=P)).then_inc(sem("l1_loaded"), 16)
                for k in range(2):
                    pool.dma_start(col_b[:, 5 + k:6 + k], t["L1_gnn_b1"][k * P:(k + 1) * P].unsqueeze(1)).then_inc(sem("l1_loaded"), 16)
            pool.dma_start(down_b[:], t["L1_ffn_b2p"].partition_broadcast(P)).then_inc(sem("l1_loaded"), 16)
            for k, name in enumerate(ROWS):
                pool.dma_start(row_b[:, k, :], t[name].partition_broadcast(P)).then_inc(sem("l1_loaded"), 16)
            with pool.Fori(0, N // STEPS) as quad:
                for step in range(STEPS):
                    k, n = step % 2, quad * 2 + step // 2 + 1
                    pool.wait_ge(*at("r_state", k, n))
                    nc.gpsimd.tensor_copy(states[:, bass.ds(quad * STEPS + step + 1, 1), :].rearrange("p a b -> p (a b)"),
                                          hidden[:, step, :]).then_inc(sem("r_kept"), 1)
            pool.wait_ge(sem("r_kept"), N + STEPS)
            pool.wait_ge(sem("l1_loaded"), L1_LOADS)
            pool.wait_ge(sem("recurrence_done"), 1)

            def hidden_columns(s, b0):
                nc.gpsimd.tensor_copy(squares(lane(s, 6)),
                                      states[:, 1:, bass.ds(b0, G)].rearrange("p n b -> p b n")).then_inc(sem("c_hs", s), 1)

            def scatter(pair, b):
                for k in range(TOP):
                    pool.indirect_dma_start(
                        routed_dram, bass.IndirectOffsetOnAxis(ap=row_idx[:, pair, b, k:k + 1], axis=0),
                        routed[:, pair, b, :], None).then_inc(sem("scattered", pair), 16)

            def both_halves(first, n1, second, n2, shared, n3, more):
                pairs_of = lambda p: () if p is None else lanes_of(p)
                one, two = pairs_of(first), pairs_of(second)
                for s in one:
                    inverse_deviation("c1", s, n1)
                if shared is not None:
                    pool.wait_ge(*at("d_slots", shared, n3))
                    carry_wait_pool(56 + shared)
                for s in two:
                    vector_sum("c_x_be3", s, n2, at("c1_normed", s, n2), lane(s, 0), lane(s, 0), row("be3"))
                for s in two:
                    inverse_deviation("c3", s, n2)
                if shared is not None:
                    for b in range(PAIR):
                        scatter(shared, b)
                for s in one:
                    inverse_deviation("c2", s, n1)
                if shared is not None:
                    pool.wait_ge(sem("scattered", shared), 16 * PAIR * TOP * n3)
                    carry_wait_pool(58 + shared).then_inc(sem("rows_free", shared), 1)
                for s in two:
                    vector_sum("c_x2_b2", s, n2, at("c_x2n", s, n2), lane(s, 3), lane(s, 5), row("b2"))
                for s in one:
                    vector_sum("c_x1_bo", s, n1, at("c_block_x1", s, n1), lane(s, 3), lane(s, 4), row("bo"))
                for tag in ("c4", "c5"):
                    for s in two:
                        inverse_deviation(tag, s, n2)
                for s in two:
                    vector_sum("c_x3_b2s", s, n2, at("c5_normed", s, n2), lane(s, 11), lane(s, 11), row("b2s"))
                if more:
                    for s in two:
                        pool.wait_ge(*at("c_hs_psum", s, n2))
                        hidden_columns(s, (n2 * LANES + s) * G)

            for s in range(LANES):
                hidden_columns(s, s * G)
            both_halves(0, 1, None, None, None, None, True)
            both_halves(1, 1, 0, 1, None, None, True)
            with pool.Fori(0, J - 2) as j:
                both_halves(0, j + 2, 1, j + 1, 0, j + 1, True)
                both_halves(1, j + 2, 0, j + 2, 1, j + 1, True)
            both_halves(0, J, 1, J - 1, 0, J - 1, True)
            both_halves(1, J, 0, J, 1, J - 1, False)
            for s in range(LANES):
                pool.wait_ge(sem("c_hs", s), J)
            nc.gpsimd.iota(table(0, EXPERTS * (TOKENS // TILE)), pattern=[[0, EXPERTS], [TILE, TOKENS // TILE]],
                           base=0, channel_multiplier=0, allow_small_or_imprecise_dtypes=True)
            nc.gpsimd.iota(table(1, TILES), pattern=[[1, TILES]], base=0, channel_multiplier=0,
                           allow_small_or_imprecise_dtypes=True).then_inc(sem("table_consts"), 1)
            both_halves(None, None, 1, J, 0, J, False)
            both_halves(None, None, None, None, 1, J, False)
            for s in range(LANES):
                pool.wait_ge(sem("out_stored", s), 16 * J + 1)
            pool.wait_ge(sem("padded"), 16 * (EXPERTS + 2))
            with pool.Fori(0, TILES // SLOTS) as j:
                for s in range(SLOTS):
                    pool.wait_ge(sem("m_y", s), j + 2)
                    carry_wait_pool(60 + s)
                    for a in range(SUB):
                        pool.indirect_dma_start(
                            t["out"], bass.IndirectOffsetOnAxis(ap=row_token[:, s, a:a + 1], axis=0),
                            squares(tile(s, 11))[:, a, :], None, compute_op=ALU.add).then_inc(sem("m_added", s), 16)
                    pool.wait_ge(sem("m_added", s), 16 * SUB * (j + 1))
                    carry_wait_pool(62 + s).then_inc(sem("m_free", s), 1)

        @block.vector
        def _(dve):
            V = nc.vector

            def carry_wait():
                V.tensor_copy(waiting[:], ones[:, 0:1])

            def measure(tag, s, n, src):
                for b in range(G):
                    last = V.bn_stats(stats[:, of_norm(tag, s), b, :], src[:, b, :])
                last.then_inc(rises(tag + "_stats", s), 1)
                dve.wait_ge(*at(tag + "_stats", s, n))
                carry_wait()
                for b in range(G):
                    last = V.bn_aggr(moments[:, of_norm(tag, s), b, :], stats[:, of_norm(tag, s), b, :])
                last.then_inc(rises(tag + "_moments", s), 1)

            def normalize(tag, s, n, src, dst):
                dve.wait_ge(*at(tag + "_rstd", s, n))
                for b in range(G):
                    last = V.tensor_scalar(dst[:, b, :], src[:, b, :], moments[:, of_norm(tag, s), b, 0:1],
                                           rstd[:, of_norm(tag, s), b:b + 1],
                                           ALU.subtract, ALU.mult)
                last.then_inc(rises(tag + "_normed", s), 1)

            def gain(tag, s, n, src, vector):
                dve.wait_ge(*at(tag + "_moments", s, n))
                for b in range(G):
                    last = V.scalar_tensor_tensor(src[:, b, :], src[:, b, :], moments[:, s, b, 0:1], row(vector)[:, 0, :],
                                                  ALU.subtract, ALU.mult)
                last.then_inc(rises(tag + "_gained", s), 1)

            def shift(tag, s, n, src, dst, added, done):
                dve.wait_ge(*at(tag + "_gained", s, n))
                dve.wait_ge(*at(tag + "_rstd", s, n))
                for b in range(G):
                    last = V.scalar_tensor_tensor(dst[:, b, :], src[:, b, :], rstd[:, s, b:b + 1], added[:, b, :],
                                                  ALU.mult, ALU.add)
                last.then_inc(rises(done, s), 1)

            dve.wait_ge(sem("adj_t_psum"), 1)
            V.tensor_copy(adj_t[:], bank(0, 0)[:, 0:P]).then_inc(sem("adj_t"), 1)
            dve.wait_ge(sem("l0_loaded"), 16 * 6)
            V.tensor_scalar(col_b[:, 2:3], col_b[:, 1:2], 0.5, None, ALU.mult).then_inc(sem("b2_half"), 1)

            dve.wait_ge(sem("adj_t"), 1)
            V.tensor_tensor(tmp[:], adj[:], adj_t[:], ALU.add).then_inc(sem("one_shot"), 1)
            dve.wait_ge(sem("one_shot"), 1)
            V.tensor_scalar(sym[:], tmp[:], 0.5, None, ALU.mult).then_inc(sem("one_shot"), 1)
            dve.wait_ge(sem("one_shot"), 2)
            V.tensor_reduce(sc[:, 0:1], sym[:], AX.X, ALU.add, apply_absolute_value=True).then_inc(sem("one_shot"), 1)
            dve.wait_ge(sem("one_shot"), 3)
            V.tensor_scalar(square[:], ones[:], sc[:, 0:1], None, ALU.mult).then_inc(sem("e_spread"), 1)
            dve.wait_ge(sem("e_bound_psum"), 1)
            V.tensor_reduce(sc[:, 1:2], bank(1, 2)[:, 0:P], AX.X, ALU.max).then_inc(sem("one_shot"), 1)
            dve.wait_ge(sem("one_shot"), 4)
            V.tensor_scalar(sc[:, 5:6], sc[:, 1:2], 1e-30, None, ALU.add).then_inc(sem("one_shot"), 1)
            dve.wait_ge(sem("one_shot"), 5)
            V.scalar_tensor_tensor(square[:], ident[:], sc[:, 5:6], sym[:], ALU.mult, ALU.add).then_inc(sem("e_copied"), 1)

            def trace_of_square(count):
                dve.wait_ge(sem("e_copied"), count)
                V.tensor_tensor_reduce(tmp[:], square[:], ident[:], 1.0, 0.0, ALU.mult, ALU.add, sc[:, 2:3]).then_inc(sem("e_diag"), 1)

            def inverse_trace(count):
                dve.wait_ge(sem("e_trace_psum"), count)
                V.reciprocal(sc[:, 3:4], bank(1, 3)[:, 0:1]).then_inc(sem("e_inv"), 1)

            trace_of_square(1)
            inverse_trace(1)
            V.tensor_scalar(tmp[:], adj[:], 0.0, None, ALU.is_gt).then_inc(sem("one_shot"), 1)
            dve.wait_ge(sem("one_shot"), 6)
            V.tensor_reduce(sc[:, 10:11], tmp[:], AX.X, ALU.max).then_inc(sem("one_shot"), 1)
            dve.wait_ge(sem("one_shot"), 7)
            V.tensor_scalar(tmp[:], tmp[:], sc[:, 10:11], 1e9, ALU.subtract, ALU.mult).then_inc(sem("one_shot"), 1)
            V.tensor_scalar(power[:], ident[:], sc[:, 10:11], None, ALU.mult).then_inc(sem("m_diag"), 1)
            dve.wait_ge(sem("one_shot"), 8)
            V.tensor_copy(mask_add[:], tmp[:].unsqueeze(1).to_broadcast([P, HEADS, P])).then_inc(sem("mask"), 1)
            dve.wait_ge(sem("m_any_psum"), 1)
            V.tensor_scalar(row_any[:], bank(1, 2)[:, 0:P], HD ** -0.5, None, ALU.mult).then_inc(sem("row_any"), 1)

            def measure_x(n):
                for s in range(LANES):
                    dve.wait_ge(sem("x_in", s), 16 * n)
                    measure("a1", s, n, squares(lane(s, 14)))

            def normalize_x(n):
                for s in range(LANES):
                    normalize("a1", s, n, squares(lane(s, 14)), squares(lane(s, 1)))

            def convolutions(n, more):
                for s in range(LANES):
                    dve.wait_ge(*at("a_z1_psum", s, n))
                    V.tensor_copy(lane(s, 3), lane_bank(s, 1)).then_inc(rises("a_z1", s), 1)
                for s in range(LANES):
                    dve.wait_ge(*at("a1_normed", s, n))
                    dve.wait_ge(sem("x1_stored", s), 16 * n - 15)
                    V.scalar_tensor_tensor(lane(s, 0), lane(s, 1), 0.5, lane(s, 14), ALU.mult, ALU.add).then_inc(rises("a_x_half", s), 1)
                for s in range(LANES):
                    dve.wait_ge(*at("a_h1_psum", s, n))
                    V.tensor_copy(lane(s, 5), lane_bank(s, 0)).then_inc(rises("a_h1", s), 1)
                if more:
                    measure_x(n + 1)
                    normalize_x(n + 1)
                for s in range(LANES):
                    dve.wait_ge(*at("a_h2_psum", s, n))
                    dve.wait_ge(*at("a_x_half", s, n))
                    V.tensor_tensor(lane(s, 0), lane(s, 0), lane_bank(s, 1), ALU.add).then_inc(rises("a_x1", s), 1)
                    dve.wait_ge(*at("a_x1", s, n))
                    measure("a2", s, n, squares(lane(s, 0)))
                for s in range(LANES):
                    normalize("a2", s, n, squares(lane(s, 0)), squares(lane(s, 8)))

            measure_x(1)
            normalize_x(1)
            with dve.Fori(0, J - 1) as j:
                convolutions(j + 1, True)
            convolutions(J, False)

            dve.wait_ge(sem("gates_loaded"), 16 * 9)
            for k in (0, 2):
                V.tensor_scalar(gate_u[:, k, :], gate_u[:, k, :], 0.5, None, ALU.mult)
                V.tensor_scalar(gate_v[:, k, :], gate_v[:, k, :], 0.25, None, ALU.mult)
                V.tensor_scalar(gate_b[:, k, :], gate_b[:, k, :], 0.5, None, ALU.mult)
            V.tensor_scalar(gate_v[:, 1, :], gate_v[:, 1, :], 0.5, None, ALU.mult).then_inc(sem("gates_scaled"), 1)

            def recur(quad, step, meanwhile):
                k, n = step % 2, quad * 2 + step // 2 + 1
                V.scalar_tensor_tensor(state_cell[:], hidden[:, (step - 1) % STEPS, :], 0.5, cell[:], ALU.mult, ALU.mult).then_inc(rises("r_hc", k), 1)
                dve.wait_ge(*at("r_gates", k, n))
                V.scalar_tensor_tensor(in_cand[:], gates[:, k, 0, :], 1.0, gates[:, k, 1, :], ALU.add, ALU.mult).then_inc(rises("r_ic", k), 1)
                dve.wait_ge(*at("r_ic", k, n))
                V.tensor_tensor(cell[:], state_cell[:], in_cand[:], ALU.add).then_inc(rises("r_cell", k), 1)
                dve.wait_ge(sem("r_kept"), quad * STEPS + step + 1)
                meanwhile()
                dve.wait_ge(*at("r_tanh", k, n))
                V.scalar_tensor_tensor(hidden[:, step, :], gates[:, k, 2, :], 1.0, cell_tanh[:], ALU.add, ALU.mult).then_inc(rises("r_state", k), 1)
                dve.wait_ge(*at("r_state", k, n))

            dve.wait_ge(sem("r_zero"), 2)

            def four_steps(quad, squares_too):
                def normed_power():
                    dve.wait_ge(sem("e_inv"), quad + 1)
                    V.tensor_scalar(power[:], square[:], sc[:, 3:4], None, ALU.mult).then_inc(sem("e_power"), 1)

                def copied_square():
                    dve.wait_ge(sem("e_square_psum"), quad + 1)
                    V.tensor_copy(square[:], bank(1, 2)[:, 0:P]).then_inc(sem("e_copied"), 1)

                for step, meanwhile in enumerate((normed_power, copied_square, lambda: trace_of_square(quad + 2),
                                                  lambda: inverse_trace(quad + 2))):
                    recur(quad, step, meanwhile if squares_too else lambda: None)

            with dve.Fori(0, N // STEPS - 1) as quad:
                four_steps(quad, True)
            four_steps(N // STEPS - 1, False)
            V.tensor_copy(sc[:, 12:13], ones[:, 0:1]).then_inc(sem("recurrence_done"), 1)
            V.tensor_tensor_reduce(tmp[:], square[:], sym[:], 1.0, 0.0, ALU.mult, ALU.add, sc[:, 4:5]).then_inc(sem("e_rayleigh"), 1)
            dve.wait_ge(sem("e_rayleigh_psum"), 1)
            V.tensor_copy(sc[:, 6:7], bank(1, 3)[:, 1:2]).then_inc(sem("one_shot"), 1)
            dve.wait_ge(sem("one_shot"), 9)
            V.tensor_scalar(sc[:, 8:9], sc[:, 6:7], sc[:, 3:4], 1e-8, ALU.mult, ALU.add).then_inc(sem("one_shot"), 1)
            dve.wait_ge(sem("one_shot"), 10)
            V.reciprocal(sc[:, 9:10], sc[:, 8:9]).then_inc(sem("one_shot"), 1)
            dve.wait_ge(sem("one_shot"), 11)
            V.tensor_scalar(square[:], adj_t[:], sc[:, 9:10], 2.0, ALU.mult, ALU.mult).then_inc(sem("one_shot"), 1)
            dve.wait_ge(sem("one_shot"), 12)
            V.tensor_tensor(lap_t[:], square[:], ident[:], ALU.subtract).then_inc(sem("lap_t"), 1)
            dve.wait_ge(sem("l1_loaded"), L1_LOADS)

            def both_halves(first, n1, second, n2, shared, n3):
                pairs_of = lambda p: () if p is None else lanes_of(p)
                one, two, three = pairs_of(first), pairs_of(second), pairs_of(shared)
                for s in one:
                    dve.wait_ge(sem("c_x1_in", s), 16 * n1)
                    dve.wait_ge(*at("c_hs_psum", s, n1))
                    V.scalar_tensor_tensor(lane(s, 0), lane_bank(s, 0), 0.5, lane(s, 0), ALU.mult, ALU.add).then_inc(rises("c_x2", s), 1)
                    dve.wait_ge(*at("c_x2", s, n1))
                    measure("c1", s, n1, squares(lane(s, 0)))
                for s in two:
                    dve.wait_ge(*at("c_wo_psum", s, n2))
                    dve.wait_ge(*at("c_x1_bo", s, n2))
                    V.tensor_tensor(lane(s, 5), lane_bank(s, 1), lane(s, 3), ALU.add).then_inc(rises("c_res2", s), 1)
                    dve.wait_ge(*at("c_res2", s, n2))
                    measure("c3", s, n2, squares(lane(s, 5)))
                for s in one:
                    normalize("c1", s, n1, squares(lane(s, 0)), squares(lane(s, 1)))
                for s in two:
                    gain("c3", s, n2, squares(lane(s, 5)), "g2")
                for s in three:
                    dve.wait_ge(*at("c_x3_b2s", s, n3))
                    dve.wait_ge(*at("e_down_psum", s, n3))
                    V.tensor_tensor(lane(s, 11), lane(s, 11), lane_bank(s, 1), ALU.add).then_inc(sem("e_y", s), 1)
                for s in two:
                    shift("c3", s, n2, squares(lane(s, 5)), squares(lane(s, 5)), row("be2"), "c_x2n")
                for s in one:
                    dve.wait_ge(*at("c_h_psum", s, n1))
                    V.tensor_tensor(squares(lane(s, 3)), squares(lane_bank(s, 0)), row("bc"), ALU.add).then_inc(rises("c_h", s), 1)
                    dve.wait_ge(*at("c_h", s, n1))
                    measure("c2", s, n1, squares(lane(s, 3)))
                for s in one:
                    gain("c2", s, n1, squares(lane(s, 3)), "g1")
                for s in one:
                    shift("c2", s, n1, squares(lane(s, 3)), squares(lane(s, 3)), row("be1"), "c2_shifted")
                    dve.wait_ge(*at("c2_shifted", s, n1))
                    V.scalar_tensor_tensor(lane(s, 4), lane(s, 3), 0.0, lane(s, 1), ALU.max, ALU.add).then_inc(rises("c_block_x1", s), 1)
                for s in two:
                    dve.wait_ge(*at("c_ff_psum", s, n2))
                    dve.wait_ge(*at("c_x2_b2", s, n2))
                    V.tensor_tensor(lane(s, 1), lane_bank(s, 1), lane(s, 3), ALU.add).then_inc(rises("c_res3", s), 1)
                    dve.wait_ge(*at("c_res3", s, n2))
                    measure("c4", s, n2, squares(lane(s, 1)))
                for s in one:
                    dve.wait_ge(*at("c_q_psum", s, n1))
                    dve.wait_ge(*at("c_x1_bo", s, n1))
                    V.tensor_tensor(squares(lane(s, 4)), squares(lane_bank(s, 0)),
                                    row_any[:].unsqueeze(1).to_broadcast([P, G, P]), ALU.mult).then_inc(rises("c_q", s), 1)
                for s in two:
                    gain("c4", s, n2, squares(lane(s, 1)), "g3")
                for s in two:
                    dve.wait_ge(*at("c_x_be3", s, n2))
                    dve.wait_ge(sem("out_stored", s), 16 * n2 - 15)
                    shift("c4", s, n2, squares(lane(s, 1)), squares(lane(s, 11)), squares(lane(s, 0)), "c_x3")
                    dve.wait_ge(*at("c_x3", s, n2))
                    measure("c5", s, n2, squares(lane(s, 11)))
                for s in one:
                    for b in range(G):
                        heads = slice(b * HEADS, (b + 1) * HEADS)
                        dve.wait_ge(*at(f"c_s{b}_psum", s, n1))
                        V.tensor_reduce(top[:, s, 0, heads], lane_banks(s)[:, b, :].rearrange("p (h m) -> p h m", h=HEADS), AX.X, ALU.max).then_inc(rises(f"c_max{b}", s), 1)
                        dve.wait_ge(*at(f"c_max{b}", s, n1))
                        V.tensor_scalar(top[:, s, 1, heads], top[:, s, 0, heads], -1.0, None, ALU.mult).then_inc(rises(f"c_negmax{b}", s), 1)
                for s in two:
                    dve.wait_ge(sem("rows_free", second), n2)
                    normalize("c5", s, n2, squares(lane(s, 11)), routed[:, second, tokens_of(s), 0:P])
                if second is not None:
                    route_start(second, n2)
                    route(second, n2)
                for s in one:
                    dve.wait_ge(*at("c_o_psum", s, n1))
                    V.reciprocal(inv_sum[:, s], attended(s)[:, :, :, HD]).then_inc(rises("c_inv", s), 1)
                    dve.wait_ge(*at("c_inv", s, n1))
                    V.tensor_tensor(squares(lane(s, 1)).rearrange("p b (h d) -> p b h d", h=HEADS),
                                    attended(s)[:, :, :, 0:HD], inv_sum[:, s].unsqueeze(3).to_broadcast([P, G, HEADS, HD]),
                                    ALU.mult).then_inc(rises("c_o", s), 1)
                if second is not None:
                    route_places(second, n2)

            def route_start(s, n):
                R = [router[:, s, k] for k in range(12)]
                wide = [P, PAIR, EXPERTS]
                logits = bank(s, 1)[:, 0:PAIR * EXPERTS].rearrange("p (b e) -> p b e", b=PAIR)
                dve.wait_ge(*at("d_logits_psum", s, n))
                V.tensor_reduce(R[0][:, :, 0], logits, AX.X, ALU.max).then_inc(rises("d_max", s), 1)
                dve.wait_ge(*at("d_max", s, n))
                V.tensor_tensor(R[1], logits, R[0][:, :, 0:1].to_broadcast(wide), ALU.subtract).then_inc(rises("d_sub", s), 1)

            def route(s, n):
                R = [router[:, s, k] for k in range(12)]
                wide = [P, PAIR, EXPERTS]
                logits = bank(s, 1)[:, 0:PAIR * EXPERTS].rearrange("p (b e) -> p b e", b=PAIR)
                dve.wait_ge(*at("d_exp", s, n))
                carry_wait()
                for b in range(PAIR):
                    last = V.max(R[3][:, b, :], R[2][:, b, :])
                last.then_inc(rises("d_top", s), 1)
                dve.wait_ge(*at("d_top", s, n))
                carry_wait()
                for b in range(PAIR):
                    last = V.max_index(best_idx[:, s, b, :], R[3][:, b, :], R[2][:, b, :])
                last.then_inc(rises("d_idx", s), 1)
                V.tensor_tensor(R[0][:, :, 0], R[3][:, :, 0], R[3][:, :, 1], ALU.add).then_inc(rises("d_den", s), 1)
                dve.wait_ge(*at("d_den", s, n))
                V.reciprocal(R[0][:, :, 1], R[0][:, :, 0]).then_inc(rises("d_inv", s), 1)
                dve.wait_ge(*at("d_inv", s, n))
                V.tensor_tensor(routed[:, s, :, P:P + TOP], R[3][:, :, 0:2], R[0][:, :, 1:2].to_broadcast([P, PAIR, 2]), ALU.mult).then_inc(rises("d_w", s), 1)
                dve.wait_ge(*at("d_idx", s, n))
                V.tensor_copy(R[0][:, :, 4:6], best_idx[:, s, :, 0:2]).then_inc(rises("d_idxf", s), 1)
                dve.wait_ge(*at("d_w", s, n))
                dve.wait_ge(*at("d_idxf", s, n))
                for k in range(TOP):
                    V.tensor_tensor(R[4 + k], expert_no[:], R[0][:, :, 4 + k:5 + k].to_broadcast(wide),
                                    ALU.is_equal).then_inc(rises(f"d_eq{k}", s), 1)
                dve.wait_ge(*at("d_eq1", s, n))
                V.tensor_tensor(chosen[:, s], R[4], R[5], ALU.add).then_inc(rises("d_chosen", s), 1)
                V.tensor_copy(routed[:, s, :, P + 2], best_idx[:, s, :, 0])
                V.tensor_copy(routed[:, s, :, P + 3].bitcast(I32), token_no[:, bass.ds((n * SLOTS + s - SLOTS) * PAIR, PAIR)])

            def route_places(s, n):
                R = [router[:, s, k] for k in range(12)]
                wide = [P, PAIR, EXPERTS]
                logits = bank(s, 1)[:, 0:PAIR * EXPERTS].rearrange("p (b e) -> p b e", b=PAIR)
                dve.wait_ge(*at("d_places_psum", s, n))
                dve.wait_ge(sem("d_counted"), n * SLOTS + s + 1 - SLOTS)
                V.tensor_tensor(R[9], logits, next_row[:].unsqueeze(1).to_broadcast(wide), ALU.add).then_inc(rises("d_place", s), 1)
                dve.wait_ge(*at("d_place", s, n))
                V.tensor_tensor(next_row[:], next_row[:], bank(s, 1)[:, PAIR * EXPERTS:(PAIR + 1) * EXPERTS],
                                ALU.add).then_inc(sem("d_counted"), 1)
                for k in range(TOP):
                    V.tensor_tensor(R[10 + k], R[4 + k], R[9], ALU.mult).then_inc(rises(f"d_prod{k}", s), 1)
                for k in range(TOP):
                    dve.wait_ge(*at(f"d_prod{k}", s, n))
                    V.tensor_reduce(R[0][:, :, 6 + k], R[10 + k], AX.X, ALU.add).then_inc(rises(f"d_slot{k}", s), 1)
                dve.wait_ge(*at("d_slot1", s, n))
                V.tensor_copy(row_idx[:, s, :, :], R[0][:, :, 6:8]).then_inc(rises("d_slots", s), 1)

            both_halves(0, 1, None, None, None, None)
            both_halves(1, 1, 0, 1, None, None)
            with dve.Fori(0, J - 1) as j:
                both_halves(0, j + 2, 1, j + 1, 0, j + 1)
                both_halves(1, j + 2, 0, j + 2, 1, j + 1)
            both_halves(None, None, 1, J, 0, J)

            dve.wait_ge(sem("d_counted"), J * SLOTS + 1)
            steps, tile_no, cells = table(0, EXPERTS * (TOKENS // TILE)), table(1, TILES), table(2, 8 * B)
            ge, part = (table(k, TILES * EXPERTS).rearrange("p (i e) -> p i e", e=EXPERTS) for k in (3, 4))
            count, tiles_of, upto = (cells[:, 8 * k:8 * k + EXPERTS] for k in range(3))
            expert_f, first_f, within, live, at_f = (cells[:, 32 + TILES * k:32 + TILES * (k + 1)] for k in range(5))
            made = [0]

            def then(op):
                op.then_inc(sem("table_step"), 1)
                made[0] += 1
                dve.wait_ge(sem("table_step"), made[0])

            dve.wait_ge(sem("table_consts"), 1)
            then(V.tensor_tensor(count, next_row[:], region_at[:], ALU.subtract))
            then(V.tensor_tensor(steps.rearrange("p (e m) -> p e m", e=EXPERTS), count.unsqueeze(2).to_broadcast(
                [P, EXPERTS, TOKENS // TILE]), steps.rearrange("p (e m) -> p e m", e=EXPERTS), ALU.is_gt))
            then(V.tensor_reduce(tiles_of, steps.rearrange("p (e m) -> p e m", e=EXPERTS), AX.X, ALU.add))
            then(V.tensor_copy(upto, tiles_of))
            for e in range(1, EXPERTS):
                then(V.tensor_tensor(upto[:, e:e + 1], upto[:, e - 1:e], tiles_of[:, e:e + 1], ALU.add))
            then(V.tensor_tensor(ge, tile_no.unsqueeze(2).to_broadcast([P, TILES, EXPERTS]),
                                 upto.unsqueeze(1).to_broadcast([P, TILES, EXPERTS]), ALU.is_ge))
            then(V.tensor_reduce(expert_f, ge, AX.X, ALU.add))
            then(V.tensor_tensor(part, ge, tiles_of.unsqueeze(1).to_broadcast([P, TILES, EXPERTS]), ALU.mult))
            then(V.tensor_reduce(first_f, part, AX.X, ALU.add))
            then(V.tensor_tensor(within, tile_no, first_f, ALU.subtract))
            then(V.tensor_scalar(live, expert_f, EXPERTS - 0.5, float(TILE), ALU.is_lt, ALU.mult))
            then(V.tensor_tensor(within, within, live, ALU.mult))
            then(V.tensor_scalar(at_f, expert_f, float(REGION), None, ALU.mult))
            then(V.tensor_tensor(at_f, at_f, within, ALU.add))
            then(V.tensor_scalar(expert_f, expert_f, EXPERTS - 1.0, None, ALU.min))
            then(V.tensor_copy(tile_at[:], at_f))
            then(V.tensor_copy(tile_expert[:], expert_f))
            V.tensor_copy(next_row_i[:], next_row[:]).then_inc(sem("tables"), 1)
            dve.wait_ge(sem("tables"), 1)

            both_halves(None, None, None, None, 1, J)

            for s in range(LANES):
                dve.wait_ge(sem("out_stored", s), 16 * J + 1)
            def stage(s, i):
                e = dve.value_load(tile_expert[0:1, bass.ds(i, 1)], min_val=0, max_val=EXPERTS - 1)
                V.tensor_copy(tile(s, 5), up_w[:, bass.ds(e + 1, 1), :].rearrange("p a f -> p (a f)"))
                V.tensor_copy(tile(s, 7)[:, 0:FC], up_b[:, bass.ds(e + 1, 1), :].rearrange("p a f -> p (a f)"))
                V.tensor_copy(tile(s, 7)[:, P:2 * P], down_b[:, bass.ds(e, 1), :].rearrange("p a d -> p (a d)"))
                V.tensor_copy(expert_now[:, s:s + 1], expert_no[:, 0, bass.ds(e, 1)])
                V.tensor_copy(tile(s, 6), down_w[:, bass.ds(e + 1, 1), :, :].rearrange("p a c d -> p (a c d)")).then_inc(sem("m_staged", s), 1)

            def experts(n, more):
                for s in range(SLOTS):
                    first, diff, part_w, weight = (row_weight[:, s, k, :] for k in range(4))
                    dve.wait_ge(sem("m_staged", s), n)
                    dve.wait_ge(sem("m_rows_in", s), 16 * n)
                    V.tensor_scalar(first, routed[:, s, :, P + 2], expert_now[:, s:s + 1], None, ALU.is_equal).then_inc(rises("m_is_first", s), 1)
                    V.tensor_tensor(diff, routed[:, s, :, P], routed[:, s, :, P + 1], ALU.subtract).then_inc(rises("m_diff", s), 1)
                    dve.wait_ge(*at("m_diff", s, n))
                    V.tensor_tensor(part_w, first, diff, ALU.mult).then_inc(rises("m_part", s), 1)
                    dve.wait_ge(*at("m_part", s, n))
                    V.tensor_tensor(weight, part_w, routed[:, s, :, P + 1], ALU.add).then_inc(rises("m_weight", s), 1)
                for s in range(SLOTS):
                    dve.wait_ge(sem("m_free", s), n)
                    dve.wait_ge(*at("m_weight", s, n))
                    dve.wait_ge(*at("m_xt_psum", s, n))
                    V.tensor_copy(row_token[:, s, :], routed[:, s, :, ROW - 1].bitcast(U32)).then_inc(rises("m_ids", s), 1)
                for s in range(SLOTS):
                    dve.wait_ge(*at("m_down_psum", s, n))
                    V.tensor_tensor(squares(tile(s, 3)), squares(bank(s, 1)),
                                    tile(s, 7)[:, P:2 * P].unsqueeze(1).to_broadcast([P, SUB, P]), ALU.add).then_inc(sem("m_biased", s), 1)
                    dve.wait_ge(sem("m_biased", s), n)
                    V.tensor_tensor(squares(tile(s, 11)), squares(tile(s, 3)),
                                    row_weight[:, s, 3, :].unsqueeze(2).to_broadcast([P, SUB, P]), ALU.mult).then_inc(sem("m_y", s), 1)
                    if more:
                        stage(s, n * SLOTS + s)

            for s in range(SLOTS):
                stage(s, s)
            with dve.Fori(0, TILES // SLOTS - 1) as j:
                experts(j + 1, True)
            experts(TILES // SLOTS, False)

        @block.scalar
        def _(act):
            A = nc.scalar
            for k, name in enumerate("ico"):
                act.dma_start(gate_u[:, k, :], t["L0_ffn_U_" + name]).then_inc(sem("gates_loaded"), 16)
                act.dma_start(gate_v[:, k, :], t["L0_ffn_V_" + name]).then_inc(sem("gates_loaded"), 16)
                act.dma_start(gate_b[:, k, :], t["L0_ffn_b_" + name].unsqueeze(0)).then_inc(sem("gates_loaded"), 16)
            act.wait_ge(sem("l0_loaded"), 16 * 6)
            act.wait_ge(sem("b2_half"), 1)
            def states_in(n):
                for s in range(LANES):
                    act.wait_ge(sem("a_x1t_psum", s), n)
                    b0 = (n * LANES - LANES + s) * G
                    A.copy(states[:, 1:, bass.ds(b0, G)].rearrange("p n b -> p b n"), squares(lane_bank(s, 2))).then_inc(sem("a_x1t", s), 1)

            def convolutions(n, follows):
                for s in range(LANES):
                    act.wait_ge(*at("a_xt_psum", s, n))
                    A.copy(lane(s, 2), lane_bank(s, 0)).then_inc(rises("a_xt", s), 1)
                if follows:
                    states_in(n - 1)
                for s in range(LANES):
                    act.wait_ge(*at("a_h1t_psum", s, n))
                    A.activation(lane(s, 4), lane_bank(s, 2), ACT.Relu, bias=col_b[:, 0:1]).then_inc(rises("a_h1t", s), 1)
                for s in range(LANES):
                    act.wait_ge(*at("a_z2_psum", s, n))
                    A.copy(lane(s, 6), lane_bank(s, 1)).then_inc(rises("a_z2", s), 1)
                for s in range(LANES):
                    act.wait_ge(*at("a_h2t_psum", s, n))
                    A.activation(lane(s, 7), lane_bank(s, 2), ACT.Relu, bias=col_b[:, 2:3], scale=0.5).then_inc(rises("a_h2t", s), 1)

            convolutions(1, False)
            with act.Fori(0, J - 1) as j:
                convolutions(j + 2, True)
            states_in(J)

            act.wait_ge(sem("gates_scaled"), 1)
            with act.Fori(0, N // 2) as pair:
                for k in range(2):
                    n = pair + 1
                    act.wait_ge(*at("r_zic_psum", k, n))
                    A.activation(gates[:, k, 0:2, :].rearrange("p g b -> p (g b)"), psum[:, 2 * k, 0:2 * B], ACT.Tanh).then_inc(rises("r_gates", k), 1)
                    act.wait_ge(*at("r_zo_psum", k, n))
                    A.activation(gates[:, k, 2, :], psum[:, 2 * k + 1, 0:B], ACT.Tanh).then_inc(rises("r_out_gate", k), 1)
                    act.wait_ge(*at("r_cell", k, n))
                    A.activation(cell_tanh[:], cell[:], ACT.Tanh, scale=0.5).then_inc(rises("r_tanh", k), 1)

            act.wait_ge(sem("l1_loaded"), L1_LOADS)

            def both_halves(first, n1, second, n2, shared, n3):
                pairs_of = lambda p: () if p is None else lanes_of(p)
                one, two, three = pairs_of(first), pairs_of(second), pairs_of(shared)
                def shared_up(c):
                    for s in three:
                        act.wait_ge(*at(f"e_up{c}_psum", s, n3))
                        A.activation(lane(s, 12 + c), lane_bank(s, 1), ACT.Gelu, bias=up_b[:, 0, c:c + 1]).then_inc(rises(f"e_up{c}", s), 1)

                shared_up(0)
                for s in two:
                    act.wait_ge(*at("c_ot_psum", s, n2))
                    A.copy(lane(s, 2), lane_bank(s, 0)).then_inc(rises("c_ot", s), 1)
                for c in range(1, FC):
                    shared_up(c)
                for s in one:
                    act.wait_ge(*at("c_xp_psum", s, n1))
                    A.copy(lane(s, 5), lane_bank(s, 0)).then_inc(rises("c_xp", s), 1)
                for s in two:
                    act.wait_ge(*at("c_x2t_psum", s, n2))
                    A.copy(lane(s, 2), lane_bank(s, 0)).then_inc(rises("c_x2t", s), 1)
                for k in range(2):
                    for s in two:
                        act.wait_ge(*at(f"c_up{k}_psum", s, n2))
                        A.activation(lane(s, 7 + k), lane_bank(s, 1 + k), ACT.Gelu, bias=col_b[:, 5 + k:6 + k]).then_inc(rises(f"c_up{k}", s), 1)
                for s in one:
                    act.wait_ge(*at("c_x1t_psum", s, n1))
                    A.copy(lane(s, 2), lane_bank(s, 0)).then_inc(rises("c_x1t", s), 1)
                for s in one:
                    act.wait_ge(*at("c_kv_psum", s, n1))
                    for h in range(HEADS):
                        last = A.activation(lane(s, 12 + h), lane_bank(s, 1), ACT.Copy, scale=head_col[:, h:h + 1])
                    last.then_inc(rises("c_k", s), 1)
                    A.copy(v_ones[:, s, :, :, 0:HD].rearrange("p b h d -> p (b h) d"),
                           lane_bank(s, 3).rearrange("p (c d) -> p c d", d=HD)).then_inc(rises("c_v", s), 1)
                for s in one:
                    for b in range(G):
                        act.wait_ge(*at(f"c_negmax{b}", s, n1))
                        for h in range(HEADS):
                            c = b * HEADS + h
                            last = A.activation(lane(s, 7, 4)[:, c * P:(c + 1) * P], lane_banks(s)[:, b, h * P:(h + 1) * P], ACT.Exp,
                                                bias=top[:, s, 1, c:c + 1])
                        last.then_inc(rises(f"c_exp{b}", s), 1)
                for s in two:
                    act.wait_ge(*at("c_x4t_psum", s, n2))
                    A.copy(lane(s, 2), lane_bank(s, 0)).then_inc(rises("c_x4t", s), 1)
                for s in one:
                    for b in range(G):
                        act.wait_ge(*at(f"c_pt{b}_psum", s, n1))
                        A.copy(lane(s, 12 + 2 * b, 2), lane_banks(s)[:, b, :]).then_inc(rises(f"c_pt{b}", s), 1)
                if second is not None:
                    act.wait_ge(*at("d_sub", second, n2))
                    A.activation(router[:, second, 2], router[:, second, 1], ACT.Exp).then_inc(rises("d_exp", second), 1)

            both_halves(0, 1, None, None, None, None)
            both_halves(1, 1, 0, 1, None, None)
            with act.Fori(0, J - 1) as j:
                both_halves(0, j + 2, 1, j + 1, 0, j + 1)
                both_halves(1, j + 2, 0, j + 2, 1, j + 1)
            both_halves(None, None, 1, J, 0, J)
            both_halves(None, None, None, None, 1, J)

            act.wait_ge(sem("tables"), 1)
            for e in range(EXPERTS // 2, EXPERTS):
                pad_expert(act, e)
            with act.Fori(0, TILES // SLOTS) as j:
                n = j + 1
                for s in range(SLOTS):
                    act.wait_ge(*at("m_xt_psum", s, n))
                    A.copy(tile(s, 2), bank(s, 0)).then_inc(rises("m_xt", s), 1)
                for s in range(SLOTS):
                    for c in range(FC):
                        act.wait_ge(*at(f"m_up{c}_psum", s, n))
                        A.activation(tile(s, 12 + c), bank(s, (1 + c) % 4), ACT.Gelu, bias=tile(s, 7)[:, c:c + 1]).then_inc(rises(f"m_h{c}", s), 1)

        @block.tensor
        def _(pe):
            T = nc.tensor

            def transposes(out, src, done):
                for b in range(src.shape[1]):
                    last = T.transpose(squares(out)[:, b, :], src[:, b, :], ident[:])
                last.then_inc(done, 1)

            def by_square(out, left, right, done):
                for b in range(G):
                    last = T.matmul(squares(out)[:, b, :], left[:, b, :], right, start=(b == 0), stop=True, skip_group_check=True)
                last.then_inc(done, 1)

            pe.wait_ge(sem("adj_loaded"), 16)
            pe.wait_ge(sem("consts"), 1)
            T.transpose(bank(0, 0)[:, 0:P], adj[:], ident[:]).then_inc(sem("adj_t_psum"), 1)
            pe.wait_ge(sem("adj_t"), 1)
            pe.wait_ge(sem("e_spread"), 1)
            T.transpose(bank(1, 2)[:, 0:P], square[:], ident[:]).then_inc(sem("e_bound_psum"), 1)
            pe.wait_ge(sem("e_diag"), 1)
            T.matmul(bank(1, 3)[:, 0:1], ones[:], sc[:, 2:3], start=True, stop=True).then_inc(sem("e_trace_psum"), 1)
            pe.wait_ge(sem("m_diag"), 1)
            T.matmul(bank(1, 2)[:, 0:P], ones[:], power[:], start=True, stop=True).then_inc(sem("m_any_psum"), 1)
            pe.wait_ge(sem("row_any"), 1)
            pe.wait_ge(sem("l0_loaded"), 16 * 6)
            def states_out(n, reader):
                for s in range(LANES):
                    pe.wait_ge(*at("a2_normed", s, n))
                    pe.wait_ge(*at("a_xt", s, reader))
                    transposes(lane_bank(s, 2), squares(lane(s, 8)), sem("a_x1t_psum", s))

            def convolutions(n, follows):
                for s in range(LANES):
                    pe.wait_ge(*at("a1_normed", s, n))
                    transposes(lane_bank(s, 0), squares(lane(s, 1)), rises("a_xt_psum", s))
                    if follows:
                        pe.wait_ge(*at("a_x1", s, n - 1))
                    by_square(lane_bank(s, 1), squares(lane(s, 1)), adj_t[:], rises("a_z1_psum", s))
                if follows:
                    states_out(n - 1, n)
                for s in range(LANES):
                    pe.wait_ge(*at("a_xt", s, n))
                    if follows:
                        pe.wait_ge(sem("a_x1t", s), n - 1)
                    T.matmul(lane_bank(s, 2), W["L0_gnn_w1_loop"][:], lane(s, 2), start=True, stop=False)
                    pe.wait_ge(*at("a_z1", s, n))
                    T.matmul(lane_bank(s, 2), W["L0_gnn_w1_neigh"][:], lane(s, 3), start=False, stop=True).then_inc(rises("a_h1t_psum", s), 1)
                for s in range(LANES):
                    pe.wait_ge(*at("a_h1t", s, n))
                    transposes(lane_bank(s, 0), squares(lane(s, 4)), rises("a_h1_psum", s))
                for s in range(LANES):
                    pe.wait_ge(*at("a_h1", s, n))
                    by_square(lane_bank(s, 1), squares(lane(s, 5)), adj_t[:], rises("a_z2_psum", s))
                for s in range(LANES):
                    T.matmul(lane_bank(s, 2), W["L0_gnn_w2_loop"][:], lane(s, 4), start=True, stop=False)
                    pe.wait_ge(*at("a_z2", s, n))
                    T.matmul(lane_bank(s, 2), W["L0_gnn_w2_neigh"][:], lane(s, 6), start=False, stop=True).then_inc(rises("a_h2t_psum", s), 1)
                for s in range(LANES):
                    pe.wait_ge(*at("a_h2t", s, n))
                    transposes(lane_bank(s, 1), squares(lane(s, 7)), rises("a_h2_psum", s))

            convolutions(1, False)
            with pe.Fori(0, J - 1) as j:
                convolutions(j + 2, True)
            states_out(J, J)

            for s in range(LANES):
                pe.wait_ge(sem("a_x1t", s), J)
            pe.wait_ge(sem("gates_scaled"), 1)

            def gate_bank(k, g):
                return psum[:, 2 * k + (g == 2), (g % 2) * B:(g % 2 + 1) * B]

            def input_part(now, k):
                for g in range(3):
                    T.matmul(gate_bank(k, g), gate_u[:, g, :], states[:, now, :], start=(g != 1), stop=False, skip_group_check=True)
                    T.matmul(gate_bank(k, g), gate_b[:, g, :], ones[0:1, :], start=False, stop=False, skip_group_check=True)

            def state_part(step, k):
                for g in range(3):
                    last = T.matmul(gate_bank(k, g), gate_v[:, g, :], hidden[:, step, :], start=False, stop=True, skip_group_check=True)
                    if g == 1:
                        last.then_inc(rises("r_zic_psum", k), 1)
                last.then_inc(rises("r_zo_psum", k), 1)

            def after_step(quad, step, more=True, between=lambda: None):
                k = step % 2
                pe.wait_ge(*at("r_state", k, quad * 2 + step // 2 + 1))
                state_part(step, 1 - k)
                between()
                if more:
                    input_part(quad * STEPS + step + 3, k)

            input_part(1, 0)
            pe.wait_ge(sem("r_zero"), 2)
            state_part(STEPS - 1, 0)
            input_part(2, 1)
            with pe.Fori(0, N // STEPS - 1) as quad:
                def squared():
                    pe.wait_ge(sem("e_power"), quad + 1)
                    T.matmul(bank(1, 2)[:, 0:P], power[:], power[:], start=True, stop=True).then_inc(sem("e_square_psum"), 1)

                def summed():
                    pe.wait_ge(sem("e_diag"), quad + 2)
                    T.matmul(bank(1, 3)[:, 0:1], ones[:], sc[:, 2:3], start=True, stop=True).then_inc(sem("e_trace_psum"), 1)

                after_step(quad, 0, between=squared)
                after_step(quad, 1)
                after_step(quad, 2, between=summed)
                after_step(quad, 3)
            for step in range(3):
                after_step(N // STEPS - 1, step, more=step < 2)
            pe.wait_ge(sem("e_rayleigh"), 1)
            T.matmul(bank(1, 3)[:, 1:2], ones[:], sc[:, 4:5], start=True, stop=True).then_inc(sem("e_rayleigh_psum"), 1)

            pe.wait_ge(sem("l1_loaded"), L1_LOADS)
            pe.wait_ge(sem("lap_t"), 1)
            pe.wait_ge(sem("mask"), 1)
            pe.wait_ge(sem("recurrence_done"), 1)

            def both_halves(first, n1, second, n2, shared, n3):
                pairs_of = lambda p: () if p is None else lanes_of(p)
                one, two, three = pairs_of(first), pairs_of(second), pairs_of(shared)
                def shared_up(c):
                    for s in three:
                        if c == 0:
                            pe.wait_ge(*at("d_place", shared, n3))
                            pe.wait_ge(sem("d_counted"), n3 * SLOTS + shared + 2 - SLOTS)
                        else:
                            pe.wait_ge(*at(f"e_up{c - 1}", s, n3))
                        T.matmul(lane_bank(s, 1), up_w[:, 0, c * P:(c + 1) * P], lane(s, 2), start=True, stop=True).then_inc(rises(f"e_up{c}_psum", s), 1)

                for s in one:
                    pe.wait_ge(sem("c_hs", s), n1)
                    transposes(lane_bank(s, 0), squares(lane(s, 6)), rises("c_hs_psum", s))
                for s in two:
                    pe.wait_ge(*at("c_o", s, n2))
                    transposes(lane_bank(s, 0), squares(lane(s, 1)), rises("c_ot_psum", s))
                shared_up(0)
                for s in two:
                    pe.wait_ge(*at("c_ot", s, n2))
                    by_square(lane_bank(s, 1), squares(lane(s, 2)), W["L1_gnn_Wo"][:], rises("c_wo_psum", s))
                shared_up(1)
                shared_up(2)
                shared_up(3)
                for s in three:
                    pe.wait_ge(*at("e_up3", s, n3))
                    for b in range(G):
                        for c in range(FC):
                            last = T.matmul(squares(lane_bank(s, 1))[:, b, :], squares(lane(s, 12 + c))[:, b, :], down_w[:, 0, c, :],
                                            start=(b == 0 and c == 0), stop=(c == FC - 1), skip_group_check=True)
                    last.then_inc(rises("e_down_psum", s), 1)
                for s in one:
                    pe.wait_ge(*at("c1_normed", s, n1))
                    by_square(lane_bank(s, 0), squares(lane(s, 1)), lap_t[:], rises("c_xp_psum", s))
                for s in one:
                    pe.wait_ge(*at("c_xp", s, n1))
                    by_square(lane_bank(s, 0), squares(lane(s, 5)), W["L1_gnn_Wc"][:], rises("c_h_psum", s))
                for s in two:
                    pe.wait_ge(*at("c_x2n", s, n2))
                    transposes(lane_bank(s, 0), squares(lane(s, 5)), rises("c_x2t_psum", s))
                for s in two:
                    pe.wait_ge(*at("c_x2t", s, n2))
                    for k in range(2):
                        T.matmul(lane_bank(s, 1 + k), W["L1_gnn_W1"][:, k * P:(k + 1) * P], lane(s, 2), start=True, stop=True).then_inc(rises(f"c_up{k}_psum", s), 1)
                for s in two:
                    for b in range(G):
                        for k in range(2):
                            if b == 0:
                                pe.wait_ge(*at(f"c_up{k}", s, n2))
                            last = T.matmul(squares(lane_bank(s, 1))[:, b, :], squares(lane(s, 7 + k))[:, b, :], w2_gnn[:, k, :],
                                            start=(b == 0 and k == 0), stop=(k == 1), skip_group_check=True)
                    last.then_inc(rises("c_ff_psum", s), 1)
                for s in one:
                    pe.wait_ge(*at("c_block_x1", s, n1))
                    transposes(lane_bank(s, 0), squares(lane(s, 4)), rises("c_x1t_psum", s))
                for s in one:
                    pe.wait_ge(*at("c_x1t", s, n1))
                    T.matmul(lane_bank(s, 0), W["L1_gnn_Wq"][:], lane(s, 2), start=True, stop=True).then_inc(rises("c_q_psum", s), 1)
                    if shared is not None:
                        pe.wait_ge(sem("e_y", s), n3)
                    T.matmul(lane_bank(s, 1), W["L1_gnn_Wk"][:], lane(s, 2), start=True, stop=True)
                    by_square(lane_bank(s, 3), squares(lane(s, 2)), W["L1_gnn_Wv"][:], rises("c_kv_psum", s))
                for s in one:
                    pe.wait_ge(*at("c_q", s, n1))
                    pe.wait_ge(*at("c_v", s, n1))
                    for b in range(G):
                        T.matmul(lane_banks(s)[:, b, :], ident_h[:], mask_add[:].rearrange("p b m -> p (b m)"), start=True,
                                 stop=False, skip_group_check=True)
                        T.matmul(lane_banks(s)[:, b, :], squares(lane(s, 4))[:, b, :],
                                 lane(s, 12, 4).rearrange("p (h b m) -> p h b m", h=HEADS, b=G)[:, :, b, :],
                                 start=False, stop=True, skip_group_check=True).then_inc(rises(f"c_s{b}_psum", s), 1)
                def score_columns(s):
                    for b in range(G):
                        pe.wait_ge(*at(f"c_exp{b}", s, n1))
                        transposes(lane_banks(s)[:, b, :], squares(lane(s, 7 + 2 * b, 2)), rises(f"c_pt{b}_psum", s))

                def weighted_values(s):
                    for b in range(G):
                        pe.wait_ge(*at(f"c_pt{b}", s, n1))
                        for h in range(HEADS):
                            last = T.matmul(attended(s)[:, b, h, :], squares(lane(s, 12 + 2 * b, 2))[:, h, :],
                                            v_ones[:, s, b, h, :], start=(h == 0), stop=True, skip_group_check=True)
                    last.then_inc(rises("c_o_psum", s), 1)

                if one:
                    score_columns(one[0])
                for s in two:
                    pe.wait_ge(*at("c5_normed", s, n2))
                    transposes(lane_bank(s, 0), routed[:, second, tokens_of(s), 0:P], rises("c_x4t_psum", s))
                if one:
                    score_columns(one[1])
                if second is not None:
                    for s in two:
                        pe.wait_ge(*at("c_x4t", s, n2))
                        for b in range(G):
                            c = s % (PAIR // G) * G + b
                            last = T.matmul(bank(second, 1)[:, c * EXPERTS:(c + 1) * EXPERTS], squares(lane(s, 2))[:, b, :],
                                            W["L1_ffn_Wr"][:], start=(c == 0), stop=True, skip_group_check=True)
                    last.then_inc(rises("d_logits_psum", second), 1)
                for s in one:
                    weighted_values(s)
                if second is not None:
                    pe.wait_ge(*at("d_chosen", second, n2))
                    picked = chosen[:, second]
                    places = bank(second, 1)[:, 0:(PAIR + 1) * EXPERTS].rearrange("p (b e) -> p b e", b=PAIR + 1)
                    T.matmul(bank(second, 1)[:, 0:PAIR * EXPERTS], before[:], picked.rearrange("p b e -> p (b e)"), start=True, stop=False, skip_group_check=True)
                    for b in range(PAIR):
                        last = T.matmul(places[:, b + 1:, :], ones_h[:], picked[:, b:b + 1, :].to_broadcast([P, PAIR - b, EXPERTS]),
                                        start=False, stop=(b == PAIR - 1), skip_group_check=True)
                    last.then_inc(rises("d_places_psum", second), 1)

            both_halves(0, 1, None, None, None, None)
            both_halves(1, 1, 0, 1, None, None)
            with pe.Fori(0, J - 1) as j:
                both_halves(0, j + 2, 1, j + 1, 0, j + 1)
                both_halves(1, j + 2, 0, j + 2, 1, j + 1)
            both_halves(None, None, 1, J, 0, J)
            both_halves(None, None, None, None, 1, J)

            for s in range(LANES):
                pe.wait_ge(sem("e_y", s), J)
            def row_columns(s, n):
                pe.wait_ge(sem("m_rows_in", s), 16 * n)
                transposes(bank(s, 0), routed[:, s, :, 0:P], rises("m_xt_psum", s))

            def experts(n, more):
                for s in range(SLOTS):
                    pe.wait_ge(*at("m_xt", s, n))
                    pe.wait_ge(sem("m_staged", s), n)
                    pe.wait_ge(sem("m_y", s), n)
                    for c in range(FC):
                        T.matmul(bank(s, (1 + c) % 4), tile(s, 5)[:, c * P:(c + 1) * P], tile(s, 2), start=True, stop=True).then_inc(rises(f"m_up{c}_psum", s), 1)
                for s in range(SLOTS):
                    for a in range(SUB):
                        for c in range(FC):
                            if a == 0:
                                pe.wait_ge(*at(f"m_h{c}", s, n))
                            last = T.matmul(squares(bank(s, 1))[:, a, :], squares(tile(s, 12 + c))[:, a, :],
                                            tile(s, 6)[:, c * P:(c + 1) * P], start=(a == 0 and c == 0), stop=(c == FC - 1),
                                            skip_group_check=True)
                    last.then_inc(rises("m_down_psum", s), 1)
                    if more:
                        row_columns(s, n + 1)

            for s in range(SLOTS):
                row_columns(s, 1)
            with pe.Fori(0, TILES // SLOTS - 1) as j:
                experts(j + 1, True)
            experts(TILES // SLOTS, False)
    return nc


_IN = ("x", "adj", "L0_gnn_w1_loop", "L0_gnn_w1_neigh", "L0_gnn_b1", "L0_gnn_w2_loop", "L0_gnn_w2_neigh",
       "L0_gnn_b2", "L0_ffn_U_i", "L0_ffn_V_i", "L0_ffn_b_i", "L0_ffn_U_c", "L0_ffn_V_c", "L0_ffn_b_c",
       "L0_ffn_U_o", "L0_ffn_V_o", "L0_ffn_b_o", "L1_gnn_Wc", "L1_gnn_bc", "L1_gnn_g1", "L1_gnn_be1",
       "L1_gnn_Wq", "L1_gnn_Wk", "L1_gnn_Wv", "L1_gnn_Wo", "L1_gnn_bo", "L1_gnn_g2", "L1_gnn_be2", "L1_gnn_W1",
       "L1_gnn_b1", "L1_gnn_W2", "L1_gnn_b2", "L1_gnn_g3", "L1_gnn_be3", "L1_ffn_Wr", "L1_ffn_W1s", "L1_ffn_b1s",
       "L1_ffn_W2s", "L1_ffn_b2s", "L1_ffn_W1p", "L1_ffn_b1p", "L1_ffn_W2p", "L1_ffn_b2p")


def kernel(**inputs):
    import numpy as _np
    import concourse.bacc as _bacc
    from concourse import mybir as _mybir
    from concourse.bass_utils import run_bass_kernel_spmd as _run

    nc = _bacc.Bacc("TRN2", target_bir_lowering=False, num_devices=1)
    arrays, tensors = {}, {}
    for name in _IN:
        a = _np.ascontiguousarray(inputs[name])
        arrays[f"in_{name}"] = a
        tensors[name] = nc.dram_tensor(f"in_{name}", a.shape, _mybir.dt.from_np(a.dtype), kind="ExternalInput").ap()
    tensors["out"] = nc.dram_tensor("out_0", (128 * 128 + TILE, 128), _mybir.dt.float32, kind="ExternalOutput").ap()
    build(nc, tensors)
    r = _run(nc, [arrays], core_ids=[0])
    return r.results[0]["out_0"][:128 * 128].reshape(128, 128, 128)
```
